# Optimizing a Trainium2 kernel written in Bass

```python
import numpy as np
import jax
import jax.numpy as jnp

def _softmax(x, axis=-1):
    return jax.nn.softmax(x, axis=axis)

def _gelu(x):
    return jax.nn.gelu(x, approximate=True)

def _silu(x):
    return jax.nn.silu(x)

def _sigmoid(x):
    return jax.nn.sigmoid(x)

def _layernorm(x, axis=-1, eps=1e-05):
    m = jnp.mean(x, axis=axis, keepdims=True)
    v = jnp.var(x, axis=axis, keepdims=True)
    return (x - m) / jnp.sqrt(v + eps)

def _scatter_add(tgt, idx, src, axis=0):
    return tgt.at[idx].add(src)

def _segment_sum(src, seg, n):
    return jax.ops.segment_sum(src, seg, n)
kernel_name = 'mk_seq_postln_d2_jaxref_r8_9c2f17'

def setup_inputs(seed: int=0):
    np.random.seed(seed)
    _w = jnp.asarray

    def _L0_attn_setup():
        import jax, jax.numpy as jnp
        import numpy as np
        H = 16
        KVH = 4
        D = 128
        HID = 256
        EPS = 1e-06
        GROUPS = H // KVH

        def elu_plus_one(x):
            return jax.nn.elu(x) + 1.0

        def _repeat_kv(x, b, s):
            x = x.reshape(b, s, KVH, 1, D)
            x = jnp.broadcast_to(x, (b, s, KVH, GROUPS, D))
            return x.reshape(b, s, H * D)

        def _split_heads(x, b, s, nh):
            return x.reshape(b, s, nh, D).transpose(0, 2, 1, 3)
        key = jax.random.key(seed)
        ks = jax.random.split(key, 8)
        s = 0.02
        return {'hidden_states': jax.random.normal(ks[0], (2, 512, HID), jnp.float32), 'Wq': jax.random.normal(ks[1], (H * D, HID), jnp.float32) * s, 'bq': jnp.zeros((H * D,), jnp.float32), 'Wk': jax.random.normal(ks[2], (KVH * D, HID), jnp.float32) * s, 'bk': jnp.zeros((KVH * D,), jnp.float32), 'Wv': jax.random.normal(ks[3], (KVH * D, HID), jnp.float32) * s, 'bv': jnp.zeros((KVH * D,), jnp.float32), 'Wo': jax.random.normal(ks[4], (HID, H * D), jnp.float32) * s}
    _L0_attn_in = _L0_attn_setup()

    def _L0_ffn_setup():
        import jax, jax.numpy as jnp
        import numpy as np
        B, T, D = (4, 128, 256)
        N, S, H = (8, 8, 8)
        ETA = 1.0
        key = jax.random.key(seed)
        ks = jax.random.split(key, 9)
        return {'x': jax.random.normal(ks[0], (B, T, D), jnp.float32), 'select_weight': jax.random.normal(ks[1], (N, D, S), jnp.float32) / D, 'select_mean_diff': jax.random.normal(ks[2], (N, D), jnp.float32) / D, 'imp_center': jax.random.normal(ks[3], (N,), jnp.float32), 'imp_slope': jax.random.normal(ks[4], (N,), jnp.float32) * 5.0, 'lora_update': jax.random.normal(ks[5], (N, D, H), jnp.float32) * 0.02, 'lora_degen': jax.random.normal(ks[6], (N, D, H), jnp.float32) * 0.02, 'bias_w': jax.random.normal(ks[7], (N, D), jnp.float32) * 0.02, 'debias_w': jax.random.normal(ks[8], (N, D), jnp.float32) * 0.02}
    _L0_ffn_in = _L0_ffn_setup()

    def _L1_attn_setup():
        import jax, jax.numpy as jnp
        import numpy as np
        D_MODEL = 256
        NUM_HEADS = 16
        HEAD_DIM = D_MODEL // NUM_HEADS
        key = jax.random.key(seed)
        ks = jax.random.split(key, 6)
        B, T = (4, 256)
        x = jax.random.normal(ks[0], (B, T, D_MODEL), dtype=jnp.float32)
        s = 1.0 / np.sqrt(D_MODEL)
        Wq = jax.random.normal(ks[1], (D_MODEL, D_MODEL), dtype=jnp.float32) * s
        Wk = jax.random.normal(ks[2], (D_MODEL, D_MODEL), dtype=jnp.float32) * s
        Wv = jax.random.normal(ks[3], (D_MODEL, D_MODEL), dtype=jnp.float32) * s
        Wo = jax.random.normal(ks[4], (D_MODEL, D_MODEL), dtype=jnp.float32) * s
        bo = jax.random.normal(ks[5], (D_MODEL,), dtype=jnp.float32) * 0.01
        return {'x': x, 'Wq': Wq, 'Wk': Wk, 'Wv': Wv, 'Wo': Wo, 'bo': bo}
    _L1_attn_in = _L1_attn_setup()

    def _L1_ffn_setup():
        import jax, jax.numpy as jnp
        import numpy as np
        B, S, H = (4, 256, 256)
        E = 8
        F = H // E
        TOPK = 2
        LORA_R = 16
        LORA_SCALE = 1.0
        key = jax.random.key(seed)
        ks = jax.random.split(key, 7)
        x = jax.random.normal(ks[0], (B, S, H), dtype=jnp.float32)
        G = jax.random.normal(ks[1], (H, E), dtype=jnp.float32)
        gate_w = jax.random.normal(ks[2], (E, F, H), dtype=jnp.float32) * np.float32(np.sqrt(2.0 / H))
        up_w = jax.random.normal(ks[3], (E, F, H), dtype=jnp.float32) * np.float32(np.sqrt(2.0 / H))
        down_w = jax.random.normal(ks[4], (E, H, F), dtype=jnp.float32) * np.float32(np.sqrt(2.0 / F))
        lora_A = jax.random.normal(ks[5], (E, LORA_R, H), dtype=jnp.float32) * np.float32(np.sqrt(2.0 / H))
        lora_B = jax.random.normal(ks[6], (E, H, LORA_R), dtype=jnp.float32) * np.float32(np.sqrt(2.0 / LORA_R))
        return {'x': x, 'G': G, 'gate_w': gate_w, 'up_w': up_w, 'down_w': down_w, 'lora_A': lora_A, 'lora_B': lora_B}
    _L1_ffn_in = _L1_ffn_setup()
    _d = {'L0_attn_hidden_states': _L0_attn_in['hidden_states'], 'L0_attn_Wq': _L0_attn_in['Wq'], 'L0_attn_bq': _L0_attn_in['bq'], 'L0_attn_Wk': _L0_attn_in['Wk'], 'L0_attn_bk': _L0_attn_in['bk'], 'L0_attn_Wv': _L0_attn_in['Wv'], 'L0_attn_bv': _L0_attn_in['bv'], 'L0_attn_Wo': _L0_attn_in['Wo'], 'L0_ffn_select_weight': _L0_ffn_in['select_weight'], 'L0_ffn_select_mean_diff': _L0_ffn_in['select_mean_diff'], 'L0_ffn_imp_center': _L0_ffn_in['imp_center'], 'L0_ffn_imp_slope': _L0_ffn_in['imp_slope'], 'L0_ffn_lora_update': _L0_ffn_in['lora_update'], 'L0_ffn_lora_degen': _L0_ffn_in['lora_degen'], 'L0_ffn_bias_w': _L0_ffn_in['bias_w'], 'L0_ffn_debias_w': _L0_ffn_in['debias_w'], 'L1_attn_Wq': _L1_attn_in['Wq'], 'L1_attn_Wk': _L1_attn_in['Wk'], 'L1_attn_Wv': _L1_attn_in['Wv'], 'L1_attn_Wo': _L1_attn_in['Wo'], 'L1_attn_bo': _L1_attn_in['bo'], 'L1_ffn_G': _L1_ffn_in['G'], 'L1_ffn_gate_w': _L1_ffn_in['gate_w'], 'L1_ffn_up_w': _L1_ffn_in['up_w'], 'L1_ffn_down_w': _L1_ffn_in['down_w'], 'L1_ffn_lora_A': _L1_ffn_in['lora_A'], 'L1_ffn_lora_B': _L1_ffn_in['lora_B']}
    _x0 = _d['L0_attn_hidden_states']
    _d['L0_attn_hidden_states'] = jax.random.normal(jax.random.fold_in(jax.random.key(seed), 1), (4, 512, 256), dtype=_x0.dtype)
    del _x0
    return _d

def reference(L0_attn_hidden_states, L0_attn_Wq, L0_attn_bq, L0_attn_Wk, L0_attn_bk, L0_attn_Wv, L0_attn_bv, L0_attn_Wo, L0_ffn_select_weight, L0_ffn_select_mean_diff, L0_ffn_imp_center, L0_ffn_imp_slope, L0_ffn_lora_update, L0_ffn_lora_degen, L0_ffn_bias_w, L0_ffn_debias_w, L1_attn_Wq, L1_attn_Wk, L1_attn_Wv, L1_attn_Wo, L1_attn_bo, L1_ffn_G, L1_ffn_gate_w, L1_ffn_up_w, L1_ffn_down_w, L1_ffn_lora_A, L1_ffn_lora_B):

    def _L0_attn_ref(hidden_states, Wq, bq, Wk, bk, Wv, bv, Wo):
        import jax, jax.numpy as jnp
        import numpy as np
        H = 16
        KVH = 4
        D = 128
        HID = 256
        EPS = 1e-06
        GROUPS = H // KVH

        def elu_plus_one(x):
            return jax.nn.elu(x) + 1.0

        def _repeat_kv(x, b, s):
            x = x.reshape(b, s, KVH, 1, D)
            x = jnp.broadcast_to(x, (b, s, KVH, GROUPS, D))
            return x.reshape(b, s, H * D)

        def _split_heads(x, b, s, nh):
            return x.reshape(b, s, nh, D).transpose(0, 2, 1, 3)
        b, s, _ = hidden_states.shape
        q = hidden_states @ Wq.T + bq
        k = hidden_states @ Wk.T + bk
        v = hidden_states @ Wv.T + bv
        k = _repeat_kv(k, b, s)
        v = _repeat_kv(v, b, s)
        q = _split_heads(q, b, s, H)
        k = _split_heads(k, b, s, H)
        v = _split_heads(v, b, s, H)
        sq = elu_plus_one(q)
        sk = elu_plus_one(k)
        kv = jnp.einsum('bhsd,bhse->bhde', sk, v)
        qkv = jnp.einsum('bhsd,bhde->bhse', sq, kv)
        k_sum = sk.sum(axis=2)
        norm = jnp.einsum('bhsd,bhd->bhs', sq, k_sum)
        attn = qkv / (norm[..., None] + EPS)
        attn = attn.transpose(0, 2, 1, 3).reshape(b, s, H * D)
        return attn @ Wo.T

    def _L0_ffn_ref(x, select_weight, select_mean_diff, imp_center, imp_slope, lora_update, lora_degen, bias_w, debias_w):
        import jax, jax.numpy as jnp
        import numpy as np
        B, T, D = (4, 128, 256)
        N, S, H = (8, 8, 8)
        ETA = 1.0
        x_diff = x[:, None, :, :] - select_mean_diff[None, :, None, :]
        x_diff = x_diff / jnp.linalg.norm(x_diff, axis=3, keepdims=True)
        cont = jnp.einsum('nds,bntd->bnts', select_weight, x_diff) ** 2
        score = cont.sum(axis=-1)
        gate = jax.nn.sigmoid(imp_slope[None, :, None] * (score - imp_center[None, :, None]))
        sel_scale = gate.max(axis=1)[..., None]
        sel_idx = gate.argmax(axis=1)
        debias = jnp.take(debias_w, sel_idx, axis=0)
        bias = jnp.take(bias_w, sel_idx, axis=0)
        upd = jnp.take(lora_update, sel_idx, axis=0)
        dgn = jnp.take(lora_degen, sel_idx, axis=0)
        x_debias = x - debias
        mod_x = jnp.einsum('btdh,btd->bth', upd, x_debias)
        degen_up = jnp.einsum('btdh,bth->btd', dgn, mod_x)
        mod_x_bias = ETA * (bias + degen_up)
        return (1.0 - sel_scale) * x + sel_scale * mod_x_bias

    def _L1_attn_ref(x, Wq, Wk, Wv, Wo, bo):
        import jax, jax.numpy as jnp
        import numpy as np
        D_MODEL = 256
        NUM_HEADS = 16
        HEAD_DIM = D_MODEL // NUM_HEADS
        B, T, D = x.shape
        H, hd = (NUM_HEADS, HEAD_DIM)
        q = (x @ Wq).reshape(B, T, H, hd).transpose(0, 2, 1, 3)
        k = (x @ Wk).reshape(B, T, H, hd).transpose(0, 2, 1, 3)
        v = (x @ Wv).reshape(B, T, H, hd).transpose(0, 2, 1, 3)
        logits = jnp.einsum('bhqd,bhkd->bhqk', q, k) / jnp.sqrt(jnp.float32(hd))
        weights = jax.nn.softmax(logits, axis=-1)
        ctx = jnp.einsum('bhqk,bhkd->bhqd', weights, v)
        ctx = jnp.transpose(ctx, (0, 1, 3, 2)).reshape(B, T, D)
        return ctx @ Wo + bo

    def _L1_ffn_ref(x, G, gate_w, up_w, down_w, lora_A, lora_B):
        import jax, jax.numpy as jnp
        import numpy as np
        B, S, H = (4, 256, 256)
        E = 8
        F = H // E
        TOPK = 2
        LORA_R = 16
        LORA_SCALE = 1.0
        scores = jax.nn.softmax(jnp.einsum('bsh,he->bse', x, G), axis=-1)
        value, indices = jax.lax.top_k(scores, TOPK)
        onehot = jax.nn.one_hot(indices, E, dtype=value.dtype)
        w = jnp.einsum('bsk,bske->bse', value, onehot)
        gate = jax.nn.silu(jnp.einsum('bsh,efh->bsef', x, gate_w))
        up = jnp.einsum('bsh,efh->bsef', x, up_w)
        gated = gate * up
        out = jnp.einsum('bsef,bse,ehf->bsh', gated, w, down_w)
        lr = jnp.einsum('bsh,erh->bser', x, lora_A)
        out = out + LORA_SCALE * jnp.einsum('bser,bse,ehr->bsh', lr, w, lora_B)
        return out
    x = L0_attn_hidden_states
    x = _layernorm(x + _L0_attn_ref(x, L0_attn_Wq, L0_attn_bq, L0_attn_Wk, L0_attn_bk, L0_attn_Wv, L0_attn_bv, L0_attn_Wo), axis=-1)
    x = _layernorm(x + _L0_ffn_ref(x, L0_ffn_select_weight, L0_ffn_select_mean_diff, L0_ffn_imp_center, L0_ffn_imp_slope, L0_ffn_lora_update, L0_ffn_lora_degen, L0_ffn_bias_w, L0_ffn_debias_w), axis=-1)
    x = _layernorm(x + _L1_attn_ref(x, L1_attn_Wq, L1_attn_Wk, L1_attn_Wv, L1_attn_Wo, L1_attn_bo), axis=-1)
    x = _layernorm(x + _L1_ffn_ref(x, L1_ffn_G, L1_ffn_gate_w, L1_ffn_up_w, L1_ffn_down_w, L1_ffn_lora_A, L1_ffn_lora_B), axis=-1)
    return x

_drawn_inputs = setup_inputs


def setup_inputs(seed=0):
    import zlib

    import numpy as np

    out = dict(_drawn_inputs(seed))
    spreads = {'L0_attn_bq': (0.0, 2.0), 'L0_attn_bk': (0.0, 2.0), 'L0_attn_bv': (0.0, 0.1)}
    factors = {'L0_attn_Wq': 49.291,
     'L0_attn_Wk': 34.366,
     'L0_ffn_select_weight': 64.0,
     'L0_ffn_select_mean_diff': 64.0,
     'L0_ffn_debias_w': 27.904}
    for name, (base, spread) in spreads.items():
        noise = np.random.default_rng([zlib.crc32(name.encode()), seed]).standard_normal(out[name].shape)
        drawn = base * np.exp(spread * noise) if base else spread * noise
        out[name] = jnp.asarray(drawn.astype(out[name].dtype))
    for name, factor in factors.items():
        out[name] = (out[name] * factor).astype(out[name].dtype)
    return out
```

```python
from contextlib import ExitStack

import concourse.bass as bass
from concourse import mybir

F32 = mybir.dt.float32
F32R = mybir.dt.float32r
ALU = mybir.AluOpType
ACT = mybir.ActivationFunctionType
AX = mybir.AxisListType

P = 128
B, T, D = 4, 512, 256
KD = D // P
NT = T // P
LN_EPS = 1e-5

H0, G0, DH0 = 16, 4, 128
J0 = H0 // G0
DEN_EPS = 1e-6
ORDER0 = [(g, j) for j in range(J0) for g in range(G0)]


def split_passes(lhs_hi, lhs_lo, rhs_hi, rhs_lo):
    return [(lhs_lo, rhs_hi), (lhs_hi, rhs_lo), (lhs_hi, rhs_hi)]


def rows(x):
    return x.rearrange("b (c p h) d -> p (b c) (h d)", p=P, h=2)


def tiles(x, b):
    return x[:, NT * b:NT * (b + 1), :] if isinstance(b, int) else x[:, bass.ds(NT * b, NT), :]


class Steps:

    def __init__(self, eng, sem, each, b):
        self.eng, self.sem, self.base, self.n = eng, sem, each * b, 0

    def __call__(self, *instructions):
        for ins in instructions:
            self.n += 1
            ins.then_inc(self.sem, 1)
        self.eng.wait_ge(self.sem, self.base + self.n)


MERGE_STEPS = 4


def merge_stats(dve, step, bn, tmp, mean, var):
    half_n = D // 2
    mean_e, m2_e, mean_o, m2_o = (bn[:, :, i:i + 1] for i in (1, 2, 4, 5))
    dist, m2, dist2 = (tmp[:, :, i:i + 1] for i in range(3))
    step(dve.tensor_tensor(dist, mean_e, mean_o, ALU.subtract),
         dve.scalar_tensor_tensor(out=m2, in0=m2_e, scalar=2 * half_n * LN_EPS, in1=m2_o, op0=ALU.add, op1=ALU.add))
    step(dve.scalar_tensor_tensor(out=mean, in0=dist, scalar=-0.5, in1=mean_e, op0=ALU.mult, op1=ALU.add),
         dve.scalar_tensor_tensor(out=dist2, in0=dist, scalar=0.25, in1=dist, op0=ALU.mult, op1=ALU.mult))
    return dve.scalar_tensor_tensor(out=var, in0=m2, scalar=1 / (2 * half_n), in1=dist2, op0=ALU.mult, op1=ALU.add)


def layer0_attention(nc, a, xs, stats):
    with ExitStack() as ctx:
        def sb(name, shape, dt=F32):
            return ctx.enter_context(nc.sbuf_tensor(name, [P] + shape, dt))

        def ps(name):
            return ctx.enter_context(nc.psum_tensor(name, [P, 512], F32))

        def sem(name):
            return ctx.enter_context(nc.semaphore(name))

        wkv_hi, wkv_lo = sb("wkv_hi", [KD, 1024], F32R), sb("wkv_lo", [KD, 1024], F32R)
        wq_hi, wq_lo = sb("wq_hi", [KD, H0 * DH0], F32R), sb("wq_lo", [KD, H0 * DH0], F32R)
        wo = sb("wo0", [H0, D])
        bq, bq1, bq_neg = sb("bq", [H0]), sb("bq1", [H0]), sb("bq_neg", [H0])
        bk, bv = sb("bk", [512]), sb("bv", [512])
        ones = sb("ones0", [1])
        part_c, part_m = sb("part_c", [1]), sb("part_m", [1])
        pick_raw, pick = sb("pick_raw", [H0]), sb("pick", [H0], F32R)
        xT = sb("xT", [KD, T])
        xT_hi, xT_lo = sb("xT_hi", [KD, T], F32R), sb("xT_lo", [KD, T], F32R)
        zk, ek = sb("zk", [2, 512]), sb("ek", [2, 512])
        sk, v = sb("sk", [NT, 512]), sb("v0", [NT, 512])
        kvT = sb("kvT", [512])
        ksel = sb("ksel", [G0, J0, 32])
        eq = sb("eq", [3, T])
        sq = sb("sq", [H0, T])
        stage = sq[:, 0:8, :].rearrange("p (s c) n -> p s (c n)", s=2)
        den, rn = sb("den", [T]), sb("rn", [T])
        rn_c, rn_parts = sb("rn_c", [T], F32R), sb("rn_parts", [T], F32R)
        m_hi, m_lo = sb("m_hi", [4, 2 * D], F32R), sb("m_lo", [4, 2 * D], F32R)
        s_hi, s_lo = sb("s_hi", [2, T], F32R), sb("s_lo", [2, T], F32R)
        res = sb("res", [NT, D])
        bn, bn_tmp = sb("bn0", [NT, 6]), sb("bn0_tmp", [NT, 3])

        bank_a = [ps("bank_a0"), ps("bank_a1")]
        bank_q = [ps(f"bank_q{i}") for i in range(3)]
        bank_n = ps("bank_n")
        bank_y = ctx.enter_context(nc.psum_tensor("bank_y", [P, 2, 512], F32))
        bank_y4 = bank_y[:, :, :].rearrange("p a (t n) -> p (a t) n", t=2)

        small_in = sem("small_in")
        wo_in, x_in, xT_in = sem("wo_in"), sem("x_in"), sem("xT_in")
        stage_in = [sem("stage_in0"), sem("stage_in1")]
        w_hi_ready, w_lo_ready = sem("w_hi_ready"), sem("w_lo_ready")
        setup_done = sem("setup_done")
        xT_hi_ready, xT_lo_ready = sem("xT_hi_ready"), sem("xT_lo_ready")
        k_done, v_done = sem("k_done"), sem("v_done")
        zk_ready, v_ready, ek_ready = sem("zk_ready"), sem("v_ready"), sem("ek_ready")
        ek_capped, sk_ready = sem("ek_capped"), sem("sk_ready")
        kvT_done, ksum_done, kvT_ready, ksel_ready = sem("kvT_done"), sem("ksum_done"), sem("kvT_ready"), sem("ksel_ready")
        q_done, eq_ready, eq_capped, sq_ready = sem("q_done"), sem("eq_ready"), sem("eq_capped"), sem("sq_ready")
        norm_done, den_ready, rn_ready, rn_c_ready, parts_ready = (
            sem("norm_done"), sem("den_ready"), sem("rn_ready"), sem("rn_c_ready"), sem("parts_ready"))
        m_done, m_hi_ready, m_lo_ready = sem("m_done"), sem("m_hi_ready"), sem("m_lo_ready")
        bc_done, scaled, s_hi_ready, s_lo_ready = sem("bc_done"), sem("scaled"), sem("s_hi_ready"), sem("s_lo_ready")
        y_done, res_ready, res_kept = sem("y_done"), sem("res_ready"), sem("res_kept")
        bn_ready, merge_step, stats_ready = sem("bn_ready"), sem("merge_step"), sem("stats_ready")

        W_STAGES = [("kv", None), ("q", 0), ("q", 1)]
        N_SMALL = 7

        def w_parts(s):
            kind, k = W_STAGES[s]
            if kind == "kv":
                return wkv_hi[:, :, :].rearrange("p k n -> p (k n)"), wkv_lo[:, :, :].rearrange("p k n -> p (k n)")
            return wq_hi[:, k, :], wq_lo[:, k, :]

        block = ctx.enter_context(nc.Block())

        @block.sync
        def _(sp):
            sp.dma_start(stage[:, 0, :], a["wkvT0"]).then_inc(stage_in[0], 16)
            sp.dma_start(xT[:, :, :], a["xT"][:, 0]).then_inc(xT_in, 16)
            sp.dma_start(stage[:, 1, :], a["wqT0"][:, 0]).then_inc(stage_in[1], 16)
            for dst, name in ((bk, "bk"), (bv, "bv"), (bq, "bq"), (pick_raw, "pick"), (part_c, "part_c"),
                              (part_m, "part_m"), (ones, "ones")):
                sp.dma_start(dst[:, :], a[name]).then_inc(small_in, 16)
            sp.dma_start(wo[:, :, :], a["woT0"]).then_inc(wo_in, 16)
            sp.wait_ge(w_lo_ready, 1)
            sp.dma_start(stage[:, 0, :], a["wqT0"][:, 1]).then_inc(stage_in[0], 16)
            sp.dma_start(xs[:, :, :].rearrange("p (c h) d -> p c (h d)", h=2), rows(a["x"])).then_inc(x_in, 16)
            with sp.Fori(0, B - 1) as b:
                after = sp.snap(b + 1)
                sp.wait_ge(xT_hi_ready, after)
                sp.wait_ge(xT_lo_ready, after)
                sp.dma_start(xT[:, :, :], a["xT"][:, bass.ds(after, 1)].rearrange("p o k n -> p (o k) n")).then_inc(xT_in, 16)

        @block.gpsimd
        def _(pool):
            pool.memset(ksel[:, :, :, :], 0.0).then_inc(setup_done, 1)
            with pool.Fori(0, B) as b:
                pool.wait_ge(res_ready, b + 1)
                pool.tensor_copy(tiles(xs, b), res[:, :, :]).then_inc(res_kept, 1)

        @block.tensor
        def _(pe):
            def key_value(b, t):
                tok = slice(t * P, (t + 1) * P)
                for part, (bank, done) in enumerate(((bank_a[0], k_done), (bank_a[1], v_done))):
                    if t == 0:
                        pe.wait_ge(m_lo_ready, 8 * b)
                    else:
                        pe.wait_ge((zk_ready, v_ready)[part], NT * b + t)
                    cols = slice(part * 512, (part + 1) * 512)
                    n = 0
                    for k in range(KD):
                        for lhs, rhs in split_passes(xT_hi[:, k, tok], xT_lo[:, k, tok], wkv_hi[:, k, cols], wkv_lo[:, k, cols]):
                            mm = pe.matmul(bank[:, :], lhs, rhs, start=n == 0, stop=n == 3 * KD - 1)
                            n += 1
                    mm.then_inc(done, 1)

            def state(b):
                pe.wait_ge(v_ready, NT * b + NT)
                pe.wait_ge(sk_ready, NT * b + NT)
                for g in range(G0):
                    hd = slice(g * DH0, (g + 1) * DH0)
                    for t in range(NT):
                        mm = pe.matmul(bank_a[0][:, hd], v[:, t, hd], sk[:, t, hd], start=t == 0, stop=t == NT - 1)
                mm.then_inc(kvT_done, 1)
                for g in range(G0):
                    hd = slice(g * DH0, (g + 1) * DH0)
                    for t in range(NT):
                        mm = pe.matmul(bank_a[1][:, g:g + 1], sk[:, t, hd], ones[:, :], start=t == 0, stop=t == NT - 1)
                mm.then_inc(ksum_done, 1)

            def query(b, n):
                g, j = ORDER0[n]
                hd = slice((J0 * g + j) * DH0, (J0 * g + j + 1) * DH0)
                if n < 3:
                    pe.wait_ge(scaled, H0 * b)
                else:
                    pe.wait_ge(sq_ready, H0 * b + n - 2)
                i = 0
                for k in range(KD):
                    for lhs, rhs in split_passes(wq_hi[:, k, hd], wq_lo[:, k, hd], xT_hi[:, k, :], xT_lo[:, k, :]):
                        mm = pe.matmul(bank_q[n % 3][:, :], lhs, rhs, start=i == 0, stop=i == 3 * KD - 1)
                        i += 1
                mm.then_inc(q_done, 1)

            def norm(b, j):
                if j == 0:
                    pe.wait_ge(ksel_ready, b + 1)
                    pe.wait_ge(den_ready, b)
                pe.wait_ge(sq_ready, H0 * b + G0 * (j + 1))
                for g in range(G0):
                    mm = pe.matmul(bank_n[32 * g:32 * g + 32, :], ksel[:, g, j, :], sq[:, G0 * j + g, :],
                                   start=j == 0, stop=j == J0 - 1)
                if j == J0 - 1:
                    mm.then_inc(norm_done, 1)

            def output_map(b, p):
                if p == 0:
                    pe.wait_ge(kvT_ready, b + 1)
                elif p == 1:
                    pe.wait_ge(ksel_ready, b + 1)
                else:
                    pe.wait_ge(m_lo_ready, 8 * b + p - 1)
                for i in range(2):
                    g, j = ORDER0[2 * p + i]
                    mm = pe.matmul(bank_a[p % 2][:, i * D:(i + 1) * D], kvT[:, g * DH0:(g + 1) * DH0], wo[:, J0 * g + j, :],
                                   start=True, stop=True)
                mm.then_inc(m_done, 1)

            def factor(b, n):
                g, j = ORDER0[n]
                h = J0 * g + j
                if n == 0:
                    pe.wait_ge(parts_ready, b + 1)
                if n < 3:
                    pe.wait_ge(sq_ready, H0 * b + H0)
                else:
                    pe.wait_ge(scaled, H0 * b + n - 2)
                pe.matmul(bank_q[(H0 + n) % 3][:, :], pick[:, h:h + 1].broadcast_to([P, P]), rn_parts[:, :],
                          start=True, stop=True).then_inc(bc_done, 1)

            def project(b, n):
                if n == 0:
                    pe.wait_ge(res_ready, b)
                pe.wait_ge(s_hi_ready, H0 * b + n + 1)
                pe.wait_ge(s_lo_ready, H0 * b + n + 1)
                if n % 2 == 0:
                    pe.wait_ge(m_lo_ready, 8 * b + n // 2 + 1)
                m = (n // 2) % 4
                cols = slice((n % 2) * D, (n % 2 + 1) * D)
                for t in range(NT):
                    tok = slice(t * P, (t + 1) * P)
                    for i, (lhs, rhs) in enumerate(split_passes(s_hi[:, n % 2, tok], s_lo[:, n % 2, tok], m_hi[:, m, cols], m_lo[:, m, cols])):
                        mm = pe.matmul(bank_y4[:, t, :], lhs, rhs,
                                       start=n == 0 and i == 0 and t % 2 == 0, stop=n == H0 - 1 and i == 2,
                                       skip_group_check=True)
                mm.then_inc(y_done, 1)

            pe.wait_ge(w_lo_ready, 1)
            pe.wait_ge(w_hi_ready, 1)
            with pe.Fori(0, B) as b:
                pe.wait_ge(xT_hi_ready, b + 1)
                pe.wait_ge(xT_lo_ready, b + 1)
                for t in range(NT):
                    key_value(b, t)
                pe.wait_ge(w_hi_ready, len(W_STAGES))
                pe.wait_ge(w_lo_ready, len(W_STAGES))
                for n in range(3):
                    query(b, n)
                pe.wait_ge(small_in, 16 * N_SMALL)
                state(b)
                for n in range(3, H0):
                    query(b, n)
                    if n % G0 == 1 and n > G0:
                        norm(b, n // G0 - 1)
                pe.wait_ge(wo_in, 16)
                output_map(b, 0)
                output_map(b, 1)
                norm(b, J0 - 1)
                output_map(b, 2)
                output_map(b, 3)
                pe.wait_ge(setup_done, 4)
                factor(b, 0)
                factor(b, 1)
                for n in range(H0):
                    if n + 2 < H0:
                        factor(b, n + 2)
                    project(b, n)
                    if n % 2 == 1 and n < 8:
                        output_map(b, 4 + n // 2)

        @block.scalar
        def _(act):
            def split_x(b):
                act.wait_ge(xT_in, 16 * (b + 1))
                act.wait_ge(q_done, H0 * b)
                act.activation(xT_hi[:, :, :], xT[:, :, :], ACT.Copy).then_inc(xT_hi_ready, 1)

            def map_hi(b, p):
                act.wait_ge(m_done, 8 * b + p + 1)
                act.wait_ge(y_done, H0 * b + max(0, 2 * (p - 4) + 2))
                act.activation(m_hi[:, p % 4, :], bank_a[p % 2][:, :], ACT.Copy).then_inc(m_hi_ready, 1)

            def query_exp(b, n):
                g, j = ORDER0[n]
                h = J0 * g + j
                act.wait_ge(q_done, H0 * b + n + 1)
                act.wait_ge(sq_ready, H0 * b + max(0, n - 2))
                act.activation(eq[:, n % 3, :], bank_q[n % 3][:, :], ACT.Relu, bias=bq_neg[:, h:h + 1], scale=-1.0).then_inc(eq_capped, 1)
                act.wait_ge(eq_capped, H0 * b + n + 1)
                act.activation(eq[:, n % 3, :], eq[:, n % 3, :], ACT.Exp, scale=-1.0).then_inc(eq_ready, 1)

            def body(b, more):
                for t in range(NT):
                    act.wait_ge(zk_ready, NT * b + t + 1)
                    act.wait_ge(sk_ready, NT * b + max(0, t - 1))
                    act.activation(ek[:, t % 2, :], zk[:, t % 2, :], ACT.Relu, scale=-1.0).then_inc(ek_capped, 1)
                    act.wait_ge(ek_capped, NT * b + t + 1)
                    act.activation(ek[:, t % 2, :], ek[:, t % 2, :], ACT.Exp, scale=-1.0).then_inc(ek_ready, 1)
                for n in range(3):
                    query_exp(b, n)
                act.wait_ge(kvT_done, b + 1)
                act.wait_ge(m_done, 8 * b)
                act.activation(kvT[:, :], bank_a[0][:, :], ACT.Copy).then_inc(kvT_ready, 1)
                for n in range(3, H0):
                    query_exp(b, n)
                map_hi(b, 0)
                map_hi(b, 1)
                act.wait_ge(rn_ready, b + 1)
                act.wait_ge(parts_ready, b)
                act.activation(rn_c[:, :], rn[:, :], ACT.Copy, scale=part_c[:, 0:1]).then_inc(rn_c_ready, 1)
                map_hi(b, 2)
                map_hi(b, 3)
                for n in range(H0):
                    act.wait_ge(scaled, H0 * b + n + 1)
                    act.wait_ge(y_done, H0 * b + max(0, n - 1))
                    act.activation(s_hi[:, n % 2, :], sq[:, n, :], ACT.Copy).then_inc(s_hi_ready, 1)
                    if n in (3, 5, 7, 9):
                        map_hi(b, 4 + (n - 3) // 2)
                    if n == 10 and more:
                        split_x(b + 1)

            for s in range(len(W_STAGES)):
                act.wait_ge(stage_in[s % 2], 16 * (s // 2 + 1))
                act.activation(w_parts(s)[0], stage[:, s % 2, :], ACT.Copy).then_inc(w_hi_ready, 1)
                if s == 0:
                    split_x(0)
            act.wait_ge(small_in, 16 * N_SMALL)
            act.activation(bq1[:, :], bq[:, :], ACT.Copy, bias=1.0).then_inc(setup_done, 1)
            act.activation(bq_neg[:, :], bq[:, :], ACT.Copy, scale=-1.0).then_inc(setup_done, 1)
            act.activation(pick[:, :], pick_raw[:, :], ACT.Copy).then_inc(setup_done, 1)
            act.wait_ge(setup_done, 4)
            with act.Fori(0, B - 1) as b:
                body(b, True)
            body(B - 1, False)

        @block.vector
        def _(dve):
            def split_x(b):
                dve.wait_ge(xT_hi_ready, b + 1)
                dve.wait_ge(q_done, H0 * b)
                dve.tensor_tensor(xT_lo[:, :, :], xT[:, :, :], xT_hi[:, :, :].bitcast(F32), ALU.subtract).then_inc(xT_lo_ready, 1)

            def finish_key(b, t):
                dve.wait_ge(ek_ready, NT * b + t + 1)
                dve.scalar_tensor_tensor(out=sk[:, t, :], in0=zk[:, t % 2, :], scalar=1.0, in1=ek[:, t % 2, :],
                                         op0=ALU.add, op1=ALU.max).then_inc(sk_ready, 1)

            def key_value(b):
                for t in range(NT):
                    if t == 0:
                        dve.wait_ge(ksum_done, b)
                    else:
                        dve.wait_ge(sk_ready, NT * b + max(0, t - 1))
                    dve.wait_ge(k_done, NT * b + t + 1)
                    dve.tensor_tensor(zk[:, t % 2, :], bank_a[0][:, :], bk[:, :], ALU.add).then_inc(zk_ready, 1)
                    dve.wait_ge(v_done, NT * b + t + 1)
                    dve.tensor_tensor(v[:, t, :], bank_a[1][:, :], bv[:, :], ALU.add).then_inc(v_ready, 1)
                    if t > 0:
                        finish_key(b, t - 1)
                finish_key(b, NT - 1)

            def query(b, n):
                g, j = ORDER0[n]
                h = J0 * g + j
                dve.wait_ge(eq_ready, H0 * b + n + 1)
                dve.scalar_tensor_tensor(out=sq[:, n, :], in0=bank_q[n % 3][:, :], scalar=bq1[:, h:h + 1], in1=eq[:, n % 3, :],
                                         op0=ALU.add, op1=ALU.max).then_inc(sq_ready, 1)

            def map_lo(b, p):
                dve.wait_ge(m_hi_ready, 8 * b + p + 1)
                dve.tensor_tensor(m_lo[:, p % 4, :], bank_a[p % 2][:, :], m_hi[:, p % 4, :].bitcast(F32), ALU.subtract).then_inc(m_lo_ready, 1)

            def scaled_lo(b, n):
                dve.wait_ge(s_hi_ready, H0 * b + n + 1)
                dve.wait_ge(scaled, H0 * b + n + 1)
                dve.tensor_tensor(s_lo[:, n % 2, :], sq[:, n, :], s_hi[:, n % 2, :].bitcast(F32), ALU.subtract).then_inc(s_lo_ready, 1)

            def body(b, more):
                key_value(b)
                dve.wait_ge(s_hi_ready, H0 * b)
                dve.wait_ge(s_lo_ready, H0 * b)
                for n in range(3):
                    query(b, n)
                dve.wait_ge(ksum_done, b + 1)
                dve.wait_ge(norm_done, b)
                for g in range(G0):
                    dst = ksel[:, g, :, :].rearrange("p j c -> p (j c)")
                    for r in range(2):
                        cp = dve.tensor_copy(dst[:, 4 * r:4 * r + 3 * 33 + 1:33], bank_a[1][:, g:g + 1].broadcast_to([P, J0]))
                cp.then_inc(ksel_ready, 1)
                for n in range(3, H0):
                    query(b, n)
                map_lo(b, 0)
                map_lo(b, 1)
                dve.wait_ge(norm_done, b + 1)
                dve.tensor_scalar(den[:, :], bank_n[:, :], DEN_EPS, None, ALU.add).then_inc(den_ready, 1)
                dve.wait_ge(den_ready, b + 1)
                dve.reciprocal(rn[:, :], den[:, :]).then_inc(rn_ready, 1)
                dve.wait_ge(rn_c_ready, b + 1)
                dve.wait_ge(rn_ready, b + 1)
                dve.wait_ge(bc_done, H0 * b)
                dve.scalar_tensor_tensor(out=rn_parts[:, :], in0=rn[:, :], scalar=part_m[:, 0:1], in1=rn_c[:, :].bitcast(F32),
                                         op0=ALU.mult, op1=ALU.add).then_inc(parts_ready, 1)
                map_lo(b, 2)
                map_lo(b, 3)
                for n in range(H0):
                    dve.wait_ge(bc_done, H0 * b + n + 1)
                    dve.tensor_tensor(sq[:, n, :], sq[:, n, :], bank_q[(H0 + n) % 3][:, :], ALU.mult).then_inc(scaled, 1)
                    if n > 0:
                        scaled_lo(b, n - 1)
                    if n in (4, 6, 8, 10):
                        map_lo(b, 4 + (n - 4) // 2)
                    if n == 12 and more:
                        split_x(b + 1)
                scaled_lo(b, H0 - 1)
                dve.wait_ge(y_done, H0 * b + H0)
                dve.wait_ge(res_kept, b)
                dve.tensor_tensor(res[:, :, :], bank_y4, tiles(xs, b), ALU.add).then_inc(res_ready, 1)
                dve.wait_ge(res_ready, b + 1)
                for t in range(NT):
                    dve.bn_stats(bn[:, t, :], res[:, t, :]).then_inc(bn_ready, 1)
                dve.wait_ge(bn_ready, NT * (b + 1))
                merge_stats(dve, Steps(dve, merge_step, MERGE_STEPS, b), bn, bn_tmp,
                            tiles(stats, b)[:, :, 0:1], tiles(stats, b)[:, :, 1:2]).then_inc(stats_ready, 1)

            for s in range(len(W_STAGES)):
                dve.wait_ge(w_hi_ready, s + 1)
                hi, lo = w_parts(s)
                dve.tensor_tensor(lo, stage[:, s % 2, :], hi.bitcast(F32), ALU.subtract).then_inc(w_lo_ready, 1)
                if s == 0:
                    split_x(0)
            dve.wait_ge(setup_done, 4)
            dve.wait_ge(small_in, 16 * N_SMALL)
            dve.wait_ge(x_in, 16)
            dve.wait_ge(w_lo_ready, len(W_STAGES))
            with dve.Fori(0, B - 1) as b:
                body(b, True)
            body(B - 1, False)


E0, S0, R0 = 8, 8, 8
W0 = E0 * (S0 + R0) + E0
U0 = E0 * R0 + E0
Z_MIN = -85.0
H1, DH1 = 16, 16
SCALE1 = DH1 ** -0.5
ROWS_S = 3 * DH1
ROWS_ST = ROWS_S + 2
SUBS = 16
LEAD = 6
SLOTS = 8
E1, F1, R1 = 8, 32, 16
WA = E1 * F1 + E1 * R1
WB = E1 * F1 + E1


def at_least(eng, sem, value):
    if not isinstance(value, int) or value > 0:
        eng.wait_ge(sem, value)


def tile(x, b, t):
    return x[:, NT * b + t, :] if isinstance(b, int) else x[:, bass.ds(NT * b + t, 1), :].rearrange("p o n -> p (o n)")


def by_tile(x):
    return x[:, :].rearrange("p (t o) -> p t o", o=1)


def over_last(x, n):
    return x.rearrange("p (a o) -> p a o", o=1).broadcast_to([x.shape[0], x.shape[1], n])


def over_tiles(x):
    return x.rearrange("p (o n) -> p o n", o=1).broadcast_to([P, NT, x.shape[1]])


def update_attention_experts(nc, a, xs, stats, out):
    with ExitStack() as ctx:
        def sb(name, shape, dt=F32, parts=P):
            return ctx.enter_context(nc.sbuf_tensor(name, [parts] + shape, dt))

        def sem(name):
            return ctx.enter_context(nc.semaphore(name))

        ident, ones = sb("ident", [P]), sb("ones1", [P])
        fw, md = sb("fw", [KD, W0]), sb("md", [KD, 2 * E0])
        fprod, fconst = sb("fprod", [KD, W0]), sb("fconst", [W0])
        slope, center, rank = sb("slope", [E0]), sb("center", [E0]), sb("rank", [E0])
        down0 = sb("down0", [D], parts=U0)
        wqkv_hi, wqkv_lo = sb("wqkv_hi", [KD, 3 * D], F32R), sb("wqkv_lo", [KD, 3 * D], F32R)
        wo, bo = sb("wo1", [2, D]), sb("bo", [D])
        win_hi, win_lo = sb("win_hi", [KD, WA + WB], F32R), sb("win_lo", [KD, WA + WB], F32R)
        down1 = sb("down1", [3, D])
        half = sb("half", [B * NT])
        rstd1 = sb("rstd1", [B * NT])
        xf = sb("xf", [NT, D])
        ssq, junk = sb("ssq", [NT]), sb("junk", [NT, D], mybir.dt.bfloat16)
        pr, pr2 = sb("pr", [NT, W0]), sb("pr2", [NT, E0 * S0])
        gt = {n: sb(f"gt_{n}", [NT, E0]) for n in (
            "score", "dist", "rdist", "rel", "cent", "z", "zc", "e", "e1", "gate", "eq", "key", "pick", "w")}
        gmax, kmax, keep = sb("gmax", [NT]), sb("kmax", [NT]), sb("keep", [NT])
        hm = sb("hm", [NT, U0])
        hmT = sb("hmT", [T], parts=U0)
        x2T_hi, x2T_lo = sb("x2T_hi", [KD, T], F32R), sb("x2T_lo", [KD, T], F32R)
        qk_hi, qk_lo = sb("qk_hi", [2, T], F32R), sb("qk_lo", [2, T], F32R)
        qs, ks = sb("qs", [H1, T], F32R, parts=64), sb("ks", [H1, T], F32R, parts=64)
        v = sb("v1", [NT, H1, 32])
        nmax = sb("nmax", [4, NT, 4])
        sh_hi, sh_lo = sb("sh_hi", [T], F32R, parts=4), sb("sh_lo", [T], F32R, parts=4)
        probs = sb("probs", [SLOTS, T])
        raw = probs[:, :, :].rearrange("p s n -> p (s n)")
        ctT, rsum, cx = sb("ctT", [T]), sb("rsum", [NT, 4]), sb("cx", [NT, D])
        xk = sb("xk", [NT, D])
        x3T_hi, x3T_lo = sb("x3T_hi", [KD, T], F32R), sb("x3T_lo", [KD, T], F32R)
        th, sg = sb("th", [2, E1 * F1]), sb("sg", [E1 * F1])
        hid = sb("hid", [NT, 3 * P])
        turned = sb("turned", [3, T])
        hidT, x1T = turned, turned[:, 0:KD, :]
        lg = sb("lg", [NT, E1])
        rt = {n: sb(f"rt_{n}", [NT, E1]) for n in (
            "rel", "e", "sc", "eq1", "key1", "pick1", "less", "eq2", "key2", "pick2", "both", "w", "wh")}
        rm = {n: sb(f"rm_{n}", [NT]) for n in ("max", "sum", "rsum", "max1", "kmax1", "max2", "kmax2")}
        ln = {i: {"bn": sb(f"ln{i}_bn", [NT, 6]), "tmp": sb(f"ln{i}_tmp", [NT, 3]), "mean": sb(f"ln{i}_mean", [NT]), "var": sb(f"ln{i}_var", [NT]),
                  "rstd": sb(f"ln{i}_rstd", [NT])} for i in (2, 3, 4)}
        scratch = nc.dram_tensor("scratch_qk", (4, 2, P, T), F32, kind="Internal").ap()

        side = ctx.enter_context(nc.psum_tensor("side", [P, 2, 512], F32))
        side4 = side[:, :, :].rearrange("p a (t n) -> p (a t) n", t=2)
        bank_s = [ctx.enter_context(nc.psum_tensor(f"bank_s{i}", [P, 512], F32)) for i in range(2)]
        bank_st = [ctx.enter_context(nc.psum_tensor(f"bank_st{i}", [P, 512], F32)) for i in range(2)]
        bank_c = ctx.enter_context(nc.psum_tensor("bank_c", [P, 512], F32))
        bank_t = ctx.enter_context(nc.psum_tensor("bank_t", [P, 512], F32))

        consts_in, raw_in = sem("consts_in"), [sem("raw_in0"), sem("raw_in1")]
        w_hi_ready, w_lo_ready = sem("w1_hi_ready"), sem("w1_lo_ready")
        half_ready, zeros_ready, v_ones_ready, k_ones_ready = sem("half_ready"), sem("zeros_ready"), sem("v_ones_ready"), sem("k_ones_ready")
        fprod_ready, fsum_done, fconst_ready = sem("fprod_ready"), sem("fsum_done"), sem("fconst_ready")
        rstd1_ready, x1_ready = sem("rstd1_ready"), sem("x1_ready")
        x1T_done, x1T_ready, ssq_ready = sem("x1T_done"), sem("x1T_ready"), sem("ssq_ready")
        pr_done, pr_ready, gate_step, zc_ready, ge_ready, hm_ready = (
            sem("pr_done"), sem("pr_ready"), sem("gate_step"), sem("zc_ready"), sem("ge_ready"), sem("hm_ready"))
        hmT_done, hmT_ready, up_done, r2_ready = sem("hmT_done"), sem("hmT_ready"), sem("up_done"), sem("r2_ready")
        bn_ready, merge_step, var_ready, rstd_ready, x_ready = (
            {i: sem(f"ln{i}_{n}_ready") for i in (2, 3, 4)} for n in ("bn", "merge", "var", "rstd", "x"))
        x2T_done, x2T_hi_ready, x2T_lo_ready, x2_kept = sem("x2T_done"), sem("x2T_hi_ready"), sem("x2T_lo_ready"), sem("x2_kept")
        qk_done, qk_hi_ready, qk_lo_ready = sem("qk_done"), sem("qk_hi_ready"), sem("qk_lo_ready")
        scratch_out = [sem("scratch_out0"), sem("scratch_out1")]
        stack_in = [sem("stack_in0"), sem("stack_in1")]
        vp_done, v_ready = sem("vp_done"), sem("v1_ready")
        s_done, max_ready = sem("s_done"), sem("max_ready")
        maxT_done, sh_hi_ready, sh_lo_ready, shift_in = sem("maxT_done"), sem("sh_hi_ready"), sem("sh_lo_ready"), sem("shift_in")
        st_done, p_ready, pv_done = sem("st_done"), sem("p_ready"), sem("pv_done")
        ct_ready, ctT_done, rsum_ready, cx_ready = sem("ct_ready"), sem("ctT_done"), sem("rsum_ready"), sem("cx_ready")
        wo_done, r3_ready = sem("wo_done"), sem("r3_ready")
        x3T_done, x3T_hi_ready, x3T_lo_ready = sem("x3T_done"), sem("x3T_hi_ready"), sem("x3T_lo_ready")
        in_done, in_copied, sg_ready, hid_ready = sem("in_done"), sem("in_copied"), sem("sg_ready"), sem("hid_ready")
        route_step, rel_ready, re_ready, hw_ready = sem("route_step"), sem("rel_ready"), sem("re_ready"), sem("hw_ready")
        hidT_done, hidT_ready, down_done, r4_ready, stored = (
            sem("hidT_done"), sem("hidT_ready"), sem("down_done"), sem("r4_ready"), sem("stored"))

        CONSTS = [(ident, "ident"), (ones, "ones_pp"), (fw, "fw"), (md, "md"), (slope, "slope"), (center, "center"),
                  (rank, "rank"), (down0, "down0"), (wo, "wo1"), (bo, "bo"), (down1, "down1")]

        def whole(t):
            return t[tuple(slice(None) for _ in t.shape)]

        block = ctx.enter_context(nc.Block())

        @block.sync
        def _(sp):
            def save_qk(b):
                for i in range(4):
                    sp.wait_ge(qk_hi_ready, 4 * b + i + 1)
                    sp.dma_start(scratch[i, 0], qk_hi[:, i % 2, :].bitcast(F32)).then_inc(scratch_out[i % 2], 16)
                    sp.wait_ge(qk_lo_ready, 4 * b + i + 1)
                    sp.dma_start(scratch[i, 1], qk_lo[:, i % 2, :].bitcast(F32)).then_inc(scratch_out[i % 2], 16)

            def load_stack(b, half_):
                if half_:
                    at_least(sp, st_done, 64 * b)
                else:
                    for i in range(2):
                        sp.wait_ge(scratch_out[i], 64 * (b + 1))
                heads = slice(8 * half_, 8 * half_ + 8)
                for w, (stack, parts) in enumerate(((qs, (0, 1, 0)), (ks, (0, 0, 1)))):
                    for i, part in enumerate(parts):
                        sp.dma_start(stack[DH1 * i:DH1 * (i + 1), heads, :].bitcast(F32),
                                     scratch[2 * w + half_, part].rearrange("(h p) n -> p h n", p=DH1)).then_inc(stack_in[half_], 16)

            def shift(b, g):
                sp.wait_ge(sh_lo_ready, 4 * b + g + 1)
                for i, part in enumerate((sh_hi, sh_lo)):
                    sp.dma_start(qs[ROWS_S + i:ROWS_S + i + 1, 4 * g:4 * g + 4, :].bitcast(F32), part[:, :].bitcast(F32)).then_inc(shift_in, 16)

            def store(b):
                sp.wait_ge(x_ready[4], NT * (b + 1))
                dst = out.rearrange("b (c p h) d -> b p c (h d)", p=P, h=2)
                dst = dst[b] if isinstance(b, int) else dst[bass.ds(b, 1)].rearrange("o p c n -> (o p) c n")
                sp.dma_start(dst, xk[:, :, :].rearrange("p (c h) d -> p c (h d)", h=2)).then_inc(stored, 16)

            def body(b, front, back):
                load_stack(b, 1)
                shift(b, 1)
                shift(b, 2)
                if front:
                    save_qk(b + 1)
                    load_stack(b + 1, 0)
                shift(b, 3)
                if front:
                    shift(b + 1, 0)
                if back:
                    store(b - 1)

            sp.dma_start(raw[:, 0:KD * 3 * D], a["wqkv1"]).then_inc(raw_in[0], 16)
            for dst, name in CONSTS:
                sp.dma_start(whole(dst), a[name]).then_inc(consts_in, 16)
            sp.dma_start(raw[:, KD * 3 * D:KD * (3 * D + WA + WB)], a["win1"]).then_inc(raw_in[1], 16)
            sp.wait_ge(k_ones_ready, 1)
            save_qk(0)
            load_stack(0, 0)
            shift(0, 0)
            body(0, True, False)
            with sp.Fori(1, B - 1) as b:
                body(b, True, True)
            body(B - 1, False, True)
            store(B - 1)
            sp.wait_ge(stored, 16 * B)

        @block.gpsimd
        def _(pool):
            def rstd(i, b):
                pool.wait_ge(var_ready[i], b + 1)
                pool.tensor_tensor(ln[i]["rstd"][:, :], ln[i]["var"][:, :], half[:, 0:NT], ALU.pow).then_inc(rstd_ready[i], 1)

            def keep_x2(b):
                pool.wait_ge(x2T_done, b + 1)
                pool.tensor_tensor(tiles(xs, b), xf[:, :, :], over_tiles(bo[:, :]), ALU.add).then_inc(x2_kept, 1)

            def body(b, front, back):
                if back:
                    rstd(3, b - 1)
                if front:
                    rstd(2, b + 1)
                    keep_x2(b + 1)
                if back:
                    rstd(4, b - 1)

            pool.memset(half[:, :], -0.5).then_inc(half_ready, 1)
            pool.wait_ge(half_ready, 1)
            pool.tensor_tensor(rstd1[:, :].rearrange("p (t o) -> p t o", o=1), stats[:, :, 1:2], half[:, :].rearrange("p (t o) -> p t o", o=1), ALU.pow).then_inc(rstd1_ready, 1)
            pool.wait_ge(rstd1_ready, 1)
            pool.memset(v[:, :, :, :], 0.0).then_inc(zeros_ready, 1)
            pool.wait_ge(zeros_ready, 1)
            pool.memset(v[:, :, :, DH1:DH1 + 1], 1.0).then_inc(v_ones_ready, 1)
            pool.wait_ge(v_ones_ready, 1)
            pool.memset(ks[32:64, :, :].bitcast(F32), 1.0).then_inc(k_ones_ready, 1)
            pool.wait_ge(k_ones_ready, 1)
            pool.wait_ge(consts_in, 16 * len(CONSTS))
            rstd(2, 0)
            keep_x2(0)
            body(0, True, False)
            with pool.Fori(1, B - 1) as b:
                body(b, True, True)
            body(B - 1, False, True)
            rstd(3, B - 1)
            rstd(4, B - 1)

        @block.tensor
        def _(pe):

            def turn(src, done):
                for k in range(KD):
                    for t in range(NT):
                        mm = pe.transpose(side[:, k, t * P:(t + 1) * P], src[:, t, k * P:(k + 1) * P], ident[:, :])
                mm.then_inc(done, 1)

            def turn_x1(b, after):
                pe.wait_ge(x1_ready, NT * (b + 1))
                at_least(pe, *after)
                turn(xf, x1T_done)

            def select(b):
                pe.wait_ge(x1T_ready, b + 1)
                for t in range(NT):
                    for k in range(KD):
                        mm = pe.matmul(side4[:, t, 0:W0], x1T[:, k, t * P:(t + 1) * P], fw[:, k, :], start=k == 0, stop=k == KD - 1)
                mm.then_inc(pr_done, 1)

            def turn_hm(b):
                pe.wait_ge(hm_ready, b + 1)
                for t in range(NT):
                    mm = pe.transpose(side[0:U0, 0, t * P:(t + 1) * P], hm[:, t, :], ident[:, :])
                mm.then_inc(hmT_done, 1)

            def update(b):
                pe.wait_ge(hmT_ready, b + 1)
                for t in range(NT):
                    mm = pe.matmul(side4[:, t, :], hmT[:, t * P:(t + 1) * P], down0[:, :], start=True, stop=True)
                mm.then_inc(up_done, 1)

            def turn_x2(b, after):
                pe.wait_ge(x_ready[2], NT * (b + 1))
                at_least(pe, *after)
                turn(xf, x2T_done)

            def query_key(b):
                pe.wait_ge(x2T_hi_ready, b + 1)
                pe.wait_ge(x2T_lo_ready, b + 1)
                for i in range(4):
                    if i >= 2:
                        pe.wait_ge(qk_lo_ready, 4 * b + i - 1)
                    cols = slice(i * P, (i + 1) * P)
                    n = 0
                    for k in range(KD):
                        for lhs, rhs in split_passes(wqkv_hi[:, k, cols], wqkv_lo[:, k, cols], x2T_hi[:, k, :], x2T_lo[:, k, :]):
                            mm = pe.matmul(side[:, i % 2, :], lhs, rhs, start=n == 0, stop=n == 3 * KD - 1)
                            n += 1
                    mm.then_inc(qk_done, 1)

            def value(b, after):
                at_least(pe, *after)
                for i in range(2):
                    for t in (2 * i, 2 * i + 1):
                        tok = slice(t * P, (t + 1) * P)
                        n = 0
                        for k in range(KD):
                            for lhs, rhs in split_passes(x2T_hi[:, k, tok], x2T_lo[:, k, tok], wqkv_hi[:, k, 2 * D:], wqkv_lo[:, k, 2 * D:]):
                                mm = pe.matmul(side4[:, t, :], lhs, rhs, start=n == 0, stop=n == 3 * KD - 1)
                                n += 1
                    mm.then_inc(vp_done, 1)

            def scores(b, h):
                if h % 8 == 0:
                    pe.wait_ge(stack_in[h // 8], 96 * (b + 1))
                for t in range(NT):
                    u = 4 * h + t
                    at_least(pe, max_ready, 64 * b + u - 1)
                    pe.matmul(bank_s[u % 2][:, :], qs[0:ROWS_S, h, t * P:(t + 1) * P], ks[0:ROWS_S, h, :],
                              start=True, stop=True).then_inc(s_done, 1)

            def turn_max(b, g, after):
                pe.wait_ge(max_ready, 64 * b + 16 * (g + 1))
                at_least(pe, *after)
                for t in range(NT):
                    mm = pe.transpose(bank_t[0:4, t * P:(t + 1) * P], nmax[:, g, t, :], ident[:, :])
                mm.then_inc(maxT_done, 1)

            def turned_scores(b, s):
                g, kt = divmod(s, 4)
                if kt == 0:
                    pe.wait_ge(shift_in, 32 * (4 * b + g + 1))
                for j in range(4):
                    h, u = 4 * g + j, 4 * s + j
                    at_least(pe, p_ready, 64 * b + u - 1)
                    pe.matmul(bank_st[u % 2][:, :], ks[0:ROWS_ST, h, kt * P:(kt + 1) * P], qs[0:ROWS_ST, h, :],
                              start=True, stop=True).then_inc(st_done, 1)

            def context(b, s):
                g, kt = divmod(s, 4)
                if s == 0:
                    pe.wait_ge(v_ready, 2 * (b + 1))
                    pe.wait_ge(v_ones_ready, 1)
                if kt == 0:
                    at_least(pe, ct_ready, 4 * b + g)
                pe.wait_ge(p_ready, 64 * b + 4 * s + 4)
                for j in range(4):
                    mm = pe.matmul(bank_c[32 * j:32 * j + 32, :], v[:, kt, 4 * g + j, :], probs[:, (4 * s + j) % SLOTS, :],
                                   start=kt == 0, stop=kt == 3)
                mm.then_inc(pv_done, 1)

            def turn_context(b, g, after):
                pe.wait_ge(ct_ready, 4 * b + g + 1)
                at_least(pe, *after)
                for t in range(NT):
                    mm = pe.transpose(bank_t[:, t * P:(t + 1) * P], ctT[:, t * P:(t + 1) * P], ident[:, :])
                mm.then_inc(ctT_done, 1)

            def out_project(b, after):
                pe.wait_ge(cx_ready, 4 * (b + 1))
                at_least(pe, *after)
                for c in range(2):
                    for half_ in range(2):
                        for i in range(2):
                            mm = pe.matmul(side4[:, 2 * c + half_, :], cx[:, 2 * half_ + i, c * P:(c + 1) * P], wo[:, i, :],
                                           start=i == 0, stop=i == 1)
                mm.then_inc(wo_done, 1)

            def turn_x3(b, after):
                pe.wait_ge(x_ready[3], NT * (b + 1))
                at_least(pe, *after)
                turn(xk, x3T_done)

            def expert_in(b, t, after):
                if t == 0:
                    pe.wait_ge(x3T_hi_ready, b + 1)
                    pe.wait_ge(x3T_lo_ready, b + 1)
                at_least(pe, *after)
                tok = slice(t * P, (t + 1) * P)
                for i, cols in enumerate((slice(0, WA), slice(WA, WA + WB))):
                    n = 0
                    for k in range(KD):
                        for lhs, rhs in split_passes(x3T_hi[:, k, tok], x3T_lo[:, k, tok], win_hi[:, k, cols], win_lo[:, k, cols]):
                            mm = pe.matmul(side[:, i, 0:cols.stop - cols.start], lhs, rhs, start=n == 0, stop=n == 3 * KD - 1)
                            n += 1
                mm.then_inc(in_done, 1)

            def turn_hidden(b):
                pe.wait_ge(hw_ready, 2 * (b + 1))
                for first in (0, 2):
                    if first:
                        pe.wait_ge(hidT_ready, 2 * b + 1)
                    for c in range(first, min(first + 2, 3)):
                        for t in range(NT):
                            mm = pe.transpose(side[:, c % 2, t * P:(t + 1) * P], hid[:, t, c * P:(c + 1) * P], ident[:, :])
                    mm.then_inc(hidT_done, 1)

            def expert_out(b):
                pe.wait_ge(hidT_ready, 2 * (b + 1))
                for t in range(NT):
                    for c in range(3):
                        mm = pe.matmul(side4[:, t, :], hidT[:, c, t * P:(t + 1) * P], down1[:, c, :], start=c == 0, stop=c == 2)
                mm.then_inc(down_done, 1)

            def body(b, front, back):
                for s in range(SUBS):
                    turned_scores(b, s)
                    if s + LEAD < H1:
                        scores(b, s + LEAD)
                    elif front:
                        scores(b + 1, s + LEAD - H1)
                    if s == 0 and back:
                        out_project(b - 1, after=(v_ready, 2 * (b + 1)))
                    if s == 0 and front:
                        turn_x1(b + 1, after=(r3_ready, b) if back else (v_ready, 2 * (b + 1)))
                    if s == 1 and front:
                        select(b + 1)
                    if s == 3 and front:
                        turn_hm(b + 1)
                    if s == 4 and front:
                        update(b + 1)
                    if s == 5 and back:
                        turn_x3(b - 1, after=(r2_ready, NT * (b + 2)) if front else (r3_ready, b))
                    if s == 6 and front:
                        turn_x2(b + 1, after=(x3T_lo_ready, b) if back else (r2_ready, NT * (b + 2)))
                    if s == 7 and front:
                        query_key(b + 1)
                    if 8 <= s < 12 and back:
                        if s > 8:
                            after = (hid_ready, NT * (b - 1) + s - 8)
                        else:
                            after = (qk_lo_ready, 4 * (b + 2)) if front else (x3T_lo_ready, b)
                        expert_in(b - 1, s - 8, after)
                    if s == 13 and back:
                        turn_hidden(b - 1)
                    if s == 14 and back:
                        expert_out(b - 1)
                    if s == 15 and front:
                        value(b + 1, after=(r4_ready, b) if back else (qk_lo_ready, 4 * (b + 2)))
                    if s == 1:
                        turn_max(b, 1, after=(cx_ready, 4 * b))
                    if s == 5:
                        turn_max(b, 2, after=(sh_lo_ready, 4 * b + 2))
                        turn_context(b, 0, after=(sh_lo_ready, 4 * b + 3))
                    if s == 9:
                        turn_max(b, 3, after=(cx_ready, 4 * b + 1))
                        turn_context(b, 1, after=(sh_lo_ready, 4 * b + 4))
                    if s == 13:
                        if front:
                            turn_max(b + 1, 0, after=(cx_ready, 4 * b + 2))
                        turn_context(b, 2, after=(sh_lo_ready, 4 * b + 5) if front else (cx_ready, 4 * b + 2))
                    context(b, s)
                turn_context(b, 3, after=(cx_ready, 4 * b + 3))

            pe.wait_ge(consts_in, 16 * len(CONSTS))
            pe.wait_ge(fprod_ready, 3)
            for k in range(KD):
                mm = pe.matmul(bank_t[:, 0:W0], ones[:, :], fprod[:, k, :], start=k == 0, stop=k == KD - 1)
            mm.then_inc(fsum_done, 1)
            turn_x1(0, after=(r3_ready, 0))
            select(0)
            turn_hm(0)
            update(0)
            turn_x2(0, after=(r2_ready, NT))
            pe.wait_ge(w_hi_ready, 2)
            pe.wait_ge(w_lo_ready, 2)
            query_key(0)
            value(0, after=(qk_lo_ready, 4))
            for h in range(LEAD):
                scores(0, h)
                if h == 3:
                    turn_max(0, 0, after=(fconst_ready, 1))
            body(0, True, False)
            with pe.Fori(1, B - 1) as b:
                body(b, True, True)
            body(B - 1, False, True)
            out_project(B - 1, after=(r4_ready, B - 1))
            turn_x3(B - 1, after=(r3_ready, B))
            for t in range(NT):
                expert_in(B - 1, t, after=(hid_ready, NT * (B - 1) + t) if t else (x3T_lo_ready, B))
            turn_hidden(B - 1)
            expert_out(B - 1)

        @block.scalar
        def _(act):
            def x1T_out(b):
                act.wait_ge(x1T_done, b + 1)
                act.activation(x1T, side[:, :, :], ACT.Copy).then_inc(x1T_ready, 1)

            def squares(b):
                act.wait_ge(x1_ready, NT * (b + 1))
                at_least(act, hm_ready, b)
                for t in range(NT):
                    act.activation(junk[:, t, :], xf[:, t, :], ACT.Square, accum_out=ssq[:, t:t + 1]).then_inc(ssq_ready, 1)

            def gate_exp(b):
                act.wait_ge(zc_ready, b + 1)
                act.activation(gt["e"][:, :, :], gt["zc"][:, :, :], ACT.Exp, scale=-1.0).then_inc(ge_ready, 1)

            def hmT_out(b):
                act.wait_ge(hmT_done, b + 1)
                act.activation(hmT[:, :], side[0:U0, 0, :], ACT.Copy).then_inc(hmT_ready, 1)

            def x2T_out(b):
                act.wait_ge(x2T_done, b + 1)
                act.activation(x2T_hi[:, :, :], side[:, :, :], ACT.Copy).then_inc(x2T_hi_ready, 1)

            def qk_out(b):
                for i in range(4):
                    act.wait_ge(qk_done, 4 * b + i + 1)
                    at_least(act, scratch_out[i % 2], 64 * b + 32 * (i // 2))
                    act.activation(qk_hi[:, i % 2, :], side[:, i % 2, :], ACT.Copy).then_inc(qk_hi_ready, 1)

            def exponentials(b, s):
                at_least(act, pv_done, SUBS * b + s - 1)
                for j in range(4):
                    u = 4 * s + j
                    act.wait_ge(st_done, 64 * b + u + 1)
                    act.activation(probs[:, u % SLOTS, :], bank_st[u % 2][:, :], ACT.Exp, scale=SCALE1).then_inc(p_ready, 1)

            def shift_hi(b, g):
                act.wait_ge(maxT_done, 4 * b + g + 1)
                at_least(act, shift_in, 32 * (4 * b + g))
                act.activation(sh_hi[:, :], bank_t[0:4, :], ACT.Copy).then_inc(sh_hi_ready, 1)

            def context_out(b, g):
                act.wait_ge(pv_done, SUBS * b + 4 * g + 4)
                at_least(act, ctT_done, 4 * b + g)
                act.activation(ctT[:, :], bank_c[:, :], ACT.Copy).then_inc(ct_ready, 1)

            def x3T_out(b):
                act.wait_ge(x3T_done, b + 1)
                act.activation(x3T_hi[:, :, :], side[:, :, :], ACT.Copy).then_inc(x3T_hi_ready, 1)

            def expert_in(b, t):
                act.wait_ge(in_done, NT * b + t + 1)
                if t == 0:
                    at_least(act, hidT_done, 2 * b)
                at_least(act, sg_ready, NT * b + max(0, t - 1))
                act.activation(th[:, t % 2, :], side[:, 0, 0:E1 * F1], ACT.Tanh, scale=0.5)
                act.activation(hid[:, t, E1 * F1:3 * P], side[:, 0, E1 * F1:WA], ACT.Copy)
                act.activation(lg[:, t, :], side[:, 1, E1 * F1:WB], ACT.Copy).then_inc(in_copied, 1)

            def route_exp(b):
                act.wait_ge(rel_ready, b + 1)
                act.activation(rt["e"][:, :, :], rt["rel"][:, :, :], ACT.Exp).then_inc(re_ready, 1)

            def hidden_out(b):
                act.wait_ge(hidT_done, 2 * b + 1)
                act.activation(hidT[:, 0:2, :], side[:, :, :], ACT.Copy).then_inc(hidT_ready, 1)
                act.wait_ge(hidT_done, 2 * b + 2)
                act.activation(hidT[:, 2, :], side[:, 0, :], ACT.Copy).then_inc(hidT_ready, 1)

            def body(b, front, back):
                for s in range(SUBS):
                    exponentials(b, s)
                    if s % 4 == 0 and s:
                        context_out(b, s // 4 - 1)
                    if s == 0 and front:
                        x1T_out(b + 1)
                        squares(b + 1)
                    if s == 2 and front:
                        gate_exp(b + 1)
                    if s == 3 and front:
                        hmT_out(b + 1)
                    if s == 5 and back:
                        x3T_out(b - 1)
                    if s == 6 and front:
                        x2T_out(b + 1)
                    if s == 7 and front:
                        qk_out(b + 1)
                    if 8 <= s < 12 and back:
                        expert_in(b - 1, s - 8)
                    if s == 12 and back:
                        route_exp(b - 1)
                    if s == 13 and back:
                        hidden_out(b - 1)
                    if s in (1, 5, 9):
                        shift_hi(b, (s + 3) // 4)
                    if s == 13 and front:
                        shift_hi(b + 1, 0)
                context_out(b, 3)

            x1T_out(0)
            squares(0)
            for i, n0, n1, hi in ((0, 0, KD * 3 * D, wqkv_hi), (1, KD * 3 * D, KD * (3 * D + WA + WB), win_hi)):
                act.wait_ge(raw_in[i], 16)
                act.activation(hi[:, :, :].rearrange("p k n -> p (k n)"), raw[:, n0:n1], ACT.Copy).then_inc(w_hi_ready, 1)
            gate_exp(0)
            hmT_out(0)
            x2T_out(0)
            qk_out(0)
            shift_hi(0, 0)
            act.wait_ge(w_lo_ready, 2)
            body(0, True, False)
            with act.Fori(1, B - 1) as b:
                body(b, True, True)
            body(B - 1, False, True)
            x3T_out(B - 1)
            for t in range(NT):
                expert_in(B - 1, t)
            route_exp(B - 1)
            hidden_out(B - 1)

        @block.vector
        def _(dve):
            def normalize_x1(b):
                if not isinstance(b, int) or b > 0:
                    dve.wait_ge(x2_kept, b)
                for t in range(NT):
                    dve.tensor_scalar(xf[:, t, :], tile(xs, b, t), tile(stats, b, t)[:, 0:1],
                                      rstd1[:, NT * b + t:NT * b + t + 1] if isinstance(b, int) else rstd1[:, bass.ds(NT * b + t, 1)],
                                      ALU.subtract, ALU.mult).then_inc(x1_ready, 1)

            def first_max(step, values, key, eq, mask, top, ktop):
                step(dve.tensor_reduce(top[:, :], values, AX.X, ALU.max))
                step(dve.tensor_tensor(eq[:, :, :], values, over_last(top[:, :], E0), ALU.is_equal))
                step(dve.tensor_tensor(key[:, :, :], eq[:, :, :], over_tiles(rank[:, :]), ALU.mult))
                step(dve.tensor_reduce(ktop[:, :], key[:, :, :], AX.X, ALU.max))
                step(dve.tensor_tensor(mask[:, :, :], key[:, :, :], over_last(ktop[:, :], E0), ALU.is_equal))

            GATE_STEPS = (6, 9)

            def gate_scores(b):
                step = Steps(dve, gate_step, sum(GATE_STEPS), b)
                dve.wait_ge(pr_done, b + 1)
                dve.tensor_tensor(pr[:, :, :], side4[:, :, 0:W0], over_tiles(fconst[:, :]), ALU.subtract).then_inc(pr_ready, 1)
                dve.wait_ge(pr_ready, b + 1)
                step(dve.tensor_tensor(pr2[:, :, :], pr[:, :, 0:E0 * S0], pr[:, :, 0:E0 * S0], ALU.mult))
                dve.tensor_reduce(gt["score"][:, :, :], pr2[:, :, :].rearrange("p t (n s) -> p t n s", s=S0), AX.X, ALU.add)
                dve.wait_ge(ssq_ready, NT * (b + 1))
                step(dve.scalar_tensor_tensor(out=gt["dist"][:, :, :], in0=pr[:, :, W0 - E0:W0], scalar=-2.0,
                                              in1=over_last(ssq[:, :], E0), op0=ALU.mult, op1=ALU.add))
                step(dve.reciprocal(gt["rdist"][:, :, :], gt["dist"][:, :, :]))
                step(dve.tensor_tensor(gt["rel"][:, :, :], gt["score"][:, :, :], gt["rdist"][:, :, :], ALU.mult))
                step(dve.tensor_tensor(gt["cent"][:, :, :], gt["rel"][:, :, :], over_tiles(center[:, :]), ALU.subtract))
                step(dve.tensor_tensor(gt["z"][:, :, :], gt["cent"][:, :, :], over_tiles(slope[:, :]), ALU.mult))
                dve.tensor_scalar(gt["zc"][:, :, :], gt["z"][:, :, :], Z_MIN, None, ALU.max).then_inc(zc_ready, 1)

            def gate_pick(b):
                step = Steps(dve, gate_step, sum(GATE_STEPS), b)
                step.n = GATE_STEPS[0]
                dve.wait_ge(ge_ready, b + 1)
                step(dve.tensor_scalar(gt["e1"][:, :, :], gt["e"][:, :, :], 1.0, None, ALU.add))
                step(dve.reciprocal(gt["gate"][:, :, :], gt["e1"][:, :, :]))
                first_max(step, gt["gate"][:, :, :], gt["key"], gt["eq"], gt["pick"], gmax, kmax)
                step(dve.tensor_scalar(keep[:, :], gmax[:, :], -1.0, 2.0, ALU.mult, ALU.add))
                step(dve.tensor_tensor(gt["w"][:, :, :], gt["pick"][:, :, :], over_last(gmax[:, :], E0), ALU.mult))
                w = gt["w"][:, :, :]
                for t in range(NT):
                    dve.tensor_tensor(hm[:, t, 0:E0 * R0].rearrange("p (n r) -> p n r", r=R0),
                                      pr[:, t, E0 * S0:E0 * (S0 + R0)].rearrange("p (n r) -> p n r", r=R0),
                                      over_last(gt["w"][:, t, :], R0), ALU.mult)
                dve.tensor_copy(hm[:, :, E0 * R0:U0], w).then_inc(hm_ready, 1)

            def stats_of(i, b, x, ready):
                for t in range(NT):
                    dve.wait_ge(ready[0], ready[1] + t if ready[2] else ready[1])
                    dve.bn_stats(ln[i]["bn"][:, t, :], x[:, t, :]).then_inc(bn_ready[i], 1)
                dve.wait_ge(bn_ready[i], NT * (b + 1))
                at_least(dve, rstd_ready[i], b)
                merge_stats(dve, Steps(dve, merge_step[i], MERGE_STEPS, b), ln[i]["bn"], ln[i]["tmp"],
                            by_tile(ln[i]["mean"]), by_tile(ln[i]["var"])).then_inc(var_ready[i], 1)

            def normalize(i, b, x):
                dve.wait_ge(rstd_ready[i], b + 1)
                for t in range(NT):
                    dve.tensor_scalar(x[:, t, :], x[:, t, :], ln[i]["mean"][:, t:t + 1], ln[i]["rstd"][:, t:t + 1],
                                      ALU.subtract, ALU.mult).then_inc(x_ready[i], 1)

            def add_update(b):
                dve.wait_ge(up_done, b + 1)
                for t in range(NT):
                    dve.scalar_tensor_tensor(out=xf[:, t, :], in0=xf[:, t, :], scalar=keep[:, t:t + 1], in1=side4[:, t, :],
                                             op0=ALU.mult, op1=ALU.add).then_inc(r2_ready, 1)
                stats_of(2, b, xf, (r2_ready, NT * b + 1, True))

            def x2T_rest(b):
                dve.wait_ge(x2T_hi_ready, b + 1)
                dve.tensor_tensor(x2T_lo[:, :, :], side[:, :, :], x2T_hi[:, :, :].bitcast(F32), ALU.subtract).then_inc(x2T_lo_ready, 1)

            def qk_rest(b):
                for i in range(4):
                    dve.wait_ge(qk_hi_ready, 4 * b + i + 1)
                    dve.tensor_tensor(qk_lo[:, i % 2, :], side[:, i % 2, :], qk_hi[:, i % 2, :].bitcast(F32), ALU.subtract).then_inc(qk_lo_ready, 1)

            def value_out(b):
                if isinstance(b, int) and b == 0:
                    dve.wait_ge(v_ones_ready, 1)
                at_least(dve, pv_done, SUBS * b)
                for i in range(2):
                    dve.wait_ge(vp_done, 2 * b + i + 1)
                    for t in (2 * i, 2 * i + 1):
                        cp = dve.tensor_copy(v[:, t, :, 0:DH1], side4[:, t, :].rearrange("p (h d) -> p h d", d=DH1))
                    cp.then_inc(v_ready, 1)

            def maxima(b, h):
                g, j = divmod(h, 4)
                if j == 0:
                    at_least(dve, maxT_done, 4 * (b - 1) + g + 1)
                for t in range(NT):
                    u = 4 * h + t
                    dve.wait_ge(s_done, 64 * b + u + 1)
                    dve.tensor_reduce(nmax[:, g, t, j:j + 1], bank_s[u % 2][:, :], AX.X, ALU.max, negate=True).then_inc(max_ready, 1)

            def shift_lo(b, g):
                dve.wait_ge(sh_hi_ready, 4 * b + g + 1)
                dve.tensor_tensor(sh_lo[:, :], bank_t[0:4, :], sh_hi[:, :].bitcast(F32), ALU.subtract).then_inc(sh_lo_ready, 1)

            def context_out(b, g):
                dve.wait_ge(ctT_done, 4 * b + g + 1)
                if g == 0:
                    at_least(dve, wo_done, b)
                tj = bank_t[:, :].rearrange("p (t j c) -> p t j c", t=NT, j=4)
                dve.reciprocal(rsum[:, :, :].rearrange("p t (j o) -> p t j o", o=1), tj[:, :, :, DH1:DH1 + 1]).then_inc(rsum_ready, 1)
                dve.wait_ge(rsum_ready, 4 * b + g + 1)
                for t in range(NT):
                    cp = dve.tensor_tensor(cx[:, t, 4 * g * DH1:4 * (g + 1) * DH1].rearrange("p (j d) -> p j d", d=DH1),
                                           tj[:, t, :, 0:DH1], over_last(rsum[:, t, :], DH1), ALU.mult)
                cp.then_inc(cx_ready, 1)

            def add_attention(b):
                dve.wait_ge(wo_done, b + 1)
                dve.wait_ge(x2_kept, b + 1)
                at_least(dve, stored, 16 * b)
                dve.tensor_tensor(xk[:, :, :], side4, tiles(xs, b), ALU.add).then_inc(r3_ready, 1)
                stats_of(3, b, xk, (r3_ready, b + 1, False))

            def x3T_rest(b):
                dve.wait_ge(x3T_hi_ready, b + 1)
                dve.tensor_tensor(x3T_lo[:, :, :], side[:, :, :], x3T_hi[:, :, :].bitcast(F32), ALU.subtract).then_inc(x3T_lo_ready, 1)

            def hidden(b, t):
                dve.wait_ge(in_copied, NT * b + t + 1)
                dve.scalar_tensor_tensor(out=sg[:, :], in0=th[:, t % 2, :], scalar=1.0, in1=side[:, 0, 0:E1 * F1],
                                         op0=ALU.add, op1=ALU.mult).then_inc(sg_ready, 1)
                dve.wait_ge(sg_ready, NT * b + t + 1)
                dve.tensor_tensor(hid[:, t, 0:E1 * F1], side[:, 1, 0:E1 * F1], sg[:, :], ALU.mult).then_inc(hid_ready, 1)

            ROUTE_STEPS = (1, 17)

            def route_rel(b):
                step = Steps(dve, route_step, sum(ROUTE_STEPS), b)
                dve.wait_ge(in_copied, NT * (b + 1))
                step(dve.tensor_reduce(rm["max"][:, :], lg[:, :, :], AX.X, ALU.max))
                dve.tensor_tensor(rt["rel"][:, :, :], lg[:, :, :], over_last(rm["max"][:, :], E1), ALU.subtract).then_inc(rel_ready, 1)

            def route(b):
                step = Steps(dve, route_step, sum(ROUTE_STEPS), b)
                step.n = ROUTE_STEPS[0]
                dve.wait_ge(re_ready, b + 1)
                step(dve.tensor_reduce(rm["sum"][:, :], rt["e"][:, :, :], AX.X, ALU.add))
                step(dve.reciprocal(rm["rsum"][:, :], rm["sum"][:, :]))
                step(dve.tensor_tensor(rt["sc"][:, :, :], rt["e"][:, :, :], over_last(rm["rsum"][:, :], E1), ALU.mult))
                first_max(step, rt["sc"][:, :, :], rt["key1"], rt["eq1"], rt["pick1"], rm["max1"], rm["kmax1"])
                step(dve.scalar_tensor_tensor(out=rt["less"][:, :, :], in0=rt["pick1"][:, :, :], scalar=-2.0, in1=rt["sc"][:, :, :],
                                              op0=ALU.mult, op1=ALU.add))
                first_max(step, rt["less"][:, :, :], rt["key2"], rt["eq2"], rt["pick2"], rm["max2"], rm["kmax2"])
                step(dve.tensor_tensor(rt["both"][:, :, :], rt["pick1"][:, :, :], rt["pick2"][:, :, :], ALU.add))
                step(dve.tensor_tensor(rt["w"][:, :, :], rt["both"][:, :, :], rt["sc"][:, :, :], ALU.mult))
                step(dve.tensor_scalar(rt["wh"][:, :, :], rt["w"][:, :, :], 0.5, None, ALU.mult))
                dve.wait_ge(hid_ready, NT * (b + 1))
                for n0, n, w in ((0, F1, "wh"), (E1 * F1, R1, "w")):
                    for t in range(NT):
                        part = hid[:, t, n0:n0 + E1 * n].rearrange("p (e f) -> p e f", f=n)
                        mul = dve.tensor_tensor(part, part, over_last(rt[w][:, t, :], n), ALU.mult)
                    mul.then_inc(hw_ready, 1)

            def add_experts(b):
                dve.wait_ge(down_done, b + 1)
                dve.tensor_tensor(xk[:, :, :], side4, xk[:, :, :], ALU.add).then_inc(r4_ready, 1)
                stats_of(4, b, xk, (r4_ready, b + 1, False))

            def body(b, front, back):
                if front:
                    normalize_x1(b + 1)
                for s in range(SUBS):
                    if s + LEAD < H1:
                        maxima(b, s + LEAD)
                    elif front:
                        maxima(b + 1, s + LEAD - H1)
                    if s == 0 and back:
                        add_attention(b - 1)
                    if s == 1 and back:
                        normalize(3, b - 1, xk)
                    if s == 1 and front:
                        gate_scores(b + 1)
                    if s == 2 and front:
                        gate_pick(b + 1)
                    if s == 4 and front:
                        add_update(b + 1)
                    if s == 5 and front:
                        normalize(2, b + 1, xf)
                    if s == 5 and back:
                        x3T_rest(b - 1)
                    if s == 6 and front:
                        x2T_rest(b + 1)
                    if s == 7 and front:
                        qk_rest(b + 1)
                    if 8 <= s < 12 and back:
                        hidden(b - 1, s - 8)
                    if s == 11 and back:
                        route_rel(b - 1)
                    if s == 12 and back:
                        route(b - 1)
                    if s == 14 and back:
                        add_experts(b - 1)
                    if s == 15 and back:
                        normalize(4, b - 1, xk)
                    if s == 15 and front:
                        value_out(b + 1)
                    if s in (1, 5, 9):
                        shift_lo(b, (s + 3) // 4)
                    if s == 13 and front:
                        shift_lo(b + 1, 0)
                    if s in (5, 9, 13):
                        context_out(b, s // 4 - 1)
                context_out(b, 3)

            dve.wait_ge(consts_in, 16 * len(CONSTS))
            for k in range(KD):
                sel = fw[:, k, 0:E0 * (S0 + R0)].rearrange("p (m n s) -> p m n s", m=2, s=S0)
                dst = fprod[:, k, 0:E0 * (S0 + R0)].rearrange("p (m n s) -> p m n s", m=2, s=S0)
                for m in range(2):
                    pd = dve.tensor_tensor(dst[:, m], sel[:, m], over_last(md[:, k, m * E0:(m + 1) * E0], S0), ALU.mult)
                pd.then_inc(fprod_ready, 1)
            dve.scalar_tensor_tensor(out=fprod[:, :, W0 - E0:W0], in0=md[:, :, 0:E0], scalar=0.5, in1=md[:, :, 0:E0],
                                     op0=ALU.mult, op1=ALU.mult).then_inc(fprod_ready, 1)
            dve.wait_ge(rstd1_ready, 1)
            normalize_x1(0)
            dve.wait_ge(fsum_done, 1)
            dve.tensor_copy(fconst[:, :], bank_t[:, 0:W0]).then_inc(fconst_ready, 1)
            dve.wait_ge(fconst_ready, 1)
            gate_scores(0)
            gate_pick(0)
            for i, n0, n1, hi, lo in ((0, 0, KD * 3 * D, wqkv_hi, wqkv_lo), (1, KD * 3 * D, KD * (3 * D + WA + WB), win_hi, win_lo)):
                dve.wait_ge(w_hi_ready, i + 1)
                dve.tensor_tensor(lo[:, :, :].rearrange("p k n -> p (k n)"), raw[:, n0:n1],
                                  hi[:, :, :].rearrange("p k n -> p (k n)").bitcast(F32), ALU.subtract).then_inc(w_lo_ready, 1)
            add_update(0)
            normalize(2, 0, xf)
            x2T_rest(0)
            qk_rest(0)
            value_out(0)
            for h in range(LEAD):
                maxima(0, h)
                if h == 3:
                    shift_lo(0, 0)
            body(0, True, False)
            with dve.Fori(1, B - 1) as b:
                body(b, True, True)
            body(B - 1, False, True)
            add_attention(B - 1)
            normalize(3, B - 1, xk)
            x3T_rest(B - 1)
            for t in range(NT):
                hidden(B - 1, t)
            route_rel(B - 1)
            route(B - 1)
            add_experts(B - 1)
            normalize(4, B - 1, xk)


def program(nc, a, out):
    with ExitStack() as ctx:
        xs = ctx.enter_context(nc.sbuf_tensor("xs", [P, B * NT, D], F32))
        stats = ctx.enter_context(nc.sbuf_tensor("stats", [P, B * NT, 2], F32))
        layer0_attention(nc, a, xs, stats)
        update_attention_experts(nc, a, xs, stats, out)


def constants():
    import numpy as np

    pick = np.zeros((P, H0), np.float32)
    part_c, part_m = np.zeros((P, 1), np.float32), np.zeros((P, 1), np.float32)
    for g in range(G0):
        for j in range(J0):
            pick[32 * g + j, J0 * g + j] = pick[32 * g + 4 + j, J0 * g + j] = 1.0
            part_c[32 * g + j], part_c[32 * g + 4 + j], part_m[32 * g + 4 + j] = 1.0, -1.0, 1.0
    return {"pick": pick, "part_c": part_c, "part_m": part_m, "ones": np.ones((P, 1), np.float32),
            "ident": np.eye(P, dtype=np.float32), "ones_pp": np.ones((P, P), np.float32),
            "rank": np.broadcast_to(np.arange(E0, 0, -1).astype(np.float32), (P, E0))}


def laid_out(i):
    import numpy as np

    def cut(w):
        return w.reshape(KD, P, -1).transpose(1, 0, 2)

    i = {k: np.asarray(v) for k, v in i.items()}
    x = i["L0_attn_hidden_states"]
    arrays = {
        "x": x,
        "xT": x.reshape(B, 2, P, 2, KD, P).transpose(5, 0, 4, 1, 3, 2).reshape(P, B, KD, T),
        "wqT0": cut(i["L0_attn_Wq"].T),
        "wkvT0": cut(np.concatenate([i["L0_attn_Wk"], i["L0_attn_Wv"]]).T).reshape(P, -1),
        "woT0": i["L0_attn_Wo"].reshape(D, H0, DH0).transpose(2, 1, 0),
        "bq": i["L0_attn_bq"].reshape(H0, DH0).T,
        "bk": np.broadcast_to(i["L0_attn_bk"], (P, 512)),
        "bv": np.broadcast_to(i["L0_attn_bv"], (P, 512)),
        "fw": cut(np.concatenate([i["L0_ffn_select_weight"].transpose(1, 0, 2).reshape(D, -1),
                                  i["L0_ffn_lora_update"].transpose(1, 0, 2).reshape(D, -1),
                                  i["L0_ffn_select_mean_diff"].T], axis=1)),
        "md": cut(np.concatenate([i["L0_ffn_select_mean_diff"].T, i["L0_ffn_debias_w"].T], axis=1)),
        "slope": np.broadcast_to(i["L0_ffn_imp_slope"], (P, E0)),
        "center": np.broadcast_to(i["L0_ffn_imp_center"], (P, E0)),
        "down0": np.concatenate([i["L0_ffn_lora_degen"].transpose(0, 2, 1).reshape(E0 * R0, D), i["L0_ffn_bias_w"]]),
        "wqkv1": cut(np.concatenate([i["L1_attn_Wq"], i["L1_attn_Wk"], i["L1_attn_Wv"]], axis=1)).reshape(P, -1),
        "wo1": i["L1_attn_Wo"].reshape(P, 2, D),
        "bo": np.broadcast_to(i["L1_attn_bo"], (P, D)),
        "win1": cut(np.concatenate([i["L1_ffn_gate_w"].reshape(-1, D), i["L1_ffn_lora_A"].reshape(-1, D),
                                    i["L1_ffn_up_w"].reshape(-1, D), i["L1_ffn_G"].T]).T).reshape(P, -1),
        "down1": np.concatenate([i["L1_ffn_down_w"].transpose(0, 2, 1).reshape(E1 * F1, D),
                                 i["L1_ffn_lora_B"].transpose(0, 2, 1).reshape(E1 * R1, D)]).reshape(3, P, D).transpose(1, 0, 2),
    }
    arrays.update(constants())
    return {k: np.ascontiguousarray(v) for k, v in arrays.items()}


def kernel(**inputs):
    import numpy as np
    import concourse.bacc as bacc
    from concourse.bass_utils import run_bass_kernel_spmd

    nc = bacc.Bacc("TRN2", target_bir_lowering=False, num_devices=1)
    arrays = laid_out(inputs)
    aps = {k: nc.dram_tensor(f"in_{k}", v.shape, F32, kind="ExternalInput").ap() for k, v in arrays.items()}
    out = nc.dram_tensor("out", (B, T, D), F32, kind="ExternalOutput").ap()
    program(nc, aps, out)
    r = run_bass_kernel_spmd(nc, [{f"in_{k}": v for k, v in arrays.items()}], core_ids=[0])
    return r.results[0]["out"]
```

```python
from contextlib import ExitStack

import concourse.bass as bass
from concourse import mybir

F32 = mybir.dt.float32
F32R = mybir.dt.float32r
ALU = mybir.AluOpType
ACT = mybir.ActivationFunctionType
AX = mybir.AxisListType

P = 128
B, T, D = 4, 512, 256
KD = D // P
NT = T // P
LN_EPS = 1e-5

H0, G0, DH0 = 16, 4, 128
J0 = H0 // G0
DEN_EPS = 1e-6
ORDER0 = [(g, j) for j in range(J0) for g in range(G0)]


def split_passes(lhs_hi, lhs_lo, rhs_hi, rhs_lo):
    return [(lhs_lo, rhs_hi), (lhs_hi, rhs_lo), (lhs_hi, rhs_hi)]


def rows(x):
    return x.rearrange("b (c p h) d -> p (b c) (h d)", p=P, h=2)


def tiles(x, b):
    return x[:, NT * b:NT * (b + 1), :] if isinstance(b, int) else x[:, bass.ds(NT * b, NT), :]


class Steps:

    def __init__(self, eng, sem, each, b):
        self.eng, self.sem, self.base, self.n = eng, sem, each * b, 0

    def __call__(self, *instructions):
        for ins in instructions:
            self.n += 1
            ins.then_inc(self.sem, 1)
        self.eng.wait_ge(self.sem, self.base + self.n)


MERGE_STEPS = 4


def merge_stats(dve, step, bn, tmp, mean, var):
    half_n = D // 2
    mean_e, m2_e, mean_o, m2_o = (bn[:, :, i:i + 1] for i in (1, 2, 4, 5))
    dist, m2, dist2 = (tmp[:, :, i:i + 1] for i in range(3))
    step(dve.tensor_tensor(dist, mean_e, mean_o, ALU.subtract),
         dve.scalar_tensor_tensor(out=m2, in0=m2_e, scalar=2 * half_n * LN_EPS, in1=m2_o, op0=ALU.add, op1=ALU.add))
    step(dve.scalar_tensor_tensor(out=mean, in0=dist, scalar=-0.5, in1=mean_e, op0=ALU.mult, op1=ALU.add),
         dve.scalar_tensor_tensor(out=dist2, in0=dist, scalar=0.25, in1=dist, op0=ALU.mult, op1=ALU.mult))
    return dve.scalar_tensor_tensor(out=var, in0=m2, scalar=1 / (2 * half_n), in1=dist2, op0=ALU.mult, op1=ALU.add)


def layer0_attention(nc, a, xs, stats):
    with ExitStack() as ctx:
        def sb(name, shape, dt=F32):
            return ctx.enter_context(nc.sbuf_tensor(name, [P] + shape, dt))

        def ps(name):
            return ctx.enter_context(nc.psum_tensor(name, [P, 512], F32))

        def sem(name):
            return ctx.enter_context(nc.semaphore(name))

        wkv_hi, wkv_lo = sb("wkv_hi", [KD, 1024], F32R), sb("wkv_lo", [KD, 1024], F32R)
        wq_hi, wq_lo = sb("wq_hi", [KD, H0 * DH0], F32R), sb("wq_lo", [KD, H0 * DH0], F32R)
        wo = sb("wo0", [H0, D])
        bq, bq1, bq_neg = sb("bq", [H0]), sb("bq1", [H0]), sb("bq_neg", [H0])
        bk, bv = sb("bk", [512]), sb("bv", [512])
        ones = sb("ones0", [1])
        part_c, part_m = sb("part_c", [1]), sb("part_m", [1])
        pick_raw, pick = sb("pick_raw", [H0]), sb("pick", [H0], F32R)
        xT = sb("xT", [KD, T])
        xT_hi, xT_lo = sb("xT_hi", [KD, T], F32R), sb("xT_lo", [KD, T], F32R)
        zk, ek = sb("zk", [2, 512]), sb("ek", [2, 512])
        sk, v = sb("sk", [NT, 512]), sb("v0", [NT, 512])
        kvT = sb("kvT", [512])
        ksel = sb("ksel", [G0, J0, 32])
        eq = sb("eq", [3, T])
        sq = sb("sq", [H0, T])
        stage = sq[:, 0:8, :].rearrange("p (s c) n -> p s (c n)", s=2)
        den, rn = sb("den", [T]), sb("rn", [T])
        rn_c, rn_parts = sb("rn_c", [T], F32R), sb("rn_parts", [T], F32R)
        m_hi, m_lo = sb("m_hi", [4, 2 * D], F32R), sb("m_lo", [4, 2 * D], F32R)
        s_hi, s_lo = sb("s_hi", [2, T], F32R), sb("s_lo", [2, T], F32R)
        res = sb("res", [NT, D])
        bn, bn_tmp = sb("bn0", [NT, 6]), sb("bn0_tmp", [NT, 3])

        bank_a = [ps("bank_a0"), ps("bank_a1")]
        bank_q = [ps(f"bank_q{i}") for i in range(3)]
        bank_n = ps("bank_n")
        bank_y = ctx.enter_context(nc.psum_tensor("bank_y", [P, 2, 512], F32))
        bank_y4 = bank_y[:, :, :].rearrange("p a (t n) -> p (a t) n", t=2)

        small_in = sem("small_in")
        wo_in, x_in, xT_in = sem("wo_in"), sem("x_in"), sem("xT_in")
        stage_in = [sem("stage_in0"), sem("stage_in1")]
        w_hi_ready, w_lo_ready = sem("w_hi_ready"), sem("w_lo_ready")
        setup_done = sem("setup_done")
        xT_hi_ready, xT_lo_ready = sem("xT_hi_ready"), sem("xT_lo_ready")
        k_done, v_done = sem("k_done"), sem("v_done")
        zk_ready, v_ready, ek_ready = sem("zk_ready"), sem("v_ready"), sem("ek_ready")
        ek_capped, sk_ready = sem("ek_capped"), sem("sk_ready")
        kvT_done, ksum_done, kvT_ready, ksel_ready = sem("kvT_done"), sem("ksum_done"), sem("kvT_ready"), sem("ksel_ready")
        q_done, eq_ready, eq_capped, sq_ready = sem("q_done"), sem("eq_ready"), sem("eq_capped"), sem("sq_ready")
        norm_done, den_ready, rn_ready, rn_c_ready, parts_ready = (
            sem("norm_done"), sem("den_ready"), sem("rn_ready"), sem("rn_c_ready"), sem("parts_ready"))
        m_done, m_hi_ready, m_lo_ready = sem("m_done"), sem("m_hi_ready"), sem("m_lo_ready")
        bc_done, scaled, s_hi_ready, s_lo_ready = sem("bc_done"), sem("scaled"), sem("s_hi_ready"), sem("s_lo_ready")
        y_done, res_ready, res_kept = sem("y_done"), sem("res_ready"), sem("res_kept")
        bn_ready, merge_step, stats_ready = sem("bn_ready"), sem("merge_step"), sem("stats_ready")

        W_STAGES = [("kv", None), ("q", 0), ("q", 1)]
        N_SMALL = 7

        def w_parts(s):
            kind, k = W_STAGES[s]
            if kind == "kv":
                return wkv_hi[:, :, :].rearrange("p k n -> p (k n)"), wkv_lo[:, :, :].rearrange("p k n -> p (k n)")
            return wq_hi[:, k, :], wq_lo[:, k, :]

        block = ctx.enter_context(nc.Block())

        @block.sync
        def _(sp):
            sp.dma_start(stage[:, 0, :], a["wkvT0"]).then_inc(stage_in[0], 16)
            sp.dma_start(xT[:, :, :], a["xT"][:, 0]).then_inc(xT_in, 16)
            sp.dma_start(stage[:, 1, :], a["wqT0"][:, 0]).then_inc(stage_in[1], 16)
            for dst, name in ((bk, "bk"), (bv, "bv"), (bq, "bq"), (pick_raw, "pick"), (part_c, "part_c"),
                              (part_m, "part_m"), (ones, "ones")):
                sp.dma_start(dst[:, :], a[name]).then_inc(small_in, 16)
            sp.dma_start(wo[:, :, :], a["woT0"]).then_inc(wo_in, 16)
            sp.wait_ge(w_lo_ready, 1)
            sp.dma_start(stage[:, 0, :], a["wqT0"][:, 1]).then_inc(stage_in[0], 16)
            sp.dma_start(xs[:, :, :].rearrange("p (c h) d -> p c (h d)", h=2), rows(a["x"])).then_inc(x_in, 16)
            with sp.Fori(0, B - 1) as b:
                after = sp.snap(b + 1)
                sp.wait_ge(xT_hi_ready, after)
                sp.wait_ge(xT_lo_ready, after)
                sp.dma_start(xT[:, :, :], a["xT"][:, bass.ds(after, 1)].rearrange("p o k n -> p (o k) n")).then_inc(xT_in, 16)

        @block.gpsimd
        def _(pool):
            pool.memset(ksel[:, :, :, :], 0.0).then_inc(setup_done, 1)
            with pool.Fori(0, B) as b:
                pool.wait_ge(res_ready, b + 1)
                pool.tensor_copy(tiles(xs, b), res[:, :, :]).then_inc(res_kept, 1)

        @block.tensor
        def _(pe):
            def key_value(b, t):
                tok = slice(t * P, (t + 1) * P)
                for part, (bank, done) in enumerate(((bank_a[0], k_done), (bank_a[1], v_done))):
                    if t == 0:
                        pe.wait_ge(m_lo_ready, 8 * b)
                    else:
                        pe.wait_ge((zk_ready, v_ready)[part], NT * b + t)
                    cols = slice(part * 512, (part + 1) * 512)
                    n = 0
                    for k in range(KD):
                        for lhs, rhs in split_passes(xT_hi[:, k, tok], xT_lo[:, k, tok], wkv_hi[:, k, cols], wkv_lo[:, k, cols]):
                            mm = pe.matmul(bank[:, :], lhs, rhs, start=n == 0, stop=n == 3 * KD - 1)
                            n += 1
                    mm.then_inc(done, 1)

            def state(b):
                pe.wait_ge(v_ready, NT * b + NT)
                pe.wait_ge(sk_ready, NT * b + NT)
                for g in range(G0):
                    hd = slice(g * DH0, (g + 1) * DH0)
                    for t in range(NT):
                        mm = pe.matmul(bank_a[0][:, hd], v[:, t, hd], sk[:, t, hd], start=t == 0, stop=t == NT - 1)
                mm.then_inc(kvT_done, 1)
                for g in range(G0):
                    hd = slice(g * DH0, (g + 1) * DH0)
                    for t in range(NT):
                        mm = pe.matmul(bank_a[1][:, g:g + 1], sk[:, t, hd], ones[:, :], start=t == 0, stop=t == NT - 1)
                mm.then_inc(ksum_done, 1)

            def query(b, n):
                g, j = ORDER0[n]
                hd = slice((J0 * g + j) * DH0, (J0 * g + j + 1) * DH0)
                if n < 3:
                    pe.wait_ge(scaled, H0 * b)
                else:
                    pe.wait_ge(sq_ready, H0 * b + n - 2)
                i = 0
                for k in range(KD):
                    for lhs, rhs in split_passes(wq_hi[:, k, hd], wq_lo[:, k, hd], xT_hi[:, k, :], xT_lo[:, k, :]):
                        mm = pe.matmul(bank_q[n % 3][:, :], lhs, rhs, start=i == 0, stop=i == 3 * KD - 1)
                        i += 1
                mm.then_inc(q_done, 1)

            def norm(b, j):
                if j == 0:
                    pe.wait_ge(ksel_ready, b + 1)
                    pe.wait_ge(den_ready, b)
                pe.wait_ge(sq_ready, H0 * b + G0 * (j + 1))
                for g in range(G0):
                    mm = pe.matmul(bank_n[32 * g:32 * g + 32, :], ksel[:, g, j, :], sq[:, G0 * j + g, :],
                                   start=j == 0, stop=j == J0 - 1)
                if j == J0 - 1:
                    mm.then_inc(norm_done, 1)

            def output_map(b, p):
                if p == 0:
                    pe.wait_ge(kvT_ready, b + 1)
                elif p == 1:
                    pe.wait_ge(ksel_ready, b + 1)
                else:
                    pe.wait_ge(m_lo_ready, 8 * b + p - 1)
                for i in range(2):
                    g, j = ORDER0[2 * p + i]
                    mm = pe.matmul(bank_a[p % 2][:, i * D:(i + 1) * D], kvT[:, g * DH0:(g + 1) * DH0], wo[:, J0 * g + j, :],
                                   start=True, stop=True)
                mm.then_inc(m_done, 1)

            def factor(b, n):
                g, j = ORDER0[n]
                h = J0 * g + j
                if n == 0:
                    pe.wait_ge(parts_ready, b + 1)
                if n < 3:
                    pe.wait_ge(sq_ready, H0 * b + H0)
                else:
                    pe.wait_ge(scaled, H0 * b + n - 2)
                pe.matmul(bank_q[(H0 + n) % 3][:, :], pick[:, h:h + 1].broadcast_to([P, P]), rn_parts[:, :],
                          start=True, stop=True).then_inc(bc_done, 1)

            def project(b, n):
                if n == 0:
                    pe.wait_ge(res_ready, b)
                pe.wait_ge(s_hi_ready, H0 * b + n + 1)
                pe.wait_ge(s_lo_ready, H0 * b + n + 1)
                if n % 2 == 0:
                    pe.wait_ge(m_lo_ready, 8 * b + n // 2 + 1)
                m = (n // 2) % 4
                cols = slice((n % 2) * D, (n % 2 + 1) * D)
                for t in range(NT):
                    tok = slice(t * P, (t + 1) * P)
                    for i, (lhs, rhs) in enumerate(split_passes(s_hi[:, n % 2, tok], s_lo[:, n % 2, tok], m_hi[:, m, cols], m_lo[:, m, cols])):
                        mm = pe.matmul(bank_y4[:, t, :], lhs, rhs,
                                       start=n == 0 and i == 0 and t % 2 == 0, stop=n == H0 - 1 and i == 2,
                                       skip_group_check=True)
                mm.then_inc(y_done, 1)

            pe.wait_ge(w_lo_ready, 1)
            pe.wait_ge(w_hi_ready, 1)
            with pe.Fori(0, B) as b:
                pe.wait_ge(xT_hi_ready, b + 1)
                pe.wait_ge(xT_lo_ready, b + 1)
                for t in range(NT):
                    key_value(b, t)
                pe.wait_ge(w_hi_ready, len(W_STAGES))
                pe.wait_ge(w_lo_ready, len(W_STAGES))
                for n in range(3):
                    query(b, n)
                pe.wait_ge(small_in, 16 * N_SMALL)
                state(b)
                for n in range(3, H0):
                    query(b, n)
                    if n % G0 == 1 and n > G0:
                        norm(b, n // G0 - 1)
                pe.wait_ge(wo_in, 16)
                output_map(b, 0)
                output_map(b, 1)
                norm(b, J0 - 1)
                output_map(b, 2)
                output_map(b, 3)
                pe.wait_ge(setup_done, 4)
                factor(b, 0)
                factor(b, 1)
                for n in range(H0):
                    if n + 2 < H0:
                        factor(b, n + 2)
                    project(b, n)
                    if n % 2 == 1 and n < 8:
                        output_map(b, 4 + n // 2)

        @block.scalar
        def _(act):
            def split_x(b):
                act.wait_ge(xT_in, 16 * (b + 1))
                act.wait_ge(q_done, H0 * b)
                act.activation(xT_hi[:, :, :], xT[:, :, :], ACT.Copy).then_inc(xT_hi_ready, 1)

            def map_hi(b, p):
                act.wait_ge(m_done, 8 * b + p + 1)
                act.wait_ge(y_done, H0 * b + max(0, 2 * (p - 4) + 2))
                act.activation(m_hi[:, p % 4, :], bank_a[p % 2][:, :], ACT.Copy).then_inc(m_hi_ready, 1)

            def query_exp(b, n):
                g, j = ORDER0[n]
                h = J0 * g + j
                act.wait_ge(q_done, H0 * b + n + 1)
                act.wait_ge(sq_ready, H0 * b + max(0, n - 2))
                act.activation(eq[:, n % 3, :], bank_q[n % 3][:, :], ACT.Relu, bias=bq_neg[:, h:h + 1], scale=-1.0).then_inc(eq_capped, 1)
                act.wait_ge(eq_capped, H0 * b + n + 1)
                act.activation(eq[:, n % 3, :], eq[:, n % 3, :], ACT.Exp, scale=-1.0).then_inc(eq_ready, 1)

            def body(b, more):
                for t in range(NT):
                    act.wait_ge(zk_ready, NT * b + t + 1)
                    act.wait_ge(sk_ready, NT * b + max(0, t - 1))
                    act.activation(ek[:, t % 2, :], zk[:, t % 2, :], ACT.Relu, scale=-1.0).then_inc(ek_capped, 1)
                    act.wait_ge(ek_capped, NT * b + t + 1)
                    act.activation(ek[:, t % 2, :], ek[:, t % 2, :], ACT.Exp, scale=-1.0).then_inc(ek_ready, 1)
                for n in range(3):
                    query_exp(b, n)
                act.wait_ge(kvT_done, b + 1)
                act.wait_ge(m_done, 8 * b)
                act.activation(kvT[:, :], bank_a[0][:, :], ACT.Copy).then_inc(kvT_ready, 1)
                for n in range(3, H0):
                    query_exp(b, n)
                map_hi(b, 0)
                map_hi(b, 1)
                act.wait_ge(rn_ready, b + 1)
                act.wait_ge(parts_ready, b)
                act.activation(rn_c[:, :], rn[:, :], ACT.Copy, scale=part_c[:, 0:1]).then_inc(rn_c_ready, 1)
                map_hi(b, 2)
                map_hi(b, 3)
                for n in range(H0):
                    act.wait_ge(scaled, H0 * b + n + 1)
                    act.wait_ge(y_done, H0 * b + max(0, n - 1))
                    act.activation(s_hi[:, n % 2, :], sq[:, n, :], ACT.Copy).then_inc(s_hi_ready, 1)
                    if n in (3, 5, 7, 9):
                        map_hi(b, 4 + (n - 3) // 2)
                    if n == 10 and more:
                        split_x(b + 1)

            for s in range(len(W_STAGES)):
                act.wait_ge(stage_in[s % 2], 16 * (s // 2 + 1))
                act.activation(w_parts(s)[0], stage[:, s % 2, :], ACT.Copy).then_inc(w_hi_ready, 1)
                if s == 0:
                    split_x(0)
            act.wait_ge(small_in, 16 * N_SMALL)
            act.activation(bq1[:, :], bq[:, :], ACT.Copy, bias=1.0).then_inc(setup_done, 1)
            act.activation(bq_neg[:, :], bq[:, :], ACT.Copy, scale=-1.0).then_inc(setup_done, 1)
            act.activation(pick[:, :], pick_raw[:, :], ACT.Copy).then_inc(setup_done, 1)
            act.wait_ge(setup_done, 4)
            with act.Fori(0, B - 1) as b:
                body(b, True)
            body(B - 1, False)

        @block.vector
        def _(dve):
            def split_x(b):
                dve.wait_ge(xT_hi_ready, b + 1)
                dve.wait_ge(q_done, H0 * b)
                dve.tensor_tensor(xT_lo[:, :, :], xT[:, :, :], xT_hi[:, :, :].bitcast(F32), ALU.subtract).then_inc(xT_lo_ready, 1)

            def finish_key(b, t):
                dve.wait_ge(ek_ready, NT * b + t + 1)
                dve.scalar_tensor_tensor(out=sk[:, t, :], in0=zk[:, t % 2, :], scalar=1.0, in1=ek[:, t % 2, :],
                                         op0=ALU.add, op1=ALU.max).then_inc(sk_ready, 1)

            def key_value(b):
                for t in range(NT):
                    if t == 0:
                        dve.wait_ge(ksum_done, b)
                    else:
                        dve.wait_ge(sk_ready, NT * b + max(0, t - 1))
                    dve.wait_ge(k_done, NT * b + t + 1)
                    dve.tensor_tensor(zk[:, t % 2, :], bank_a[0][:, :], bk[:, :], ALU.add).then_inc(zk_ready, 1)
                    dve.wait_ge(v_done, NT * b + t + 1)
                    dve.tensor_tensor(v[:, t, :], bank_a[1][:, :], bv[:, :], ALU.add).then_inc(v_ready, 1)
                    if t > 0:
                        finish_key(b, t - 1)
                finish_key(b, NT - 1)

            def query(b, n):
                g, j = ORDER0[n]
                h = J0 * g + j
                dve.wait_ge(eq_ready, H0 * b + n + 1)
                dve.scalar_tensor_tensor(out=sq[:, n, :], in0=bank_q[n % 3][:, :], scalar=bq1[:, h:h + 1], in1=eq[:, n % 3, :],
                                         op0=ALU.add, op1=ALU.max).then_inc(sq_ready, 1)

            def map_lo(b, p):
                dve.wait_ge(m_hi_ready, 8 * b + p + 1)
                dve.tensor_tensor(m_lo[:, p % 4, :], bank_a[p % 2][:, :], m_hi[:, p % 4, :].bitcast(F32), ALU.subtract).then_inc(m_lo_ready, 1)

            def scaled_lo(b, n):
                dve.wait_ge(s_hi_ready, H0 * b + n + 1)
                dve.wait_ge(scaled, H0 * b + n + 1)
                dve.tensor_tensor(s_lo[:, n % 2, :], sq[:, n, :], s_hi[:, n % 2, :].bitcast(F32), ALU.subtract).then_inc(s_lo_ready, 1)

            def body(b, more):
                key_value(b)
                dve.wait_ge(s_hi_ready, H0 * b)
                dve.wait_ge(s_lo_ready, H0 * b)
                for n in range(3):
                    query(b, n)
                dve.wait_ge(ksum_done, b + 1)
                dve.wait_ge(norm_done, b)
                for g in range(G0):
                    dst = ksel[:, g, :, :].rearrange("p j c -> p (j c)")
                    for r in range(2):
                        cp = dve.tensor_copy(dst[:, 4 * r:4 * r + 3 * 33 + 1:33], bank_a[1][:, g:g + 1].broadcast_to([P, J0]))
                cp.then_inc(ksel_ready, 1)
                for n in range(3, H0):
                    query(b, n)
                map_lo(b, 0)
                map_lo(b, 1)
                dve.wait_ge(norm_done, b + 1)
                dve.tensor_scalar(den[:, :], bank_n[:, :], DEN_EPS, None, ALU.add).then_inc(den_ready, 1)
                dve.wait_ge(den_ready, b + 1)
                dve.reciprocal(rn[:, :], den[:, :]).then_inc(rn_ready, 1)
                dve.wait_ge(rn_c_ready, b + 1)
                dve.wait_ge(rn_ready, b + 1)
                dve.wait_ge(bc_done, H0 * b)
                dve.scalar_tensor_tensor(out=rn_parts[:, :], in0=rn[:, :], scalar=part_m[:, 0:1], in1=rn_c[:, :].bitcast(F32),
                                         op0=ALU.mult, op1=ALU.add).then_inc(parts_ready, 1)
                map_lo(b, 2)
                map_lo(b, 3)
                for n in range(H0):
                    dve.wait_ge(bc_done, H0 * b + n + 1)
                    dve.tensor_tensor(sq[:, n, :], sq[:, n, :], bank_q[(H0 + n) % 3][:, :], ALU.mult).then_inc(scaled, 1)
                    if n > 0:
                        scaled_lo(b, n - 1)
                    if n in (4, 6, 8, 10):
                        map_lo(b, 4 + (n - 4) // 2)
                    if n == 12 and more:
                        split_x(b + 1)
                scaled_lo(b, H0 - 1)
                dve.wait_ge(y_done, H0 * b + H0)
                dve.wait_ge(res_kept, b)
                dve.tensor_tensor(res[:, :, :], bank_y4, tiles(xs, b), ALU.add).then_inc(res_ready, 1)
                dve.wait_ge(res_ready, b + 1)
                for t in range(NT):
                    dve.bn_stats(bn[:, t, :], res[:, t, :]).then_inc(bn_ready, 1)
                dve.wait_ge(bn_ready, NT * (b + 1))
                merge_stats(dve, Steps(dve, merge_step, MERGE_STEPS, b), bn, bn_tmp,
                            tiles(stats, b)[:, :, 0:1], tiles(stats, b)[:, :, 1:2]).then_inc(stats_ready, 1)

            for s in range(len(W_STAGES)):
                dve.wait_ge(w_hi_ready, s + 1)
                hi, lo = w_parts(s)
                dve.tensor_tensor(lo, stage[:, s % 2, :], hi.bitcast(F32), ALU.subtract).then_inc(w_lo_ready, 1)
                if s == 0:
                    split_x(0)
            dve.wait_ge(setup_done, 4)
            dve.wait_ge(small_in, 16 * N_SMALL)
            dve.wait_ge(x_in, 16)
            dve.wait_ge(w_lo_ready, len(W_STAGES))
            with dve.Fori(0, B - 1) as b:
                body(b, True)
            body(B - 1, False)


E0, S0, R0 = 8, 8, 8
W0 = E0 * (S0 + R0) + E0
U0 = E0 * R0 + E0
Z_MIN = -85.0
H1, DH1 = 16, 16
SCALE1 = DH1 ** -0.5
ROWS_S = 3 * DH1
ROWS_ST = ROWS_S + 2
SUBS = 16
LEAD = 6
SLOTS = 8
E1, F1, R1 = 8, 32, 16
WA = E1 * F1 + E1 * R1
WB = E1 * F1 + E1


def at_least(eng, sem, value):
    if not isinstance(value, int) or value > 0:
        eng.wait_ge(sem, value)


def tile(x, b, t):
    return x[:, NT * b + t, :] if isinstance(b, int) else x[:, bass.ds(NT * b + t, 1), :].rearrange("p o n -> p (o n)")


def by_tile(x):
    return x[:, :].rearrange("p (t o) -> p t o", o=1)


def over_last(x, n):
    return x.rearrange("p (a o) -> p a o", o=1).broadcast_to([x.shape[0], x.shape[1], n])


def over_tiles(x):
    return x.rearrange("p (o n) -> p o n", o=1).broadcast_to([P, NT, x.shape[1]])


def update_attention_experts(nc, a, xs, stats, out):
    with ExitStack() as ctx:
        def sb(name, shape, dt=F32, parts=P):
            return ctx.enter_context(nc.sbuf_tensor(name, [parts] + shape, dt))

        def sem(name):
            return ctx.enter_context(nc.semaphore(name))

        ident, ones = sb("ident", [P]), sb("ones1", [P])
        fw, md = sb("fw", [KD, W0]), sb("md", [KD, 2 * E0])
        fprod, fconst = sb("fprod", [KD, W0]), sb("fconst", [W0])
        slope, center, rank = sb("slope", [E0]), sb("center", [E0]), sb("rank", [E0])
        down0 = sb("down0", [D], parts=U0)
        wqkv_hi, wqkv_lo = sb("wqkv_hi", [KD, 3 * D], F32R), sb("wqkv_lo", [KD, 3 * D], F32R)
        wo, bo = sb("wo1", [2, D]), sb("bo", [D])
        win_hi, win_lo = sb("win_hi", [KD, WA + WB], F32R), sb("win_lo", [KD, WA + WB], F32R)
        down1 = sb("down1", [3, D])
        half = sb("half", [B * NT])
        rstd1 = sb("rstd1", [B * NT])
        xf = sb("xf", [NT, D])
        ssq, junk = sb("ssq", [NT]), sb("junk", [NT, D], mybir.dt.bfloat16)
        pr, pr2 = sb("pr", [NT, W0]), sb("pr2", [NT, E0 * S0])
        gt = {n: sb(f"gt_{n}", [NT, E0]) for n in (
            "score", "dist", "rdist", "rel", "cent", "z", "zc", "e", "e1", "gate", "eq", "key", "pick", "w")}
        gmax, kmax, keep = sb("gmax", [NT]), sb("kmax", [NT]), sb("keep", [NT])
        hm = sb("hm", [NT, U0])
        hmT = sb("hmT", [T], parts=U0)
        x2T_hi, x2T_lo = sb("x2T_hi", [KD, T], F32R), sb("x2T_lo", [KD, T], F32R)
        qk_hi, qk_lo = sb("qk_hi", [2, T], F32R), sb("qk_lo", [2, T], F32R)
        qs, ks = sb("qs", [H1, T], F32R, parts=64), sb("ks", [H1, T], F32R, parts=64)
        v = sb("v1", [NT, H1, 32])
        nmax = sb("nmax", [4, NT, 4])
        sh_hi, sh_lo = sb("sh_hi", [T], F32R, parts=4), sb("sh_lo", [T], F32R, parts=4)
        probs = sb("probs", [SLOTS, T])
        raw = probs[:, :, :].rearrange("p s n -> p (s n)")
        ctT, rsum, cx = sb("ctT", [T]), sb("rsum", [NT, 4]), sb("cx", [NT, D])
        xk = sb("xk", [NT, D])
        x3T_hi, x3T_lo = sb("x3T_hi", [KD, T], F32R), sb("x3T_lo", [KD, T], F32R)
        th, sg = sb("th", [2, E1 * F1]), sb("sg", [E1 * F1])
        hid = sb("hid", [NT, 3 * P])
        turned = sb("turned", [3, T])
        hidT, x1T = turned, turned[:, 0:KD, :]
        lg = sb("lg", [NT, E1])
        rt = {n: sb(f"rt_{n}", [NT, E1]) for n in (
            "rel", "e", "sc", "eq1", "key1", "pick1", "less", "eq2", "key2", "pick2", "both", "w", "wh")}
        rm = {n: sb(f"rm_{n}", [NT]) for n in ("max", "sum", "rsum", "max1", "kmax1", "max2", "kmax2")}
        ln = {i: {"bn": sb(f"ln{i}_bn", [NT, 6]), "tmp": sb(f"ln{i}_tmp", [NT, 3]), "mean": sb(f"ln{i}_mean", [NT]), "var": sb(f"ln{i}_var", [NT]),
                  "rstd": sb(f"ln{i}_rstd", [NT])} for i in (2, 3, 4)}
        scratch = nc.dram_tensor("scratch_qk", (4, 2, DH1, P // DH1, T), F32, kind="Internal").ap()

        side = ctx.enter_context(nc.psum_tensor("side", [P, 2, 512], F32))
        side4 = side[:, :, :].rearrange("p a (t n) -> p (a t) n", t=2)
        bank_s = [ctx.enter_context(nc.psum_tensor(f"bank_s{i}", [P, 512], F32)) for i in range(2)]
        bank_st = [ctx.enter_context(nc.psum_tensor(f"bank_st{i}", [P, 512], F32)) for i in range(2)]
        bank_c = ctx.enter_context(nc.psum_tensor("bank_c", [P, 512], F32))
        bank_t = ctx.enter_context(nc.psum_tensor("bank_t", [P, 512], F32))

        consts_in, raw_in = sem("consts_in"), [sem("raw_in0"), sem("raw_in1")]
        w_hi_ready, w_lo_ready = sem("w1_hi_ready"), sem("w1_lo_ready")
        half_ready, zeros_ready, v_ones_ready, k_ones_ready = sem("half_ready"), sem("zeros_ready"), sem("v_ones_ready"), sem("k_ones_ready")
        fprod_ready, fsum_done, fconst_ready = sem("fprod_ready"), sem("fsum_done"), sem("fconst_ready")
        rstd1_ready, x1_ready = sem("rstd1_ready"), sem("x1_ready")
        x1T_done, x1T_ready, ssq_ready = sem("x1T_done"), sem("x1T_ready"), sem("ssq_ready")
        pr_done, pr_ready, gate_step, zc_ready, ge_ready, hm_ready = (
            sem("pr_done"), sem("pr_ready"), sem("gate_step"), sem("zc_ready"), sem("ge_ready"), sem("hm_ready"))
        hmT_done, hmT_ready, up_done, r2_ready = sem("hmT_done"), sem("hmT_ready"), sem("up_done"), sem("r2_ready")
        bn_ready, merge_step, var_ready, rstd_ready, x_ready = (
            {i: sem(f"ln{i}_{n}_ready") for i in (2, 3, 4)} for n in ("bn", "merge", "var", "rstd", "x"))
        x2T_done, x2T_hi_ready, x2T_lo_ready, x2_kept = sem("x2T_done"), sem("x2T_hi_ready"), sem("x2T_lo_ready"), sem("x2_kept")
        qk_done, qk_hi_ready, qk_lo_ready = sem("qk_done"), sem("qk_hi_ready"), sem("qk_lo_ready")
        scratch_out = [sem("scratch_out0"), sem("scratch_out1")]
        stack_in = [sem("stack_in0"), sem("stack_in1")]
        vp_done, v_ready = sem("vp_done"), sem("v1_ready")
        s_done, max_ready = sem("s_done"), sem("max_ready")
        maxT_done, sh_hi_ready, sh_lo_ready, shift_in = sem("maxT_done"), sem("sh_hi_ready"), sem("sh_lo_ready"), sem("shift_in")
        st_done, p_ready, pv_done = sem("st_done"), sem("p_ready"), sem("pv_done")
        ct_ready, ctT_done, rsum_ready, cx_ready = sem("ct_ready"), sem("ctT_done"), sem("rsum_ready"), sem("cx_ready")
        wo_done, r3_ready = sem("wo_done"), sem("r3_ready")
        x3T_done, x3T_hi_ready, x3T_lo_ready = sem("x3T_done"), sem("x3T_hi_ready"), sem("x3T_lo_ready")
        in_done, in_copied, sg_ready, hid_ready = sem("in_done"), sem("in_copied"), sem("sg_ready"), sem("hid_ready")
        route_step, rel_ready, re_ready, hw_ready = sem("route_step"), sem("rel_ready"), sem("re_ready"), sem("hw_ready")
        hidT_done, hidT_ready, down_done, r4_ready, stored = (
            sem("hidT_done"), sem("hidT_ready"), sem("down_done"), sem("r4_ready"), sem("stored"))

        CONSTS = [(ident, "ident"), (ones, "ones_pp"), (fw, "fw"), (md, "md"), (slope, "slope"), (center, "center"),
                  (rank, "rank"), (down0, "down0"), (wo, "wo1"), (bo, "bo")]

        def whole(t):
            return t[tuple(slice(None) for _ in t.shape)]

        block = ctx.enter_context(nc.Block())

        @block.sync
        def _(sp):
            def save_qk(b, half_):
                for i in (2 * half_, 2 * half_ + 1):
                    for part, (src, ready) in enumerate(((qk_hi, qk_hi_ready), (qk_lo, qk_lo_ready))):
                        sp.wait_ge(ready, 4 * b + i + 1)
                        sp.dma_start(scratch[i, part].rearrange("p h n -> h p n"), src[:, i % 2, :].bitcast(F32)).then_inc(scratch_out[i % 2], 16)

            def load_stack(b, half_):
                for i in range(2):
                    sp.wait_ge(scratch_out[i], 64 * b + 32 * (half_ + 1))
                if half_:
                    at_least(sp, st_done, 64 * b)
                heads = slice(8 * half_, 8 * half_ + 8)
                for stack, i, pair_rows, single_rows in ((qs, 2 * half_, 0, 2 * DH1), (ks, 2 * half_ + 1, DH1, 0)):
                    sp.dma_start(stack[pair_rows:pair_rows + 2 * DH1, heads, :].bitcast(F32),
                                 scratch[i].rearrange("a p h n -> (a p) h n")).then_inc(stack_in[half_], 16)
                    sp.dma_start(stack[single_rows:single_rows + DH1, heads, :].bitcast(F32), scratch[i, 0]).then_inc(stack_in[half_], 16)

            def shift(b, g):
                sp.wait_ge(sh_lo_ready, 4 * b + g + 1)
                for i, part in enumerate((sh_hi, sh_lo)):
                    sp.dma_start(qs[ROWS_S + i:ROWS_S + i + 1, 4 * g:4 * g + 4, :].bitcast(F32), part[:, :].bitcast(F32)).then_inc(shift_in, 16)

            def store(b):
                sp.wait_ge(x_ready[4], NT * (b + 1))
                dst = out.rearrange("b (c p h) d -> b p c (h d)", p=P, h=2)
                dst = dst[b] if isinstance(b, int) else dst[bass.ds(b, 1)].rearrange("o p c n -> (o p) c n")
                sp.dma_start(dst, xk[:, :, :].rearrange("p (c h) d -> p c (h d)", h=2)).then_inc(stored, 16)

            def body(b, front, back):
                load_stack(b, 1)
                shift(b, 1)
                shift(b, 2)
                if front:
                    save_qk(b + 1, 0)
                    load_stack(b + 1, 0)
                    save_qk(b + 1, 1)
                shift(b, 3)
                if front:
                    shift(b + 1, 0)
                if back:
                    store(b - 1)

            sp.dma_start(raw[:, 0:KD * 3 * D], a["wqkv1"]).then_inc(raw_in[0], 16)
            for dst, name in CONSTS:
                sp.dma_start(whole(dst), a[name]).then_inc(consts_in, 16)
            sp.dma_start(down1[:, :, :], a["down1"]).then_inc(stored, 16)
            sp.dma_start(raw[:, KD * 3 * D:KD * (3 * D + WA + WB)], a["win1"]).then_inc(raw_in[1], 16)
            sp.wait_ge(k_ones_ready, 1)
            save_qk(0, 0)
            load_stack(0, 0)
            save_qk(0, 1)
            shift(0, 0)
            body(0, True, False)
            with sp.Fori(1, B - 1) as b:
                body(b, True, True)
            body(B - 1, False, True)
            store(B - 1)
            sp.wait_ge(stored, 16 * B + 16)

        @block.gpsimd
        def _(pool):
            def rstd(i, b):
                pool.wait_ge(var_ready[i], b + 1)
                pool.tensor_tensor(ln[i]["rstd"][:, :], ln[i]["var"][:, :], half[:, 0:NT], ALU.pow).then_inc(rstd_ready[i], 1)

            def keep_x2(b):
                pool.wait_ge(x2T_done, b + 1)
                pool.tensor_tensor(tiles(xs, b), xf[:, :, :], over_tiles(bo[:, :]), ALU.add).then_inc(x2_kept, 1)

            def body(b, front, back):
                if back:
                    rstd(3, b - 1)
                if front:
                    rstd(2, b + 1)
                    keep_x2(b + 1)
                if back:
                    rstd(4, b - 1)

            pool.memset(half[:, :], -0.5).then_inc(half_ready, 1)
            pool.wait_ge(half_ready, 1)
            pool.tensor_tensor(rstd1[:, :].rearrange("p (t o) -> p t o", o=1), stats[:, :, 1:2], half[:, :].rearrange("p (t o) -> p t o", o=1), ALU.pow).then_inc(rstd1_ready, 1)
            pool.wait_ge(rstd1_ready, 1)
            pool.memset(v[:, :, :, :], 0.0).then_inc(zeros_ready, 1)
            pool.wait_ge(zeros_ready, 1)
            pool.memset(v[:, :, :, DH1:DH1 + 1], 1.0).then_inc(v_ones_ready, 1)
            pool.wait_ge(v_ones_ready, 1)
            pool.memset(ks[32:64, :, :].bitcast(F32), 1.0).then_inc(k_ones_ready, 1)
            pool.wait_ge(k_ones_ready, 1)
            pool.wait_ge(consts_in, 16 * len(CONSTS))
            rstd(2, 0)
            keep_x2(0)
            body(0, True, False)
            with pool.Fori(1, B - 1) as b:
                body(b, True, True)
            body(B - 1, False, True)
            rstd(3, B - 1)
            rstd(4, B - 1)

        @block.tensor
        def _(pe):

            def turn(src, done):
                for k in range(KD):
                    for t in range(NT):
                        mm = pe.transpose(side[:, k, t * P:(t + 1) * P], src[:, t, k * P:(k + 1) * P], ident[:, :])
                mm.then_inc(done, 1)

            def turn_x1(b, after):
                pe.wait_ge(x1_ready, NT * (b + 1))
                at_least(pe, *after)
                turn(xf, x1T_done)

            def select(b):
                pe.wait_ge(x1T_ready, b + 1)
                for t in range(NT):
                    for k in range(KD):
                        mm = pe.matmul(side4[:, t, 0:W0], x1T[:, k, t * P:(t + 1) * P], fw[:, k, :], start=k == 0, stop=k == KD - 1)
                mm.then_inc(pr_done, 1)

            def turn_hm(b, after):
                pe.wait_ge(hm_ready, b + 1)
                at_least(pe, *after)
                for t in range(NT):
                    mm = pe.transpose(side[0:U0, 0, t * P:(t + 1) * P], hm[:, t, :], ident[:, :])
                mm.then_inc(hmT_done, 1)

            def update(b):
                pe.wait_ge(hmT_ready, b + 1)
                for t in range(NT):
                    mm = pe.matmul(side4[:, t, :], hmT[:, t * P:(t + 1) * P], down0[:, :], start=True, stop=True)
                mm.then_inc(up_done, 1)

            def turn_x2(b, after):
                pe.wait_ge(x_ready[2], NT * (b + 1))
                at_least(pe, *after)
                turn(xf, x2T_done)

            def query_key(b, parts):
                if 0 in parts:
                    pe.wait_ge(x2T_hi_ready, b + 1)
                    pe.wait_ge(x2T_lo_ready, b + 1)
                for i in parts:
                    if i >= 2:
                        pe.wait_ge(qk_lo_ready, 4 * b + i - 1)
                    first = (i % 2) * D + (i // 2) * P
                    cols = slice(first, first + P)
                    n = 0
                    for k in range(KD):
                        for lhs, rhs in split_passes(wqkv_hi[:, k, cols], wqkv_lo[:, k, cols], x2T_hi[:, k, :], x2T_lo[:, k, :]):
                            mm = pe.matmul(side[:, i % 2, :], lhs, rhs, start=n == 0, stop=n == 3 * KD - 1)
                            n += 1
                    mm.then_inc(qk_done, 1)

            def value(b):
                for i in range(2):
                    for t in (2 * i, 2 * i + 1):
                        tok = slice(t * P, (t + 1) * P)
                        n = 0
                        for k in range(KD):
                            for lhs, rhs in split_passes(x2T_hi[:, k, tok], x2T_lo[:, k, tok], wqkv_hi[:, k, 2 * D:], wqkv_lo[:, k, 2 * D:]):
                                mm = pe.matmul(side4[:, t, :], lhs, rhs, start=n == 0, stop=n == 3 * KD - 1)
                                n += 1
                    mm.then_inc(vp_done, 1)

            def score(b, h, t):
                if h % 8 == 0 and t == 0:
                    pe.wait_ge(stack_in[h // 8], 64 * (b + 1))
                u = 4 * h + t
                at_least(pe, max_ready, 64 * b + u - 1)
                pe.matmul(bank_s[u % 2][:, :], qs[0:ROWS_S, h, t * P:(t + 1) * P], ks[0:ROWS_S, h, :],
                          start=True, stop=True).then_inc(s_done, 1)

            def turn_max(b, g, after):
                pe.wait_ge(max_ready, 64 * b + 16 * (g + 1))
                at_least(pe, *after)
                for t in range(NT):
                    mm = pe.transpose(bank_t[0:4, t * P:(t + 1) * P], nmax[:, g, t, :], ident[:, :])
                mm.then_inc(maxT_done, 1)

            def turned_score(b, s, j):
                g, kt = divmod(s, 4)
                if kt == 0 and j == 0:
                    pe.wait_ge(shift_in, 32 * (4 * b + g + 1))
                h, u = 4 * g + j, 4 * s + j
                at_least(pe, p_ready, 64 * b + u - 1)
                pe.matmul(bank_st[u % 2][:, :], ks[0:ROWS_ST, h, kt * P:(kt + 1) * P], qs[0:ROWS_ST, h, :],
                          start=True, stop=True).then_inc(st_done, 1)

            def context(b, s):
                g, kt = divmod(s, 4)
                if s == 0:
                    pe.wait_ge(v_ready, 2 * (b + 1))
                    pe.wait_ge(v_ones_ready, 1)
                if kt == 0:
                    at_least(pe, ct_ready, 4 * b + g)
                pe.wait_ge(p_ready, 64 * b + 4 * s + 4)
                for j in range(4):
                    mm = pe.matmul(bank_c[32 * j:32 * j + 32, :], v[:, kt, 4 * g + j, :], probs[:, (4 * s + j) % SLOTS, :],
                                   start=kt == 0, stop=kt == 3)
                mm.then_inc(pv_done, 1)

            def turn_context(b, g, after):
                pe.wait_ge(ct_ready, 4 * b + g + 1)
                at_least(pe, *after)
                for t in range(NT):
                    mm = pe.transpose(bank_t[:, t * P:(t + 1) * P], ctT[:, t * P:(t + 1) * P], ident[:, :])
                mm.then_inc(ctT_done, 1)

            def out_project(b, after):
                pe.wait_ge(cx_ready, 4 * (b + 1))
                at_least(pe, *after)
                for c in range(2):
                    for half_ in range(2):
                        for i in range(2):
                            mm = pe.matmul(side4[:, 2 * c + half_, :], cx[:, 2 * half_ + i, c * P:(c + 1) * P], wo[:, i, :],
                                           start=i == 0, stop=i == 1)
                mm.then_inc(wo_done, 1)

            def turn_x3(b, after):
                pe.wait_ge(x_ready[3], NT * (b + 1))
                at_least(pe, *after)
                turn(xk, x3T_done)

            def expert_in(b, t, after):
                if t == 0:
                    pe.wait_ge(x3T_hi_ready, b + 1)
                    pe.wait_ge(x3T_lo_ready, b + 1)
                at_least(pe, *after)
                tok = slice(t * P, (t + 1) * P)
                for i, cols in enumerate((slice(0, WA), slice(WA, WA + WB))):
                    n = 0
                    for k in range(KD):
                        for lhs, rhs in split_passes(x3T_hi[:, k, tok], x3T_lo[:, k, tok], win_hi[:, k, cols], win_lo[:, k, cols]):
                            mm = pe.matmul(side[:, i, 0:cols.stop - cols.start], lhs, rhs, start=n == 0, stop=n == 3 * KD - 1)
                            n += 1
                mm.then_inc(in_done, 1)

            def turn_hidden(b, thirds):
                if 0 in thirds:
                    pe.wait_ge(hw_ready, 2 * (b + 1))
                else:
                    pe.wait_ge(hidT_ready, 2 * b + 1)
                for c in thirds:
                    for t in range(NT):
                        mm = pe.transpose(side[:, c % 2, t * P:(t + 1) * P], hid[:, t, c * P:(c + 1) * P], ident[:, :])
                mm.then_inc(hidT_done, 1)

            def expert_out(b):
                pe.wait_ge(hidT_ready, 2 * (b + 1))
                for t in range(NT):
                    for c in range(3):
                        mm = pe.matmul(side4[:, t, :], hidT[:, c, t * P:(t + 1) * P], down1[:, c, :], start=c == 0, stop=c == 2)
                mm.then_inc(down_done, 1)

            def pair(b, s, js, front):
                for j in js:
                    turned_score(b, s, j)
                    if s + LEAD < H1:
                        score(b, s + LEAD, j)
                    elif front:
                        score(b + 1, s + LEAD - H1, j)

            def body(b, front, back):
                for s in range(SUBS):
                    pair(b, s, (0, 1), front)
                    if s:
                        context(b, s - 1)
                    elif back:
                        context(b - 1, SUBS - 1)
                    if s == 0:
                        value(b)
                    if s == 1 and back:
                        turn_context(b - 1, 3, after=(sh_lo_ready, 4 * b + 1))
                    if s in (5, 9, 13):
                        turn_context(b, s // 4 - 1, after=(sh_lo_ready, 4 * b + s // 4 + 1))
                    if s in (2, 6, 10):
                        turn_max(b, s // 4 + 1, after=(cx_ready, 4 * b + s // 4))
                    if s == 14 and front:
                        turn_max(b + 1, 0, after=(cx_ready, 4 * b + 3))
                    if s == 1 and front:
                        turn_x1(b + 1, after=(v_ready, 2 * (b + 1)))
                    if s == 2 and front:
                        select(b + 1)
                    if s == 3 and back:
                        out_project(b - 1, after=(pr_ready, b + 2) if front else (v_ready, 2 * (b + 1)))
                    if s == 4 and front:
                        turn_hm(b + 1, after=(r3_ready, b) if back else (pr_ready, b + 2))
                    if s == 5 and front:
                        update(b + 1)
                    if s == 6 and back:
                        turn_x3(b - 1, after=(r2_ready, NT * (b + 2)) if front else (r3_ready, b))
                    if s == 7 and front:
                        turn_x2(b + 1, after=(x3T_lo_ready, b) if back else (r2_ready, NT * (b + 2)))
                    if s == 8 and front:
                        query_key(b + 1, (0, 1))
                    if s == 12 and back:
                        expert_in(b - 1, 3, after=(hid_ready, NT * (b - 1) + 3))
                    if s == 14 and back:
                        turn_hidden(b - 1, (2,))
                    pair(b, s, (2, 3), front)
                    if s == 8 and front:
                        query_key(b + 1, (2, 3))
                    if s == 9 and back:
                        expert_in(b - 1, 0, after=(qk_lo_ready, 4 * (b + 2)) if front else (x3T_lo_ready, b))
                    if s in (10, 11) and back:
                        expert_in(b - 1, s - 9, after=(hid_ready, NT * (b - 1) + s - 9))
                    if s == 13 and back:
                        turn_hidden(b - 1, (0, 1))
                    if s == 14 and back:
                        expert_out(b - 1)

            pe.wait_ge(consts_in, 16 * len(CONSTS))
            pe.wait_ge(fprod_ready, 3)
            for k in range(KD):
                mm = pe.matmul(bank_t[:, 0:W0], ones[:, :], fprod[:, k, :], start=k == 0, stop=k == KD - 1)
            mm.then_inc(fsum_done, 1)
            turn_x1(0, after=(r3_ready, 0))
            select(0)
            turn_hm(0, after=(pr_ready, 1))
            update(0)
            turn_x2(0, after=(r2_ready, NT))
            pe.wait_ge(w_hi_ready, 2)
            pe.wait_ge(w_lo_ready, 2)
            query_key(0, range(4))
            for h in range(LEAD):
                for t in range(NT):
                    score(0, h, t)
                if h == 4:
                    turn_max(0, 0, after=(fconst_ready, 1))
            body(0, True, False)
            with pe.Fori(1, B - 1) as b:
                body(b, True, True)
            body(B - 1, False, True)
            context(B - 1, SUBS - 1)
            turn_context(B - 1, 3, after=(cx_ready, 4 * B - 1))
            out_project(B - 1, after=(r4_ready, B - 1))
            turn_x3(B - 1, after=(r3_ready, B))
            for t in range(NT):
                expert_in(B - 1, t, after=(hid_ready, NT * (B - 1) + t) if t else (x3T_lo_ready, B))
            turn_hidden(B - 1, (0, 1))
            turn_hidden(B - 1, (2,))
            expert_out(B - 1)

        @block.scalar
        def _(act):
            def x1T_out(b):
                act.wait_ge(x1T_done, b + 1)
                act.activation(x1T, side[:, :, :], ACT.Copy).then_inc(x1T_ready, 1)

            def squares(b):
                act.wait_ge(x1_ready, NT * (b + 1))
                at_least(act, hm_ready, b)
                for t in range(NT):
                    act.activation(junk[:, t, :], xf[:, t, :], ACT.Square, accum_out=ssq[:, t:t + 1]).then_inc(ssq_ready, 1)

            def gate_exp(b):
                act.wait_ge(zc_ready, b + 1)
                act.activation(gt["e"][:, :, :], gt["zc"][:, :, :], ACT.Exp, scale=-1.0).then_inc(ge_ready, 1)

            def hmT_out(b):
                act.wait_ge(hmT_done, b + 1)
                act.activation(hmT[:, :], side[0:U0, 0, :], ACT.Copy).then_inc(hmT_ready, 1)

            def x2T_out(b):
                act.wait_ge(x2T_done, b + 1)
                act.activation(x2T_hi[:, :, :], side[:, :, :], ACT.Copy).then_inc(x2T_hi_ready, 1)

            def qk_out(b, parts):
                for i in parts:
                    act.wait_ge(qk_done, 4 * b + i + 1)
                    at_least(act, scratch_out[i % 2], 64 * b + 32 * (i // 2))
                    act.activation(qk_hi[:, i % 2, :], side[:, i % 2, :], ACT.Copy).then_inc(qk_hi_ready, 1)

            def exponentials(b, s, js):
                if 0 in js:
                    at_least(act, pv_done, SUBS * b + s - 1)
                for j in js:
                    u = 4 * s + j
                    act.wait_ge(st_done, 64 * b + u + 1)
                    act.activation(probs[:, u % SLOTS, :], bank_st[u % 2][:, :], ACT.Exp, scale=SCALE1).then_inc(p_ready, 1)

            def shift_hi(b, g):
                act.wait_ge(maxT_done, 4 * b + g + 1)
                at_least(act, shift_in, 32 * (4 * b + g))
                act.activation(sh_hi[:, :], bank_t[0:4, :], ACT.Copy).then_inc(sh_hi_ready, 1)

            def context_out(b, g):
                act.wait_ge(pv_done, SUBS * b + 4 * g + 4)
                at_least(act, ctT_done, 4 * b + g)
                act.activation(ctT[:, :], bank_c[:, :], ACT.Copy).then_inc(ct_ready, 1)

            def x3T_out(b):
                act.wait_ge(x3T_done, b + 1)
                act.activation(x3T_hi[:, :, :], side[:, :, :], ACT.Copy).then_inc(x3T_hi_ready, 1)

            def expert_in(b, t):
                act.wait_ge(in_done, NT * b + t + 1)
                if t >= 2:
                    act.wait_ge(sg_ready, NT * b + t - 1)
                act.activation(th[:, t % 2, :], side[:, 0, 0:E1 * F1], ACT.Tanh, scale=0.5)
                act.activation(hid[:, t, E1 * F1:3 * P], side[:, 0, E1 * F1:WA], ACT.Copy)
                act.activation(lg[:, t, :], side[:, 1, E1 * F1:WB], ACT.Copy).then_inc(in_copied, 1)

            def route_exp(b):
                act.wait_ge(rel_ready, b + 1)
                act.activation(rt["e"][:, :, :], rt["rel"][:, :, :], ACT.Exp).then_inc(re_ready, 1)

            def hidden_out(b):
                act.wait_ge(hidT_done, 2 * b + 1)
                act.activation(hidT[:, 0:2, :], side[:, :, :], ACT.Copy).then_inc(hidT_ready, 1)
                act.wait_ge(hidT_done, 2 * b + 2)
                act.activation(hidT[:, 2, :], side[:, 0, :], ACT.Copy).then_inc(hidT_ready, 1)

            def body(b, front, back):
                for s in range(SUBS):
                    exponentials(b, s, (0, 1))
                    if s == 3 and front:
                        gate_exp(b + 1)
                    if s == 9 and front:
                        qk_out(b + 1, (2, 3))
                    if s == 8 and front:
                        qk_out(b + 1, (0, 1))
                    if 10 <= s < 13 and back:
                        expert_in(b - 1, s - 10)
                    if s == 14 and back:
                        hidden_out(b - 1)
                    exponentials(b, s, (2, 3))
                    if s == 0 and back:
                        context_out(b - 1, 3)
                    if s in (4, 8, 12):
                        context_out(b, s // 4 - 1)
                    if s in (2, 6, 10):
                        shift_hi(b, s // 4 + 1)
                    if s == 14 and front:
                        shift_hi(b + 1, 0)
                    if s == 1 and front:
                        x1T_out(b + 1)
                        squares(b + 1)
                    if s == 4 and front:
                        hmT_out(b + 1)
                    if s == 6 and back:
                        x3T_out(b - 1)
                    if s == 7 and front:
                        x2T_out(b + 1)
                    if s == 12 and back:
                        expert_in(b - 1, 3)
                        route_exp(b - 1)

            x1T_out(0)
            squares(0)
            for i, n0, n1, hi in ((0, 0, KD * 3 * D, wqkv_hi), (1, KD * 3 * D, KD * (3 * D + WA + WB), win_hi)):
                act.wait_ge(raw_in[i], 16)
                act.activation(hi[:, :, :].rearrange("p k n -> p (k n)"), raw[:, n0:n1], ACT.Copy).then_inc(w_hi_ready, 1)
            gate_exp(0)
            hmT_out(0)
            x2T_out(0)
            qk_out(0, range(4))
            shift_hi(0, 0)
            act.wait_ge(w_lo_ready, 2)
            body(0, True, False)
            with act.Fori(1, B - 1) as b:
                body(b, True, True)
            body(B - 1, False, True)
            context_out(B - 1, 3)
            x3T_out(B - 1)
            for t in range(NT):
                expert_in(B - 1, t)
            route_exp(B - 1)
            hidden_out(B - 1)

        @block.vector
        def _(dve):
            def normalize_x1(b):
                if not isinstance(b, int) or b > 0:
                    dve.wait_ge(x2_kept, b)
                for t in range(NT):
                    dve.tensor_scalar(xf[:, t, :], tile(xs, b, t), tile(stats, b, t)[:, 0:1],
                                      rstd1[:, NT * b + t:NT * b + t + 1] if isinstance(b, int) else rstd1[:, bass.ds(NT * b + t, 1)],
                                      ALU.subtract, ALU.mult).then_inc(x1_ready, 1)

            def first_max(step, values, key, eq, mask, top, ktop):
                step(dve.tensor_reduce(top[:, :], values, AX.X, ALU.max))
                step(dve.tensor_tensor(eq[:, :, :], values, over_last(top[:, :], E0), ALU.is_equal))
                step(dve.tensor_tensor(key[:, :, :], eq[:, :, :], over_tiles(rank[:, :]), ALU.mult))
                step(dve.tensor_reduce(ktop[:, :], key[:, :, :], AX.X, ALU.max))
                step(dve.tensor_tensor(mask[:, :, :], key[:, :, :], over_last(ktop[:, :], E0), ALU.is_equal))

            GATE_STEPS = (6, 9)

            def gate_scores(b):
                step = Steps(dve, gate_step, sum(GATE_STEPS), b)
                dve.wait_ge(pr_done, b + 1)
                dve.tensor_tensor(pr[:, :, :], side4[:, :, 0:W0], over_tiles(fconst[:, :]), ALU.subtract).then_inc(pr_ready, 1)
                dve.wait_ge(pr_ready, b + 1)
                step(dve.tensor_tensor(pr2[:, :, :], pr[:, :, 0:E0 * S0], pr[:, :, 0:E0 * S0], ALU.mult))
                dve.tensor_reduce(gt["score"][:, :, :], pr2[:, :, :].rearrange("p t (n s) -> p t n s", s=S0), AX.X, ALU.add)
                dve.wait_ge(ssq_ready, NT * (b + 1))
                step(dve.scalar_tensor_tensor(out=gt["dist"][:, :, :], in0=pr[:, :, W0 - E0:W0], scalar=-2.0,
                                              in1=over_last(ssq[:, :], E0), op0=ALU.mult, op1=ALU.add))
                step(dve.reciprocal(gt["rdist"][:, :, :], gt["dist"][:, :, :]))
                step(dve.tensor_tensor(gt["rel"][:, :, :], gt["score"][:, :, :], gt["rdist"][:, :, :], ALU.mult))
                step(dve.tensor_tensor(gt["cent"][:, :, :], gt["rel"][:, :, :], over_tiles(center[:, :]), ALU.subtract))
                step(dve.tensor_tensor(gt["z"][:, :, :], gt["cent"][:, :, :], over_tiles(slope[:, :]), ALU.mult))
                dve.tensor_scalar(gt["zc"][:, :, :], gt["z"][:, :, :], Z_MIN, None, ALU.max).then_inc(zc_ready, 1)

            def gate_pick(b):
                step = Steps(dve, gate_step, sum(GATE_STEPS), b)
                step.n = GATE_STEPS[0]
                dve.wait_ge(ge_ready, b + 1)
                step(dve.tensor_scalar(gt["e1"][:, :, :], gt["e"][:, :, :], 1.0, None, ALU.add))
                step(dve.reciprocal(gt["gate"][:, :, :], gt["e1"][:, :, :]))
                first_max(step, gt["gate"][:, :, :], gt["key"], gt["eq"], gt["pick"], gmax, kmax)
                step(dve.tensor_scalar(keep[:, :], gmax[:, :], -1.0, 2.0, ALU.mult, ALU.add))
                step(dve.tensor_tensor(gt["w"][:, :, :], gt["pick"][:, :, :], over_last(gmax[:, :], E0), ALU.mult))
                w = gt["w"][:, :, :]
                for t in range(NT):
                    dve.tensor_tensor(hm[:, t, 0:E0 * R0].rearrange("p (n r) -> p n r", r=R0),
                                      pr[:, t, E0 * S0:E0 * (S0 + R0)].rearrange("p (n r) -> p n r", r=R0),
                                      over_last(gt["w"][:, t, :], R0), ALU.mult)
                dve.tensor_copy(hm[:, :, E0 * R0:U0], w).then_inc(hm_ready, 1)

            def stats_of(i, b, x, ready):
                for t in range(NT):
                    dve.wait_ge(ready[0], ready[1] + t if ready[2] else ready[1])
                    dve.bn_stats(ln[i]["bn"][:, t, :], x[:, t, :]).then_inc(bn_ready[i], 1)
                dve.wait_ge(bn_ready[i], NT * (b + 1))
                merge_stats(dve, Steps(dve, merge_step[i], MERGE_STEPS, b), ln[i]["bn"], ln[i]["tmp"],
                            by_tile(ln[i]["mean"]), by_tile(ln[i]["var"])).then_inc(var_ready[i], 1)

            def normalize(i, b, x):
                dve.wait_ge(rstd_ready[i], b + 1)
                for t in range(NT):
                    dve.tensor_scalar(x[:, t, :], x[:, t, :], ln[i]["mean"][:, t:t + 1], ln[i]["rstd"][:, t:t + 1],
                                      ALU.subtract, ALU.mult).then_inc(x_ready[i], 1)

            def add_update(b):
                dve.wait_ge(up_done, b + 1)
                for t in range(NT):
                    dve.scalar_tensor_tensor(out=xf[:, t, :], in0=xf[:, t, :], scalar=keep[:, t:t + 1], in1=side4[:, t, :],
                                             op0=ALU.mult, op1=ALU.add).then_inc(r2_ready, 1)
                stats_of(2, b, xf, (r2_ready, NT * b + 1, True))

            def x2T_rest(b):
                dve.wait_ge(x2T_hi_ready, b + 1)
                dve.tensor_tensor(x2T_lo[:, :, :], side[:, :, :], x2T_hi[:, :, :].bitcast(F32), ALU.subtract).then_inc(x2T_lo_ready, 1)

            def qk_rest(b, parts):
                for i in parts:
                    dve.wait_ge(qk_hi_ready, 4 * b + i + 1)
                    dve.tensor_tensor(qk_lo[:, i % 2, :], side[:, i % 2, :], qk_hi[:, i % 2, :].bitcast(F32), ALU.subtract).then_inc(qk_lo_ready, 1)

            def value_out(b):
                if isinstance(b, int) and b == 0:
                    dve.wait_ge(v_ones_ready, 1)
                at_least(dve, pv_done, SUBS * b)
                for i in range(2):
                    dve.wait_ge(vp_done, 2 * b + i + 1)
                    for t in (2 * i, 2 * i + 1):
                        cp = dve.tensor_copy(v[:, t, :, 0:DH1], side4[:, t, :].rearrange("p (h d) -> p h d", d=DH1))
                    cp.then_inc(v_ready, 1)

            def maxima(b, h, ts):
                g, j = divmod(h, 4)
                if j == 0 and 0 in ts:
                    at_least(dve, maxT_done, 4 * (b - 1) + g + 1)
                for t in ts:
                    u = 4 * h + t
                    dve.wait_ge(s_done, 64 * b + u + 1)
                    dve.tensor_reduce(nmax[:, g, t, j:j + 1], bank_s[u % 2][:, :], AX.X, ALU.max, negate=True).then_inc(max_ready, 1)

            def shift_lo(b, g):
                dve.wait_ge(sh_hi_ready, 4 * b + g + 1)
                dve.tensor_tensor(sh_lo[:, :], bank_t[0:4, :], sh_hi[:, :].bitcast(F32), ALU.subtract).then_inc(sh_lo_ready, 1)

            def context_out(b, g):
                dve.wait_ge(ctT_done, 4 * b + g + 1)
                if g == 0:
                    at_least(dve, wo_done, b)
                tj = bank_t[:, :].rearrange("p (t j c) -> p t j c", t=NT, j=4)
                dve.reciprocal(rsum[:, :, :].rearrange("p t (j o) -> p t j o", o=1), tj[:, :, :, DH1:DH1 + 1]).then_inc(rsum_ready, 1)
                dve.wait_ge(rsum_ready, 4 * b + g + 1)
                for t in range(NT):
                    cp = dve.tensor_tensor(cx[:, t, 4 * g * DH1:4 * (g + 1) * DH1].rearrange("p (j d) -> p j d", d=DH1),
                                           tj[:, t, :, 0:DH1], over_last(rsum[:, t, :], DH1), ALU.mult)
                cp.then_inc(cx_ready, 1)

            def add_attention(b):
                dve.wait_ge(wo_done, b + 1)
                dve.wait_ge(x2_kept, b + 1)
                dve.wait_ge(stored, 16 * b + 16)
                dve.tensor_tensor(xk[:, :, :], side4, tiles(xs, b), ALU.add).then_inc(r3_ready, 1)
                stats_of(3, b, xk, (r3_ready, b + 1, False))

            def x3T_rest(b):
                dve.wait_ge(x3T_hi_ready, b + 1)
                dve.tensor_tensor(x3T_lo[:, :, :], side[:, :, :], x3T_hi[:, :, :].bitcast(F32), ALU.subtract).then_inc(x3T_lo_ready, 1)

            def hidden(b, t):
                dve.wait_ge(in_copied, NT * b + t + 1)
                dve.scalar_tensor_tensor(out=sg[:, :], in0=th[:, t % 2, :], scalar=1.0, in1=side[:, 0, 0:E1 * F1],
                                         op0=ALU.add, op1=ALU.mult).then_inc(sg_ready, 1)
                dve.wait_ge(sg_ready, NT * b + t + 1)
                dve.tensor_tensor(hid[:, t, 0:E1 * F1], side[:, 1, 0:E1 * F1], sg[:, :], ALU.mult).then_inc(hid_ready, 1)

            ROUTE_STEPS = (1, 17)

            def route_rel(b):
                step = Steps(dve, route_step, sum(ROUTE_STEPS), b)
                dve.wait_ge(in_copied, NT * (b + 1))
                step(dve.tensor_reduce(rm["max"][:, :], lg[:, :, :], AX.X, ALU.max))
                dve.tensor_tensor(rt["rel"][:, :, :], lg[:, :, :], over_last(rm["max"][:, :], E1), ALU.subtract).then_inc(rel_ready, 1)

            def route(b):
                step = Steps(dve, route_step, sum(ROUTE_STEPS), b)
                step.n = ROUTE_STEPS[0]
                dve.wait_ge(re_ready, b + 1)
                step(dve.tensor_reduce(rm["sum"][:, :], rt["e"][:, :, :], AX.X, ALU.add))
                step(dve.reciprocal(rm["rsum"][:, :], rm["sum"][:, :]))
                step(dve.tensor_tensor(rt["sc"][:, :, :], rt["e"][:, :, :], over_last(rm["rsum"][:, :], E1), ALU.mult))
                first_max(step, rt["sc"][:, :, :], rt["key1"], rt["eq1"], rt["pick1"], rm["max1"], rm["kmax1"])
                step(dve.scalar_tensor_tensor(out=rt["less"][:, :, :], in0=rt["pick1"][:, :, :], scalar=-2.0, in1=rt["sc"][:, :, :],
                                              op0=ALU.mult, op1=ALU.add))
                first_max(step, rt["less"][:, :, :], rt["key2"], rt["eq2"], rt["pick2"], rm["max2"], rm["kmax2"])
                step(dve.tensor_tensor(rt["both"][:, :, :], rt["pick1"][:, :, :], rt["pick2"][:, :, :], ALU.add))
                step(dve.tensor_tensor(rt["w"][:, :, :], rt["both"][:, :, :], rt["sc"][:, :, :], ALU.mult))
                step(dve.tensor_scalar(rt["wh"][:, :, :], rt["w"][:, :, :], 0.5, None, ALU.mult))
                dve.wait_ge(hid_ready, NT * (b + 1))
                for n0, n, w in ((0, F1, "wh"), (E1 * F1, R1, "w")):
                    for t in range(NT):
                        part = hid[:, t, n0:n0 + E1 * n].rearrange("p (e f) -> p e f", f=n)
                        mul = dve.tensor_tensor(part, part, over_last(rt[w][:, t, :], n), ALU.mult)
                    mul.then_inc(hw_ready, 1)

            def add_experts(b):
                dve.wait_ge(down_done, b + 1)
                dve.tensor_tensor(xk[:, :, :], side4, xk[:, :, :], ALU.add).then_inc(r4_ready, 1)
                stats_of(4, b, xk, (r4_ready, b + 1, False))

            def pair(b, s, ts, front):
                if s + LEAD < H1:
                    maxima(b, s + LEAD, ts)
                elif front:
                    maxima(b + 1, s + LEAD - H1, ts)

            def body(b, front, back):
                for s in range(SUBS):
                    pair(b, s, (0, 1), front)
                    if s == 0 and front:
                        normalize_x1(b + 1)
                    if s == 9 and front:
                        qk_rest(b + 1, (2, 3))
                    if s == 3 and front:
                        gate_pick(b + 1)
                    if s == 8 and front:
                        qk_rest(b + 1, (0, 1))
                    if 10 <= s < 13 and back:
                        hidden(b - 1, s - 10)
                    if s == 13 and back:
                        route(b - 1)
                    if s == 15 and back:
                        add_experts(b - 1)
                    pair(b, s, (2, 3), front)
                    if s == 0:
                        value_out(b)
                    if s == 1 and back:
                        context_out(b - 1, 3)
                    if s in (2, 6, 10):
                        shift_lo(b, s // 4 + 1)
                    if s == 14 and front:
                        shift_lo(b + 1, 0)
                    if s == 2 and front:
                        gate_scores(b + 1)
                    if s == 3 and back:
                        add_attention(b - 1)
                    if s in (5, 9, 13):
                        context_out(b, s // 4 - 1)
                    if s == 4 and back:
                        normalize(3, b - 1, xk)
                    if s == 5 and front:
                        add_update(b + 1)
                    if s == 6 and front:
                        normalize(2, b + 1, xf)
                    if s == 6 and back:
                        x3T_rest(b - 1)
                    if s == 7 and front:
                        x2T_rest(b + 1)
                    if s == 12 and back:
                        hidden(b - 1, 3)
                        route_rel(b - 1)
                    if s == 15 and back:
                        normalize(4, b - 1, xk)

            dve.wait_ge(consts_in, 16 * len(CONSTS))
            for k in range(KD):
                sel = fw[:, k, 0:E0 * (S0 + R0)].rearrange("p (m n s) -> p m n s", m=2, s=S0)
                dst = fprod[:, k, 0:E0 * (S0 + R0)].rearrange("p (m n s) -> p m n s", m=2, s=S0)
                for m in range(2):
                    pd = dve.tensor_tensor(dst[:, m], sel[:, m], over_last(md[:, k, m * E0:(m + 1) * E0], S0), ALU.mult)
                pd.then_inc(fprod_ready, 1)
            dve.scalar_tensor_tensor(out=fprod[:, :, W0 - E0:W0], in0=md[:, :, 0:E0], scalar=0.5, in1=md[:, :, 0:E0],
                                     op0=ALU.mult, op1=ALU.mult).then_inc(fprod_ready, 1)
            dve.wait_ge(rstd1_ready, 1)
            normalize_x1(0)
            dve.wait_ge(fsum_done, 1)
            dve.tensor_copy(fconst[:, :], bank_t[:, 0:W0]).then_inc(fconst_ready, 1)
            dve.wait_ge(fconst_ready, 1)
            gate_scores(0)
            gate_pick(0)
            for i, n0, n1, hi, lo in ((0, 0, KD * 3 * D, wqkv_hi, wqkv_lo), (1, KD * 3 * D, KD * (3 * D + WA + WB), win_hi, win_lo)):
                dve.wait_ge(w_hi_ready, i + 1)
                dve.tensor_tensor(lo[:, :, :].rearrange("p k n -> p (k n)"), raw[:, n0:n1],
                                  hi[:, :, :].rearrange("p k n -> p (k n)").bitcast(F32), ALU.subtract).then_inc(w_lo_ready, 1)
            add_update(0)
            normalize(2, 0, xf)
            x2T_rest(0)
            qk_rest(0, range(4))
            for h in range(LEAD):
                maxima(0, h, range(NT))
                if h == 4:
                    shift_lo(0, 0)
            body(0, True, False)
            with dve.Fori(1, B - 1) as b:
                body(b, True, True)
            body(B - 1, False, True)
            context_out(B - 1, 3)
            add_attention(B - 1)
            normalize(3, B - 1, xk)
            x3T_rest(B - 1)
            for t in range(NT):
                hidden(B - 1, t)
            route_rel(B - 1)
            route(B - 1)
            add_experts(B - 1)
            normalize(4, B - 1, xk)


def program(nc, a, out):
    with ExitStack() as ctx:
        xs = ctx.enter_context(nc.sbuf_tensor("xs", [P, B * NT, D], F32))
        stats = ctx.enter_context(nc.sbuf_tensor("stats", [P, B * NT, 2], F32))
        layer0_attention(nc, a, xs, stats)
        update_attention_experts(nc, a, xs, stats, out)


def constants():
    import numpy as np

    pick = np.zeros((P, H0), np.float32)
    part_c, part_m = np.zeros((P, 1), np.float32), np.zeros((P, 1), np.float32)
    for g in range(G0):
        for j in range(J0):
            pick[32 * g + j, J0 * g + j] = pick[32 * g + 4 + j, J0 * g + j] = 1.0
            part_c[32 * g + j], part_c[32 * g + 4 + j], part_m[32 * g + 4 + j] = 1.0, -1.0, 1.0
    return {"pick": pick, "part_c": part_c, "part_m": part_m, "ones": np.ones((P, 1), np.float32),
            "ident": np.eye(P, dtype=np.float32), "ones_pp": np.ones((P, P), np.float32),
            "rank": np.broadcast_to(np.arange(E0, 0, -1).astype(np.float32), (P, E0))}


def laid_out(i):
    import numpy as np

    def cut(w):
        return w.reshape(KD, P, -1).transpose(1, 0, 2)

    i = {k: np.asarray(v) for k, v in i.items()}
    x = i["L0_attn_hidden_states"]
    arrays = {
        "x": x,
        "xT": x.reshape(B, 2, P, 2, KD, P).transpose(5, 0, 4, 1, 3, 2).reshape(P, B, KD, T),
        "wqT0": cut(i["L0_attn_Wq"].T),
        "wkvT0": cut(np.concatenate([i["L0_attn_Wk"], i["L0_attn_Wv"]]).T).reshape(P, -1),
        "woT0": i["L0_attn_Wo"].reshape(D, H0, DH0).transpose(2, 1, 0),
        "bq": i["L0_attn_bq"].reshape(H0, DH0).T,
        "bk": np.broadcast_to(i["L0_attn_bk"], (P, 512)),
        "bv": np.broadcast_to(i["L0_attn_bv"], (P, 512)),
        "fw": cut(np.concatenate([i["L0_ffn_select_weight"].transpose(1, 0, 2).reshape(D, -1),
                                  i["L0_ffn_lora_update"].transpose(1, 0, 2).reshape(D, -1),
                                  i["L0_ffn_select_mean_diff"].T], axis=1)),
        "md": cut(np.concatenate([i["L0_ffn_select_mean_diff"].T, i["L0_ffn_debias_w"].T], axis=1)),
        "slope": np.broadcast_to(i["L0_ffn_imp_slope"], (P, E0)),
        "center": np.broadcast_to(i["L0_ffn_imp_center"], (P, E0)),
        "down0": np.concatenate([i["L0_ffn_lora_degen"].transpose(0, 2, 1).reshape(E0 * R0, D), i["L0_ffn_bias_w"]]),
        "wqkv1": cut(np.concatenate([i["L1_attn_Wq"], i["L1_attn_Wk"], i["L1_attn_Wv"]], axis=1)).reshape(P, -1),
        "wo1": i["L1_attn_Wo"].reshape(P, 2, D),
        "bo": np.broadcast_to(i["L1_attn_bo"], (P, D)),
        "win1": cut(np.concatenate([i["L1_ffn_gate_w"].reshape(-1, D), i["L1_ffn_lora_A"].reshape(-1, D),
                                    i["L1_ffn_up_w"].reshape(-1, D), i["L1_ffn_G"].T]).T).reshape(P, -1),
        "down1": np.concatenate([i["L1_ffn_down_w"].transpose(0, 2, 1).reshape(E1 * F1, D),
                                 i["L1_ffn_lora_B"].transpose(0, 2, 1).reshape(E1 * R1, D)]).reshape(3, P, D).transpose(1, 0, 2),
    }
    arrays.update(constants())
    return {k: np.ascontiguousarray(v) for k, v in arrays.items()}


def kernel(**inputs):
    import numpy as np
    import concourse.bacc as bacc
    from concourse.bass_utils import run_bass_kernel_spmd

    nc = bacc.Bacc("TRN2", target_bir_lowering=False, num_devices=1)
    arrays = laid_out(inputs)
    aps = {k: nc.dram_tensor(f"in_{k}", v.shape, F32, kind="ExternalInput").ap() for k, v in arrays.items()}
    out = nc.dram_tensor("out", (B, T, D), F32, kind="ExternalOutput").ap()
    program(nc, aps, out)
    r = run_bass_kernel_spmd(nc, [{f"in_{k}": v for k, v in arrays.items()}], core_ids=[0])
    return r.results[0]["out"]
```

```python
from contextlib import ExitStack

import concourse.bass as bass
from concourse import mybir

F32 = mybir.dt.float32
F32R = mybir.dt.float32r
ALU = mybir.AluOpType
ACT = mybir.ActivationFunctionType
AX = mybir.AxisListType

P = 128
B, T, D = 4, 512, 256
KD = D // P
NT = T // P
LN_EPS = 1e-5

H0, G0, DH0 = 16, 4, 128
J0 = H0 // G0
DEN_EPS = 1e-6
ORDER0 = [(g, j) for j in range(J0) for g in range(G0)]


E0, S0, R0 = 8, 8, 8
W0 = E0 * (S0 + R0) + E0
U0 = E0 * R0 + E0
Z_MIN = -85.0
H1, DH1 = 16, 16
SCALE1 = DH1 ** -0.5
ROWS_S = 3 * DH1
ROWS_ST = ROWS_S + 2
SUBS = 16
LEAD = 6
SLOTS = 8
E1, F1, R1 = 8, 32, 16
WA = E1 * F1 + E1 * R1
WB = E1 * F1
W1 = WA + WB + E1


def tile(x, b, t):
    return x[:, NT * b + t, :] if isinstance(b, int) else x[:, bass.ds(NT * b + t, 1), :].rearrange("p o n -> p (o n)")
RAW_SPLIT = KD * 3 * D
RAW_END = RAW_SPLIT + KD * W1


def whole(t):
    return t[tuple(slice(None) for _ in t.shape)]


def split_passes(lhs_hi, lhs_lo, rhs_hi, rhs_lo):
    return [(lhs_lo, rhs_hi), (lhs_hi, rhs_lo), (lhs_hi, rhs_hi)]


def rows(x):
    return x.rearrange("b (c p h) d -> p (b c) (h d)", p=P, h=2)


def at_least(eng, sem, value):
    if not isinstance(value, int) or value > 0:
        eng.wait_ge(sem, value)


def tiles(x, b):
    return x[:, NT * b:NT * (b + 1), :] if isinstance(b, int) else x[:, bass.ds(NT * b, NT), :]


class Steps:

    def __init__(self, eng, sem, each, b):
        self.eng, self.sem, self.base, self.n = eng, sem, each * b, 0

    def __call__(self, *instructions):
        for ins in instructions:
            self.n += 1
            ins.then_inc(self.sem, 1)
        self.eng.wait_ge(self.sem, self.base + self.n)


MERGE_STEPS = 4


def merge_stats(dve, step, bn, tmp, mean_neg, var):
    half_n = D // 2
    mean_e, m2_e, mean_o, m2_o = (bn[:, :, i:i + 1] for i in (1, 2, 4, 5))
    dist, m2, dist2 = (tmp[:, :, i:i + 1] for i in range(3))
    step(dve.tensor_tensor(dist, mean_e, mean_o, ALU.subtract),
         dve.scalar_tensor_tensor(out=m2, in0=m2_e, scalar=2 * half_n * LN_EPS, in1=m2_o, op0=ALU.add, op1=ALU.add))
    step(dve.scalar_tensor_tensor(out=mean_neg, in0=dist, scalar=0.5, in1=mean_e, op0=ALU.mult, op1=ALU.subtract),
         dve.scalar_tensor_tensor(out=dist2, in0=dist, scalar=0.25, in1=dist, op0=ALU.mult, op1=ALU.mult))
    return dve.scalar_tensor_tensor(out=var, in0=m2, scalar=1 / (2 * half_n), in1=dist2, op0=ALU.mult, op1=ALU.add)


def layer0_attention(nc, a, kept):
    with ExitStack() as ctx:
        def sb(name, shape, dt=F32):
            return ctx.enter_context(nc.sbuf_tensor(name, [P] + shape, dt))

        def ps(name):
            return ctx.enter_context(nc.psum_tensor(name, [P, 512], F32))

        def sem(name):
            return ctx.enter_context(nc.semaphore(name))

        xs, stats = kept.xs, kept.stats
        wkv_hi, wkv_lo = kept.wkv[:, 0], kept.wkv[:, 1]
        wq_hi, wq_lo = sb("wq_hi", [KD, H0 * DH0], F32R), sb("wq_lo", [KD, H0 * DH0], F32R)
        wo = sb("wo0", [H0, D])
        bq, bq1, bq_neg = sb("bq", [H0]), sb("bq1", [H0]), sb("bq_neg", [H0])
        bk, bv = sb("bk", [512]), sb("bv", [512])
        ones = sb("ones0", [1])
        part_c, part_m = sb("part_c", [1]), sb("part_m", [1])
        pick_raw, pick = sb("pick_raw", [H0]), sb("pick", [H0], F32R)
        xT = sb("xT", [KD, T])
        xT_hi, xT_lo = sb("xT_hi", [KD, T], F32R), sb("xT_lo", [KD, T], F32R)
        zk, ek = sb("zk", [2, 512]), sb("ek", [2, 512])
        sk, v = sb("sk", [NT, 512]), sb("v0", [NT, 512])
        sk_sum = sb("sk_sum", [512])
        kvT = sb("kvT", [512])
        ksel = sb("ksel", [G0, J0, 32])
        eq = sb("eq", [3, T])
        sq = sb("sq", [H0, T])
        stage = sq[:, 0:12, :].rearrange("p (s c) n -> p s (c n)", s=3)
        den, rn = sb("den", [T]), sb("rn", [T])
        rn_c, rn_parts = sb("rn_c", [T], F32R), sb("rn_parts", [2, T], F32R)
        m_hi, m_lo = sb("m_hi", [4, 2 * D], F32R), sb("m_lo", [4, 2 * D], F32R)
        s_hi, s_lo = sb("s_hi", [2, T], F32R), sb("s_lo", [2, T], F32R)
        res = sb("res", [NT, D])
        bn, bn_tmp = sb("bn0", [NT, 6]), sb("bn0_tmp", [NT, 3])

        bank_a = [ps("bank_a0"), ps("bank_a1")]
        bank_q = [ps(f"bank_q{i}") for i in range(3)]
        bank_n = ps("bank_n")
        bank_y = ctx.enter_context(nc.psum_tensor("bank_y", [P, 2, 512], F32))
        bank_y4 = bank_y[:, :, :].rearrange("p a (t n) -> p (a t) n", t=2)

        ones_in, kv_bias_in, small_in = sem("ones_in"), sem("kv_bias_in"), sem("small_in")
        wo_in, x_in, xT_in = sem("wo_in"), sem("x_in"), sem("xT_in")
        stage_in = [sem(f"stage_in{s}") for s in range(3)]
        w_hi_ready, w_lo_ready = sem("w_hi_ready"), sem("w_lo_ready")
        setup_done = sem("setup_done")
        xT_hi_ready, xT_lo_ready = sem("xT_hi_ready"), sem("xT_lo_ready")
        k_done, v_done = sem("k_done"), sem("v_done")
        zk_ready, v_ready, ek_ready = sem("zk_ready"), sem("v_ready"), sem("ek_ready")
        ek_capped, sk_ready = sem("ek_capped"), sem("sk_ready")
        sk_sum_step = sem("sk_sum_step")
        kvT_done, ksum_done, kvT_ready, ksel_ready = sem("kvT_done"), sem("ksum_done"), sem("kvT_ready"), sem("ksel_ready")
        q_done, eq_ready, eq_capped, sq_ready = sem("q_done"), sem("eq_ready"), sem("eq_capped"), sem("sq_ready")
        norm_done, den_ready, rn_ready, rn_c_ready, parts_ready = (
            sem("norm_done"), sem("den_ready"), sem("rn_ready"), sem("rn_c_ready"), sem("parts_ready"))
        m_done, m_hi_ready, m_lo_ready = sem("m_done"), sem("m_hi_ready"), sem("m_lo_ready")
        bc_done, scaled, s_hi_ready = sem("bc_done"), sem("scaled"), sem("s_hi_ready")
        s_lo_ready = [sem("s_lo_ready_even"), sem("s_lo_ready_odd")]
        y_done, res_ready, res_kept = sem("y_done"), sem("res_ready"), sem("res_kept")
        bn_ready, merge_step, stats_ready = sem("bn_ready"), sem("merge_step"), sem("stats_ready")

        W_STAGES = [("kv", None), ("q", 0), ("q", 1)]
        N_SMALL = 4
        PARTS_AT = 10
        MAP_AT = (4, 6, 14, 15)

        def w_parts(s):
            kind, k = W_STAGES[s]
            if kind == "kv":
                return wkv_hi[:, :, :].rearrange("p k n -> p (k n)"), wkv_lo[:, :, :].rearrange("p k n -> p (k n)")
            return wq_hi[:, k, :], wq_lo[:, k, :]

        block = ctx.enter_context(nc.Block())

        @block.sync
        def _(sp):
            sp.dma_start(stage[:, 0, :], a["wkvT0"]).then_inc(stage_in[0], 16)
            sp.dma_start(xT[:, :, :], a["xT"][:, 0]).then_inc(xT_in, 16)
            sp.dma_start(ones[:, :], a["ones"]).then_inc(ones_in, 16)
            for dst, name in ((bk, "bk"), (bv, "bv")):
                sp.dma_start(dst[:, :], a[name]).then_inc(kv_bias_in, 16)
            for k in range(KD):
                sp.dma_start(stage[:, 1 + k, :], a["wqT0"][:, k]).then_inc(stage_in[1 + k], 16)
            for dst, name in ((bq, "bq"), (pick_raw, "pick"), (part_c, "part_c"),
                              (part_m, "part_m")):
                sp.dma_start(dst[:, :], a[name]).then_inc(small_in, 16)
            sp.dma_start(wo[:, :, :], a["woT0"]).then_inc(wo_in, 16)
            sp.dma_start(xs[:, :, :].rearrange("p (c h) d -> p c (h d)", h=2), rows(a["x"])).then_inc(x_in, 16)
            with sp.Fori(0, B - 1) as b:
                after = sp.snap(b + 1)
                sp.wait_ge(xT_hi_ready, after)
                sp.wait_ge(xT_lo_ready, after)
                sp.dma_start(xT[:, :, :], a["xT"][:, bass.ds(after, 1)].rearrange("p o k n -> p (o k) n")).then_inc(xT_in, 16)
            for name, t in kept.consts.items():
                sp.dma_start(whole(t), a[name]).then_inc(kept.consts_in, 16)
            sp.wait_ge(v_done, NT * B)
            raw = kept.shared[:, :, :].rearrange("p s n -> p (s n)")
            for i, (name, n0, n1) in enumerate((("wqkv1", 0, RAW_SPLIT), ("win1", RAW_SPLIT, RAW_END))):
                sp.dma_start(raw[:, n0:n1], a[name]).then_inc(kept.raw_in[i], 16)

        @block.gpsimd
        def _(pool):
            pool.memset(ksel[:, :, :, :], 0.0).then_inc(setup_done, 1)

            def scaled_lo(b, n):
                pool.wait_ge(s_hi_ready, H0 * b + n + 1)
                at_least(pool, s_lo_ready[1], H0 // 2 * b + n // 2)
                pool.tensor_tensor(s_lo[:, 1, :], sq[:, n, :], s_hi[:, 1, :].bitcast(F32), ALU.subtract).then_inc(s_lo_ready[1], 1)

            def keep(b):
                pool.wait_ge(res_ready, b + 1)
                pool.wait_ge(s_lo_ready[1], H0 // 2 * (b + 1))
                pool.tensor_copy(tiles(xs, b), res[:, :, :]).then_inc(res_kept, 1)

            def sum_keys(b):
                at_least(pool, ksum_done, b)
                for t in range(1, NT):
                    pool.wait_ge(sk_ready, NT * b + t + 1)
                    at_least(pool, sk_sum_step, (NT - 1) * b + t - 1)
                    pool.tensor_tensor(sk_sum[:, :], sk[:, 0, :] if t == 1 else sk_sum[:, :], sk[:, t, :], ALU.add).then_inc(sk_sum_step, 1)

            def body(b, last):
                sum_keys(b)
                if last:
                    keep(b - 1)
                pool.wait_ge(sk_sum_step, (NT - 1) * (b + 1))
                for n in range(1, H0, 2):
                    if n == 1:
                        at_least(pool, res_kept, b)
                    scaled_lo(b, n)

            body(0, False)
            with pool.Fori(1, B) as b:
                body(b, True)
            keep(B - 1)

        @block.tensor
        def _(pe):
            def key_value(b, t):
                tok = slice(t * P, (t + 1) * P)
                for part, (bank, done) in enumerate(((bank_a[0], k_done), (bank_a[1], v_done))):
                    if t == 0:
                        at_least(pe, m_lo_ready, 8 * b)
                    else:
                        pe.wait_ge((zk_ready, v_ready)[part], NT * b + t)
                    cols = slice(part * 512, (part + 1) * 512)
                    n = 0
                    for k in range(KD):
                        for lhs, rhs in split_passes(xT_hi[:, k, tok], xT_lo[:, k, tok], wkv_hi[:, k, cols], wkv_lo[:, k, cols]):
                            mm = pe.matmul(bank[:, :], lhs, rhs, start=n == 0, stop=n == 3 * KD - 1)
                            n += 1
                    mm.then_inc(done, 1)

            def state(b):
                pe.wait_ge(ones_in, 16)
                pe.wait_ge(v_ready, NT * b + NT)
                pe.wait_ge(sk_ready, NT * b + NT)
                for g in range(G0):
                    hd = slice(g * DH0, (g + 1) * DH0)
                    for t in range(NT):
                        mm = pe.matmul(bank_a[0][:, hd], v[:, t, hd], sk[:, t, hd], start=t == 0, stop=t == NT - 1)
                mm.then_inc(kvT_done, 1)
                pe.wait_ge(sk_sum_step, (NT - 1) * (b + 1))
                for g in range(G0):
                    mm = pe.matmul(bank_a[1][:, g:g + 1], sk_sum[:, g * DH0:(g + 1) * DH0], ones[:, :], start=True, stop=True)
                mm.then_inc(ksum_done, 1)

            def query(b, n):
                g, j = ORDER0[n]
                hd = slice((J0 * g + j) * DH0, (J0 * g + j + 1) * DH0)
                if n < 3:
                    at_least(pe, scaled, H0 * b)
                else:
                    pe.wait_ge(sq_ready, H0 * b + n - 2)
                i = 0
                for k in range(KD):
                    for lhs, rhs in split_passes(wq_hi[:, k, hd], wq_lo[:, k, hd], xT_hi[:, k, :], xT_lo[:, k, :]):
                        mm = pe.matmul(bank_q[n % 3][:, :], lhs, rhs, start=i == 0, stop=i == 3 * KD - 1)
                        i += 1
                mm.then_inc(q_done, 1)

            def norm(b, j):
                if j == 0:
                    pe.wait_ge(ksel_ready, b + 1)
                if j % 2 == 0:
                    at_least(pe, den_ready, 2 * b + j // 2)
                pe.wait_ge(sq_ready, H0 * b + G0 * (j + 1))
                for g in range(G0):
                    mm = pe.matmul(bank_n[32 * g:32 * g + 32, :], ksel[:, g, j, :], sq[:, G0 * j + g, :],
                                   start=j % 2 == 0, stop=j % 2 == 1)
                if j % 2 == 1:
                    mm.then_inc(norm_done, 1)

            def output_map(b, p):
                if p == 0:
                    pe.wait_ge(kvT_ready, b + 1)
                elif p == 1:
                    pe.wait_ge(ksel_ready, b + 1)
                else:
                    pe.wait_ge(m_lo_ready, 8 * b + p - 1)
                for i in range(2):
                    g, j = ORDER0[2 * p + i]
                    mm = pe.matmul(bank_a[p % 2][:, i * D:(i + 1) * D], kvT[:, g * DH0:(g + 1) * DH0], wo[:, J0 * g + j, :],
                                   start=True, stop=True)
                mm.then_inc(m_done, 1)

            def factor(b, n):
                g, j = ORDER0[n]
                h = J0 * g + j
                if n % (H0 // 2) == 0:
                    pe.wait_ge(parts_ready, 2 * b + n // (H0 // 2) + 1)
                if n < 3:
                    pe.wait_ge(sq_ready, H0 * b + H0 + n - 2)
                else:
                    pe.wait_ge(scaled, H0 * b + n - 2)
                pe.matmul(bank_q[(H0 + n) % 3][:, :], pick[:, h:h + 1].broadcast_to([P, P]), rn_parts[:, n // (H0 // 2), :],
                          start=True, stop=True).then_inc(bc_done, 1)

            def project(b, n):
                if n == 0:
                    at_least(pe, res_ready, b)
                pe.wait_ge(s_hi_ready, H0 * b + n + 1)
                pe.wait_ge(s_lo_ready[n % 2], H0 // 2 * b + n // 2 + 1)
                if n % 2 == 0:
                    pe.wait_ge(m_lo_ready, 8 * b + n // 2 + 1)
                m = (n // 2) % 4
                cols = slice((n % 2) * D, (n % 2 + 1) * D)
                for t in range(NT):
                    tok = slice(t * P, (t + 1) * P)
                    for i, (lhs, rhs) in enumerate(split_passes(s_hi[:, n % 2, tok], s_lo[:, n % 2, tok], m_hi[:, m, cols], m_lo[:, m, cols])):
                        mm = pe.matmul(bank_y4[:, t, :], lhs, rhs,
                                       start=n == 0 and i == 0 and t % 2 == 0, stop=n == H0 - 1 and i == 2,
                                       skip_group_check=True)
                mm.then_inc(y_done, 1)

            pe.wait_ge(w_lo_ready, 1)
            pe.wait_ge(w_hi_ready, 1)

            def body(b, first):
                pe.wait_ge(xT_hi_ready, b + 1)
                pe.wait_ge(xT_lo_ready, b + 1)
                for t in range(NT):
                    key_value(b, t)
                if first:
                    state(b)
                    pe.wait_ge(w_hi_ready, len(W_STAGES))
                    pe.wait_ge(w_lo_ready, len(W_STAGES))
                for n in range(3):
                    query(b, n)
                if not first:
                    state(b)
                pe.wait_ge(wo_in, 16)
                for n in range(3, H0):
                    query(b, n)
                    if n in MAP_AT:
                        output_map(b, MAP_AT.index(n))
                    if n % G0 == 1 and n > G0:
                        norm(b, n // G0 - 1)
                pe.wait_ge(setup_done, 4)
                factor(b, 0)
                factor(b, 1)
                norm(b, J0 - 1)
                for n in range(H0):
                    if n + 2 < H0:
                        factor(b, n + 2)
                    project(b, n)
                    if n % 2 == 1 and n < 8:
                        output_map(b, 4 + n // 2)

            body(0, True)
            with pe.Fori(1, B) as b:
                body(b, False)

        @block.scalar
        def _(act):
            def split_x(b):
                act.wait_ge(xT_in, 16 * (b + 1))
                at_least(act, q_done, H0 * b)
                act.activation(xT_hi[:, :, :], xT[:, :, :], ACT.Copy).then_inc(xT_hi_ready, 1)

            def map_hi(b, p):
                act.wait_ge(m_done, 8 * b + p + 1)
                at_least(act, y_done, H0 * b + max(0, 2 * (p - 4) + 2))
                act.activation(m_hi[:, p % 4, :], bank_a[p % 2][:, :], ACT.Copy).then_inc(m_hi_ready, 1)

            def factor_hi(b, half_):
                act.wait_ge(rn_ready, 2 * (2 * b + half_ + 1))
                at_least(act, parts_ready, 2 * b + half_)
                act.activation(rn_c[:, :], rn[:, :], ACT.Copy, scale=part_c[:, 0:1]).then_inc(rn_c_ready, 1)

            def query_exp(b, n):
                g, j = ORDER0[n]
                h = J0 * g + j
                act.wait_ge(q_done, H0 * b + n + 1)
                at_least(act, sq_ready, H0 * b + max(0, n - 2))
                act.activation(eq[:, n % 3, :], bank_q[n % 3][:, :], ACT.Relu, bias=bq_neg[:, h:h + 1], scale=-1.0).then_inc(eq_capped, 1)
                act.wait_ge(eq_capped, H0 * b + n + 1)
                act.activation(eq[:, n % 3, :], eq[:, n % 3, :], ACT.Exp, scale=-1.0).then_inc(eq_ready, 1)

            def split_weights(s):
                act.wait_ge(stage_in[s], 16)
                act.activation(w_parts(s)[0], stage[:, s, :], ACT.Copy).then_inc(w_hi_ready, 1)

            def set_up():
                act.wait_ge(small_in, 16 * N_SMALL)
                act.activation(bq1[:, :], bq[:, :], ACT.Copy, bias=1.0).then_inc(setup_done, 1)
                act.activation(bq_neg[:, :], bq[:, :], ACT.Copy, scale=-1.0).then_inc(setup_done, 1)
                act.activation(pick[:, :], pick_raw[:, :], ACT.Copy).then_inc(setup_done, 1)
                act.wait_ge(setup_done, 4)

            def body(b, first, more):
                for t in range(NT):
                    act.wait_ge(zk_ready, NT * b + t + 1)
                    at_least(act, sk_ready, NT * b + max(0, t - 1))
                    act.activation(ek[:, t % 2, :], zk[:, t % 2, :], ACT.Relu, scale=-1.0).then_inc(ek_capped, 1)
                    act.wait_ge(ek_capped, NT * b + t + 1)
                    act.activation(ek[:, t % 2, :], ek[:, t % 2, :], ACT.Exp, scale=-1.0).then_inc(ek_ready, 1)
                    if first and t > 1:
                        split_weights(t - 1)
                if first:
                    set_up()
                for n in range(3):
                    query_exp(b, n)
                act.wait_ge(kvT_done, b + 1)
                at_least(act, m_done, 8 * b)
                act.activation(kvT[:, :], bank_a[0][:, :], ACT.Copy).then_inc(kvT_ready, 1)
                for n in range(3, H0):
                    query_exp(b, n)
                    if n in MAP_AT:
                        map_hi(b, MAP_AT.index(n))
                    if n == PARTS_AT + 3:
                        factor_hi(b, 0)
                for n in range(H0):
                    if n == 4:
                        factor_hi(b, 1)
                    act.wait_ge(scaled, H0 * b + n + 1)
                    at_least(act, y_done, H0 * b + max(0, n - 1))
                    act.activation(s_hi[:, n % 2, :], sq[:, n, :], ACT.Copy).then_inc(s_hi_ready, 1)
                    if n in (3, 5, 7, 9):
                        map_hi(b, 4 + (n - 3) // 2)
                    if n == 10 and more:
                        split_x(b + 1)

            split_weights(0)
            split_x(0)
            body(0, True, True)
            with act.Fori(1, B - 1) as b:
                body(b, False, True)
            body(B - 1, False, False)

        @block.vector
        def _(dve):
            def split_x(b):
                dve.wait_ge(xT_hi_ready, b + 1)
                at_least(dve, q_done, H0 * b)
                dve.tensor_tensor(xT_lo[:, :, :], xT[:, :, :], xT_hi[:, :, :].bitcast(F32), ALU.subtract).then_inc(xT_lo_ready, 1)

            def finish_key(b, t):
                dve.wait_ge(ek_ready, NT * b + t + 1)
                dve.scalar_tensor_tensor(out=sk[:, t, :], in0=zk[:, t % 2, :], scalar=1.0, in1=ek[:, t % 2, :],
                                         op0=ALU.add, op1=ALU.max).then_inc(sk_ready, 1)

            def split_weights(s):
                dve.wait_ge(w_hi_ready, s + 1)
                hi, lo = w_parts(s)
                dve.tensor_tensor(lo, stage[:, s, :], hi.bitcast(F32), ALU.subtract).then_inc(w_lo_ready, 1)

            def key_value(b, last):
                for t in range(NT):
                    if t == 0:
                        at_least(dve, ksum_done, b)
                    else:
                        at_least(dve, sk_ready, NT * b + max(0, t - 1))
                    dve.wait_ge(k_done, NT * b + t + 1)
                    dve.tensor_tensor(zk[:, t % 2, :], bank_a[0][:, :], bk[:, :], ALU.add).then_inc(zk_ready, 1)
                    dve.wait_ge(v_done, NT * b + t + 1)
                    dve.tensor_tensor(v[:, t, :], bank_a[1][:, :], bv[:, :], ALU.add).then_inc(v_ready, 1)
                    if t > 0:
                        finish_key(b, t - 1)
                    if t == 1 and last:
                        residual(b - 1)
                    if t == 3 and not last:
                        split_weights(1)
                finish_key(b, NT - 1)

            def query(b, n):
                g, j = ORDER0[n]
                h = J0 * g + j
                dve.wait_ge(eq_ready, H0 * b + n + 1)
                dve.scalar_tensor_tensor(out=sq[:, n, :], in0=bank_q[n % 3][:, :], scalar=bq1[:, h:h + 1], in1=eq[:, n % 3, :],
                                         op0=ALU.add, op1=ALU.max).then_inc(sq_ready, 1)

            def map_lo(b, p):
                dve.wait_ge(m_hi_ready, 8 * b + p + 1)
                dve.tensor_tensor(m_lo[:, p % 4, :], bank_a[p % 2][:, :], m_hi[:, p % 4, :].bitcast(F32), ALU.subtract).then_inc(m_lo_ready, 1)

            def scaled_lo(b, n):
                dve.wait_ge(s_hi_ready, H0 * b + n + 1)
                dve.wait_ge(scaled, H0 * b + n + 1)
                dve.tensor_tensor(s_lo[:, 0, :], sq[:, n, :], s_hi[:, 0, :].bitcast(F32), ALU.subtract).then_inc(s_lo_ready[0], 1)

            def invert(b, half_):
                dve.wait_ge(norm_done, 2 * b + half_ + 1)
                dve.tensor_scalar(den[:, :], bank_n[:, :], DEN_EPS, None, ALU.add).then_inc(den_ready, 1)

            def invert_tokens(b, half_, i):
                dve.wait_ge(den_ready, 2 * b + half_ + 1)
                tok = slice(i * T // 2, (i + 1) * T // 2)
                dve.reciprocal(rn[:, tok], den[:, tok]).then_inc(rn_ready, 1)

            def parts(b, half_):
                dve.wait_ge(rn_c_ready, 2 * b + half_ + 1)
                at_least(dve, bc_done, H0 * b)
                dve.scalar_tensor_tensor(out=rn_parts[:, half_, :], in0=rn[:, :], scalar=part_m[:, 0:1], in1=rn_c[:, :].bitcast(F32),
                                         op0=ALU.mult, op1=ALU.add).then_inc(parts_ready, 1)

            def residual(b):
                dve.wait_ge(y_done, H0 * (b + 1))
                at_least(dve, res_kept, b)
                dve.wait_ge(x_in, 16)
                dve.tensor_tensor(res[:, :, :], bank_y4, tiles(xs, b), ALU.add).then_inc(res_ready, 1)

            def residual_stats(b):
                dve.wait_ge(res_ready, b + 1)
                for t in range(NT):
                    dve.bn_stats(bn[:, t, :], res[:, t, :]).then_inc(bn_ready, 1)
                dve.wait_ge(bn_ready, NT * (b + 1))
                merge_stats(dve, Steps(dve, merge_step, MERGE_STEPS, b), bn, bn_tmp,
                            tiles(stats, b)[:, :, 0:1], tiles(stats, b)[:, :, 1:2]).then_inc(stats_ready, 1)

            def body(b, last, more):
                key_value(b, last)
                if not last:
                    split_weights(2)
                    dve.wait_ge(setup_done, 4)
                    dve.wait_ge(small_in, 16 * N_SMALL)
                at_least(dve, s_hi_ready, H0 * b)
                for i in range(2):
                    at_least(dve, s_lo_ready[i], H0 // 2 * b)
                for n in range(3):
                    query(b, n)
                dve.wait_ge(ksum_done, b + 1)
                at_least(dve, norm_done, 2 * b)
                for g in range(G0):
                    dst = ksel[:, g, :, :].rearrange("p j c -> p (j c)")
                    for r in range(2):
                        cp = dve.tensor_copy(dst[:, 4 * r:4 * r + 3 * 33 + 1:33], bank_a[1][:, g:g + 1].broadcast_to([P, J0]))
                cp.then_inc(ksel_ready, 1)
                for n in range(3, H0):
                    query(b, n)
                    if n == 7 and last:
                        residual_stats(b - 1)
                    if n == PARTS_AT:
                        invert(b, 0)
                    if n in (PARTS_AT, PARTS_AT + 1):
                        invert_tokens(b, 0, n - PARTS_AT)
                    if n == PARTS_AT + 4:
                        parts(b, 0)
                    if n in MAP_AT:
                        map_lo(b, MAP_AT.index(n))
                for n in range(H0):
                    dve.wait_ge(bc_done, H0 * b + n + 1)
                    dve.tensor_tensor(sq[:, n, :], sq[:, n, :], bank_q[(H0 + n) % 3][:, :], ALU.mult).then_inc(scaled, 1)
                    if n % 2 == 1:
                        scaled_lo(b, n - 1)
                    if n == 0:
                        invert(b, 1)
                    if n in (1, 2):
                        invert_tokens(b, 1, n - 1)
                    if n == 5:
                        parts(b, 1)
                    if n in (4, 6, 8, 10):
                        map_lo(b, 4 + (n - 4) // 2)
                    if n == 12 and more:
                        split_x(b + 1)

            split_weights(0)
            split_x(0)
            dve.wait_ge(kv_bias_in, 32)
            body(0, False, True)
            with dve.Fori(1, B - 1) as b:
                body(b, True, True)
            body(B - 1, True, False)
            residual(B - 1)
            residual_stats(B - 1)


def by_tile(x):
    return x[:, :].rearrange("p (t o) -> p t o", o=1)


def over_last(x, n):
    return x.rearrange("p (a o) -> p a o", o=1).broadcast_to([x.shape[0], x.shape[1], n])


def over_tiles(x):
    return x.rearrange("p (o n) -> p o n", o=1).broadcast_to([P, NT, x.shape[1]])


def update_attention_experts(nc, a, kept, out):
    with ExitStack() as ctx:
        def sb(name, shape, dt=F32, parts=P):
            return ctx.enter_context(nc.sbuf_tensor(name, [parts] + shape, dt))

        def sem(name):
            return ctx.enter_context(nc.semaphore(name))

        xs, stats = kept.xs, kept.stats
        ident, ones, fw, md, slope, center, rank = kept.consts.values()
        fprod, fconst = sb("fprod", [KD, W0]), sb("fconst", [W0])
        down0 = sb("down0", [D], parts=U0)
        wqkv_hi, wqkv_lo = sb("wqkv_hi", [KD, 3 * D], F32R), sb("wqkv_lo", [KD, 3 * D], F32R)
        wo, bo = sb("wo1", [2, D]), sb("bo", [D])
        win_hi, win_lo = sb("win_hi", [KD, W1], F32R), sb("win_lo", [KD, W1], F32R)
        down1 = sb("down1", [3, D])
        half = sb("half", [B * NT])
        ones_row, ones_row_ready = sb("ones_row", [P], F32R, parts=2), sem("ones_row_ready")
        rstd1 = sb("rstd1", [B * NT])
        xf = sb("xf", [NT, D])
        ssq = sb("ssq", [NT])
        pr, pr2 = sb("pr", [NT, W0]), sb("pr2", [NT, E0 * S0])
        gt = {n: sb(f"gt_{n}", [NT, E0]) for n in (
            "score", "dist", "rdist", "rel", "cent", "z", "zc", "e", "e1", "gate", "eq", "key", "pick")}
        gmax, kmax, keep = sb("gmax", [NT]), sb("kmax", [NT]), sb("keep", [NT])
        hm = sb("hm", [NT, U0])
        hmT = sb("hmT", [T], parts=U0)
        x2T_hi, x2T_lo = sb("x2T_hi", [KD, T], F32R), sb("x2T_lo", [KD, T], F32R)
        qk_hi, qk_lo = sb("qk_hi", [2, T], F32R), sb("qk_lo", [2, T], F32R)
        qs, ks = sb("qs", [H1, T], F32R, parts=64), sb("ks", [H1, T], F32R, parts=64)
        v = sb("v1", [NT, H1, 32])
        nmax = sb("nmax", [4, NT, 4])
        nmax_parts = sb("nmax_parts", [NT, 8], F32R)
        sh = sb("sh", [T], F32R, parts=8)
        probs = kept.shared
        raw = probs[:, :, :].rearrange("p s n -> p (s n)")
        ctT, rsum, cx = sb("ctT", [T]), sb("rsum", [NT, 4]), sb("cx", [NT, D])
        xk = sb("xk", [NT, D])
        x3T_hi, x3T_lo = sb("x3T_hi", [KD, T], F32R), sb("x3T_lo", [KD, T], F32R)
        th, sg, uw = sb("th", [2, E1 * F1]), sb("sg", [E1 * F1]), sb("uw", [E1 * F1])
        hid = sb("hid", [NT, 3 * P])
        turned = sb("turned", [3, T])
        hidT, x1T = turned, turned[:, 0:KD, :]
        lgT = turned[0:E1, KD, :]
        squared = turned[:, KD, :].bitcast(mybir.dt.bfloat16).rearrange("p (t d) -> p t d", t=NT)
        rt = {n: sb(f"rt_{n}", [NT, E1]) for n in (
            "rel", "e", "sc", "eq1", "key1", "pick1", "less", "eq2", "key2", "pick2", "both", "w", "wh")}
        rm = {n: sb(f"rm_{n}", [NT]) for n in ("max", "sum", "rsum", "max1", "kmax1", "max2", "kmax2")}
        ln = {i: {"bn": sb(f"ln{i}_bn", [NT, 6]), "tmp": sb(f"ln{i}_tmp", [NT, 3]), "mean_neg": sb(f"ln{i}_mean_neg", [NT]), "shift": sb(f"ln{i}_shift", [NT]), "var": sb(f"ln{i}_var", [NT]),
                  "rstd": sb(f"ln{i}_rstd", [NT])} for i in (2, 3, 4)}
        scratch = nc.dram_tensor("scratch_qk", (4, 2, DH1, P // DH1, T), F32, kind="Internal").ap()

        side = ctx.enter_context(nc.psum_tensor("side", [P, 2, 512], F32))
        side4 = side[:, :, :].rearrange("p a (t n) -> p (a t) n", t=2)
        bank_s = [ctx.enter_context(nc.psum_tensor(f"bank_s{i}", [P, 512], F32)) for i in range(2)]
        bank_st = [ctx.enter_context(nc.psum_tensor(f"bank_st{i}", [P, 512], F32)) for i in range(2)]
        bank_c = ctx.enter_context(nc.psum_tensor("bank_c", [P, 512], F32))
        bank_t = ctx.enter_context(nc.psum_tensor("bank_t", [P, 512], F32))

        side_banks = (side[:, 0, :], side[:, 1, :])
        last_banks = (side_banks, (bank_s[0], bank_s[1]), (bank_st[0], bank_st[1]), (bank_c, bank_t))

        tile_banks = tuple(bank[:, 0:D] for bank in bank_s + bank_st)
        side_tiles = tuple(side4[:, t, :] for t in range(NT))

        consts_in, raw_in = sem("consts_in"), kept.raw_in
        w_hi_ready, w_lo_ready = sem("w1_hi_ready"), sem("w1_lo_ready")
        half_ready, zeros_ready, v_ones_ready, k_ones_in = sem("half_ready"), sem("zeros_ready"), sem("v_ones_ready"), sem("k_ones_in")
        fprod_ready, fsum_done, fconst_ready = sem("fprod_ready"), sem("fsum_done"), sem("fconst_ready")
        rstd1_ready, x1_ready = sem("rstd1_ready"), sem("x1_ready")
        x1T_done, x1T_ready, ssq_ready = sem("x1T_done"), sem("x1T_ready"), sem("ssq_ready")
        pr_done, pr_ready, gate_step, zc_ready, ge_ready, gate_ready, hm_ready = (
            sem("pr_done"), sem("pr_ready"), sem("gate_step"), sem("zc_ready"), sem("ge_ready"), sem("gate_ready"), sem("hm_ready"))
        hmT_done, hmT_ready, up_done, r2_ready = sem("hmT_done"), sem("hmT_ready"), sem("up_done"), sem("r2_ready")
        bn_ready, merge_step, var_ready, rstd_ready, shift_ready, x_ready = (
            {i: sem(f"ln{i}_{n}_ready") for i in (2, 3, 4)} for n in ("bn", "merge", "var", "rstd", "shift", "x"))
        x2T_done, x2T_hi_ready, x2T_lo_ready, x2_kept = sem("x2T_done"), sem("x2T_hi_ready"), sem("x2T_lo_ready"), sem("x2_kept")
        qk_done, qk_hi_ready, qk_lo_ready = sem("qk_done"), sem("qk_hi_ready"), sem("qk_lo_ready")
        scratch_out = [sem("scratch_out0"), sem("scratch_out1")]
        stack_in = [sem("stack_in0"), sem("stack_in1")]
        vp_done, v_ready = sem("vp_done"), sem("v1_ready")
        s_done, max_ready = sem("s_done"), sem("max_ready")
        nmax_hi_ready, nmax_lo_ready = sem("nmax_hi_ready"), sem("nmax_lo_ready")
        maxT_done, sh_ready, shift_in = sem("maxT_done"), sem("sh_ready"), sem("shift_in")
        st_done, p_ready, pv_done = sem("st_done"), sem("p_ready"), sem("pv_done")
        ct_ready, ctT_done, rsum_ready, cx_ready = sem("ct_ready"), sem("ctT_done"), sem("rsum_ready"), sem("cx_ready")
        wo_done, r3_ready = sem("wo_done"), sem("r3_ready")
        x3T_done, x3T_hi_ready, x3T_lo_ready = sem("x3T_done"), sem("x3T_hi_ready"), sem("x3T_lo_ready")
        in_done, th_ready, uw_ready, sg_ready, hid_ready = sem("in_done"), sem("th_ready"), sem("uw_ready"), sem("sg_ready"), sem("hid_ready")
        lgT_done, lgT_ready, lg_done = sem("lgT_done"), sem("lgT_ready"), sem("lg_done")
        route_step, rel_ready, re_ready, w_ready = sem("route_step"), sem("rel_ready"), sem("re_ready"), sem("w_ready")
        hidT_done, hidT_ready, down_done, r4_ready, stored = (
            sem("hidT_done"), sem("hidT_ready"), sem("down_done"), sem("r4_ready"), sem("stored"))

        CONSTS = [(down0, "down0"), (bo, "bo"), (wo, "wo1")]
        block = ctx.enter_context(nc.Block())

        @block.sync
        def _(sp):
            def save_qk(b, half_):
                for i in (2 * half_, 2 * half_ + 1):
                    for part, (src, ready) in enumerate(((qk_hi, qk_hi_ready), (qk_lo, qk_lo_ready))):
                        sp.wait_ge(ready, 4 * b + i + 1)
                        sp.dma_start(scratch[i, part].rearrange("p h n -> h p n"), src[:, i % 2, :].bitcast(F32)).then_inc(scratch_out[i % 2], 16)

            def load_stack(b, half_):
                heads = slice(8 * half_, 8 * half_ + 8)
                for stack, i, pair_rows, single_rows in ((qs, 2 * half_, 0, 2 * DH1), (ks, 2 * half_ + 1, DH1, 0)):
                    sp.wait_ge(scratch_out[i % 2], 64 * b + 32 * (half_ + 1))
                    sp.dma_start(stack[pair_rows:pair_rows + 2 * DH1, heads, :].bitcast(F32),
                                 scratch[i].rearrange("a p h n -> (a p) h n")).then_inc(stack_in[half_], 16)
                    sp.dma_start(stack[single_rows:single_rows + DH1, heads, :].bitcast(F32), scratch[i, 0]).then_inc(stack_in[half_], 16)

            def shift(b, g):
                sp.wait_ge(sh_ready, 4 * b + g + 1)
                for i in range(2):
                    sp.dma_start(qs[ROWS_S + i:ROWS_S + i + 1, 4 * g:4 * g + 4, :].bitcast(F32), sh[4 * i:4 * i + 4, :].bitcast(F32)).then_inc(shift_in, 16)

            def store(b):
                sp.wait_ge(x_ready[4], NT * (b + 1))
                dst = out.rearrange("b (c p h) d -> b p c (h d)", p=P, h=2)
                dst = dst[b] if isinstance(b, int) else dst[bass.ds(b, 1)].rearrange("o p c n -> (o p) c n")
                sp.dma_start(dst, xk[:, :, :].rearrange("p (c h) d -> p c (h d)", h=2)).then_inc(stored, 16)

            def body(b, front, back):
                load_stack(b, 1)
                shift(b, 1)
                shift(b, 2)
                if front:
                    save_qk(b + 1, 0)
                    load_stack(b + 1, 0)
                    save_qk(b + 1, 1)
                shift(b, 3)
                if front:
                    shift(b + 1, 0)
                if back:
                    store(b - 1)
                else:
                    sp.wait_ge(st_done, 64 * (b + 1))

            for dst, name in CONSTS:
                sp.dma_start(whole(dst), a[name]).then_inc(consts_in, 16)
            sp.dma_start(down1[:, :, :], a["down1"]).then_inc(stored, 16)
            sp.wait_ge(ones_row_ready, 1)
            sp.dma_start(ks[ROWS_S:ROWS_ST, :, :].rearrange("p h (c m) -> p (h c) m", m=P).bitcast(F32),
                         ones_row[:, :].rearrange("p (o m) -> p o m", o=1).broadcast_to([2, H1 * NT, P]).bitcast(F32)).then_inc(k_ones_in, 16)
            save_qk(0, 0)
            load_stack(0, 0)
            save_qk(0, 1)
            shift(0, 0)
            body(0, True, False)
            with sp.Fori(1, B - 1) as b:
                body(b, True, True)
            body(B - 1, False, True)
            for c in range(2):
                sp.wait_ge(x_ready[4], NT * (B - 1) + 2 * (c + 1))
                sp.dma_start(out[B - 1, c * 2 * P:(c + 1) * 2 * P].rearrange("(p h) d -> p (h d)", h=2),
                             xk[:, 2 * c:2 * c + 2, :].rearrange("p h d -> p (h d)")).then_inc(stored, 16)
            sp.wait_ge(stored, 16 * (B + 2))

        @block.gpsimd
        def _(pool):
            def rstd(i, b):
                pool.wait_ge(var_ready[i], b + 1)
                pool.tensor_tensor(ln[i]["rstd"][:, :], ln[i]["var"][:, :], half[:, 0:NT], ALU.pow).then_inc(rstd_ready[i], 1)
                pool.wait_ge(rstd_ready[i], b + 1)
                pool.tensor_tensor(ln[i]["shift"][:, :], ln[i]["mean_neg"][:, :], ln[i]["rstd"][:, :], ALU.mult).then_inc(shift_ready[i], 1)

            def hidden_update(b):
                pool.wait_ge(gate_ready, b + 1)
                for t in range(NT):
                    pool.tensor_tensor(hm[:, t, 0:E0 * R0].rearrange("p (n r) -> p n r", r=R0),
                                       pr[:, t, E0 * S0:E0 * (S0 + R0)].rearrange("p (n r) -> p n r", r=R0),
                                       over_last(hm[:, t, E0 * R0:U0], R0), ALU.mult).then_inc(hm_ready, 1)

            def keep_x2(b):
                pool.wait_ge(x2T_done, b + 1)
                pool.tensor_tensor(tiles(xs, b), xf[:, :, :], over_tiles(bo[:, :]), ALU.add).then_inc(x2_kept, 1)

            def body(b, front, back):
                if front:
                    hidden_update(b + 1)
                if back:
                    rstd(3, b - 1)
                if front:
                    rstd(2, b + 1)
                    keep_x2(b + 1)
                if back:
                    rstd(4, b - 1)

            pool.memset(half[:, :], -0.5).then_inc(half_ready, 1)
            pool.wait_ge(half_ready, 1)
            for i, part in enumerate((slice(0, NT), slice(NT, B * NT))):
                pool.tensor_tensor(rstd1[:, part].rearrange("p (t o) -> p t o", o=1), stats[:, part, 1:2],
                                   half[:, part].rearrange("p (t o) -> p t o", o=1), ALU.pow).then_inc(rstd1_ready, 1)
                pool.wait_ge(rstd1_ready, i + 1)
            pool.memset(v[:, :, :, :], 0.0).then_inc(zeros_ready, 1)
            pool.wait_ge(zeros_ready, 1)
            pool.memset(v[:, :, :, DH1:DH1 + 1], 1.0).then_inc(v_ones_ready, 1)
            pool.wait_ge(v_ones_ready, 1)
            hidden_update(0)
            pool.wait_ge(consts_in, 16 * len(CONSTS))
            rstd(2, 0)
            keep_x2(0)
            body(0, True, False)
            with pool.Fori(1, B - 1) as b:
                body(b, True, True)
            body(B - 1, False, True)
            rstd(3, B - 1)
            rstd(4, B - 1)

        @block.tensor
        def _(pe):

            def turn(src, done, ready, b, after):
                for t in range(NT):
                    pe.wait_ge(ready, NT * b + t + 1)
                    if t == 0:
                        at_least(pe, *after)
                    for k in range(KD):
                        mm = pe.transpose(side[:, k, t * P:(t + 1) * P], src[:, t, k * P:(k + 1) * P], ident[:, :])
                mm.then_inc(done, 1)

            def turn_x1(b, after):
                turn(xf, x1T_done, x1_ready, b, after)

            def select(b):
                pe.wait_ge(x1T_ready, b + 1)
                for t in range(NT):
                    for k in range(KD):
                        mm = pe.matmul(side4[:, t, 0:W0], x1T[:, k, t * P:(t + 1) * P], fw[:, k, :], start=k == 0, stop=k == KD - 1)
                mm.then_inc(pr_done, 1)

            def turn_hm(b, after):
                pe.wait_ge(hm_ready, NT * (b + 1))
                at_least(pe, *after)
                for t in range(NT):
                    mm = pe.transpose(side[0:U0, 0, t * P:(t + 1) * P], hm[:, t, :], ident[:, :])
                mm.then_inc(hmT_done, 1)

            def update(b, after, to=side_tiles):
                at_least(pe, *after)
                pe.wait_ge(hmT_ready, b + 1)
                for t in range(NT):
                    pe.matmul(to[t], hmT[:, t * P:(t + 1) * P], down0[:, :], start=True, stop=True).then_inc(up_done, 1)

            def turn_x2(b, after):
                turn(xf, x2T_done, x_ready[2], b, after)

            def query_key(b, parts):
                if 0 in parts:
                    pe.wait_ge(x2T_hi_ready, b + 1)
                    pe.wait_ge(x2T_lo_ready, b + 1)
                for i in parts:
                    if i >= 2:
                        pe.wait_ge(qk_lo_ready, 4 * b + i - 1)
                    first = (i % 2) * D + (i // 2) * P
                    cols = slice(first, first + P)
                    n = 0
                    for k in range(KD):
                        for lhs, rhs in split_passes(wqkv_hi[:, k, cols], wqkv_lo[:, k, cols], x2T_hi[:, k, :], x2T_lo[:, k, :]):
                            mm = pe.matmul(side[:, i % 2, :], lhs, rhs, start=n == 0, stop=n == 3 * KD - 1)
                            n += 1
                    mm.then_inc(qk_done, 1)

            def value(b, banks):
                for i in banks:
                    for t in (2 * i, 2 * i + 1):
                        tok = slice(t * P, (t + 1) * P)
                        n = 0
                        for k in range(KD):
                            for lhs, rhs in split_passes(x2T_hi[:, k, tok], x2T_lo[:, k, tok], wqkv_hi[:, k, 2 * D:], wqkv_lo[:, k, 2 * D:]):
                                mm = pe.matmul(side4[:, t, :], lhs, rhs, start=n == 0, stop=n == 3 * KD - 1)
                                n += 1
                    mm.then_inc(vp_done, 1)

            def score(b, h, t):
                if h % 8 == 0 and t == 0:
                    pe.wait_ge(stack_in[h // 8], 64 * (b + 1))
                u = 4 * h + t
                at_least(pe, max_ready, 64 * b + u - 1)
                pe.matmul(bank_s[u % 2][:, :], qs[0:ROWS_S, h, t * P:(t + 1) * P], ks[0:ROWS_S, h, :],
                          start=True, stop=True).then_inc(s_done, 1)

            def turn_max(b, g, after):
                pe.wait_ge(nmax_lo_ready, 4 * b + g + 1)
                at_least(pe, *after)
                for t in range(NT):
                    mm = pe.transpose(bank_t[0:8, t * P:(t + 1) * P], nmax_parts[:, t, :].bitcast(F32), ident[:, :])
                mm.then_inc(maxT_done, 1)

            def turned_score(b, s, j):
                g, kt = divmod(s, 4)
                if kt == 0 and j == 0:
                    pe.wait_ge(shift_in, 32 * (4 * b + g + 1))
                h, u = 4 * g + j, 4 * s + j
                at_least(pe, p_ready, 64 * b + u - 1)
                pe.matmul(bank_st[u % 2][:, :], ks[0:ROWS_ST, h, kt * P:(kt + 1) * P], qs[0:ROWS_ST, h, :],
                          start=True, stop=True).then_inc(st_done, 1)

            def context(b, s):
                g, kt = divmod(s, 4)
                if s == 0:
                    pe.wait_ge(v_ready, 2 * (b + 1))
                    pe.wait_ge(v_ones_ready, 1)
                if kt == 0:
                    at_least(pe, ct_ready, 4 * b + g)
                pe.wait_ge(p_ready, 64 * b + 4 * s + 4)
                for j in range(4):
                    mm = pe.matmul(bank_c[32 * j:32 * j + 32, :], v[:, kt, 4 * g + j, :], probs[:, (4 * s + j) % SLOTS, :],
                                   start=kt == 0, stop=kt == 3)
                mm.then_inc(pv_done, 1)

            def turn_context(b, g, after):
                pe.wait_ge(ct_ready, 4 * b + g + 1)
                at_least(pe, *after)
                for t in range(NT):
                    mm = pe.transpose(bank_t[:, t * P:(t + 1) * P], ctT[:, t * P:(t + 1) * P], ident[:, :])
                mm.then_inc(ctT_done, 1)

            def out_project(b, after, to=side_tiles):
                pe.wait_ge(cx_ready, 4 * (b + 1))
                at_least(pe, *after)
                for c in range(2):
                    for half_ in range(2):
                        for i in range(2):
                            mm = pe.matmul(to[2 * c + half_], cx[:, 2 * half_ + i, c * P:(c + 1) * P], wo[:, i, :],
                                           start=i == 0, stop=i == 1)
                        mm.then_inc(wo_done, 1)

            def turn_x3(b, after):
                turn(xk, x3T_done, x_ready[3], b, after)

            def route(b, after):
                pe.wait_ge(x3T_hi_ready, b + 1)
                pe.wait_ge(x3T_lo_ready, b + 1)
                at_least(pe, *after)
                n = 0
                for k in range(KD):
                    for lhs, rhs in split_passes(win_hi[:, k, WA + WB:], win_lo[:, k, WA + WB:], x3T_hi[:, k, :], x3T_lo[:, k, :]):
                        mm = pe.matmul(bank_t[0:E1, :], lhs, rhs, start=n == 0, stop=n == 3 * KD - 1)
                        n += 1
                mm.then_inc(lgT_done, 1)

            def turn_logits(b):
                pe.wait_ge(lgT_ready, b + 1)
                for t in range(NT):
                    mm = pe.matmul(bank_t[:, t * E1:(t + 1) * E1], lgT[:, t * P:(t + 1) * P], ident[0:E1, 0:E1], start=True, stop=True)
                mm.then_inc(lg_done, 1)

            def expert_in(b, t, after, banks=side_banks):
                at_least(pe, *after)
                tok = slice(t * P, (t + 1) * P)
                for i, cols in enumerate((slice(0, WA), slice(WA, WA + WB))):
                    n = 0
                    for k in range(KD):
                        for lhs, rhs in split_passes(x3T_hi[:, k, tok], x3T_lo[:, k, tok], win_hi[:, k, cols], win_lo[:, k, cols]):
                            mm = pe.matmul(banks[i][:, 0:cols.stop - cols.start], lhs, rhs, start=n == 0, stop=n == 3 * KD - 1)
                            n += 1
                mm.then_inc(in_done, 1)

            def turn_hidden(b, thirds):
                if 0 in thirds:
                    pe.wait_ge(hid_ready, NT * (b + 1))
                else:
                    pe.wait_ge(hidT_ready, 2 * b + 1)
                for c in thirds:
                    for t in range(NT):
                        mm = pe.transpose(side[:, c % 2, t * P:(t + 1) * P], hid[:, t, c * P:(c + 1) * P], ident[:, :])
                mm.then_inc(hidT_done, 1)

            def expert_out(b, ts, to=side_tiles):
                if 0 in ts:
                    pe.wait_ge(hidT_ready, 2 * (b + 1))
                for t in ts:
                    for c in range(3):
                        mm = pe.matmul(to[t], hidT[:, c, t * P:(t + 1) * P], down1[:, c, :], start=c == 0, stop=c == 2)
                    mm.then_inc(down_done, 1)

            def pair(b, s, js, front):
                for j in js:
                    turned_score(b, s, j)
                    if s + LEAD < H1:
                        score(b, s + LEAD, j)
                    elif front:
                        score(b + 1, s + LEAD - H1, j)

            def body(b, front, back):
                for s in range(SUBS):
                    pair(b, s, (0, 1), front)
                    if s:
                        context(b, s - 1)
                    elif back:
                        context(b - 1, SUBS - 1)
                    if s == 0 and back:
                        value(b, (0,))
                    if s == 1 and back:
                        turn_context(b - 1, 3, after=(sh_ready, 4 * b + 1))
                    if s in (5, 9, 13):
                        turn_context(b, s // 4 - 1, after=(rel_ready, b) if s == 9 and back else (sh_ready, 4 * b + s // 4 + 1))
                    if s in (2, 6, 10):
                        turn_max(b, s // 4 + 1, after=(cx_ready, 4 * b + s // 4))
                    if s == 14 and front:
                        turn_max(b + 1, 0, after=(cx_ready, 4 * b + 3))
                    if s == 1 and front:
                        turn_x1(b + 1, after=(v_ready, 2 * (b + 1)))
                    if s == 2 and front:
                        select(b + 1)
                    if s == 3 and back:
                        out_project(b - 1, after=(pr_ready, b + 2) if front else (v_ready, 2 * (b + 1)))
                    if s == 4 and front:
                        turn_hm(b + 1, after=(r3_ready, b) if back else (pr_ready, b + 2))
                    if s == 5 and back:
                        turn_x3(b - 1, after=(hmT_ready, b + 2) if front else (r3_ready, b))
                    if s == 7 and front:
                        turn_x2(b + 1, after=(r2_ready, NT * (b + 2)))
                    if s == 8 and front:
                        query_key(b + 1, (0, 1))
                    if s == 9 and back:
                        expert_in(b - 1, 0, after=(qk_lo_ready, 4 * (b + 2)) if front else (x3T_lo_ready, b))
                    if 10 <= s < 13 and back:
                        expert_in(b - 1, s - 9, after=(hid_ready, NT * (b - 1) + s - 9))
                    if s == 13 and back:
                        turn_hidden(b - 1, (0, 1))
                    if s == 14 and back:
                        expert_out(b - 1, (0, 1))
                    pair(b, s, (2, 3), front)
                    if s == 0 and back:
                        value(b, (1,))
                    if s == 8 and front:
                        query_key(b + 1, (2, 3))
                    if s == 5 and front:
                        update(b + 1, after=(x3T_lo_ready, b) if back else (hmT_ready, b + 2))
                    if s == 6 and back:
                        route(b - 1, after=(sh_ready, 4 * b + 3))
                    if s == 7 and back:
                        turn_logits(b - 1)
                    if s == 13 and back:
                        turn_hidden(b - 1, (2,))
                    if s == 14 and back:
                        expert_out(b - 1, (2, 3))

            pe.wait_ge(kept.consts_in, 16 * len(kept.consts))
            turn_x1(0, after=(r3_ready, 0))
            pe.wait_ge(fprod_ready, 3)
            for k in range(KD):
                mm = pe.matmul(bank_t[:, 0:W0], ones[:, :], fprod[:, k, :], start=k == 0, stop=k == KD - 1)
            mm.then_inc(fsum_done, 1)
            select(0)
            pe.wait_ge(consts_in, 16 * len(CONSTS))
            turn_hm(0, after=(pr_ready, 1))
            update(0, (pr_ready, 1), tile_banks)
            turn_x2(0, after=(r2_ready, NT))
            pe.wait_ge(w_hi_ready, 2)
            pe.wait_ge(w_lo_ready, 2)
            query_key(0, range(4))
            pe.wait_ge(qk_lo_ready, 4)
            value(0, (0, 1))
            for h in range(LEAD):
                for t in range(NT):
                    score(0, h, t)
                if h == 4:
                    turn_max(0, 0, after=(fconst_ready, 1))
            pe.wait_ge(k_ones_in, 16)
            body(0, True, False)
            with pe.Fori(1, B - 1) as b:
                body(b, True, True)
            body(B - 1, False, True)
            context(B - 1, SUBS - 1)
            turn_context(B - 1, 3, after=(cx_ready, 4 * B - 1))
            out_project(B - 1, (ct_ready, 4 * B), tile_banks)
            turn_x3(B - 1, after=(r4_ready, 2 * (B - 1)))
            route(B - 1, after=(cx_ready, 4 * B))
            for t in range(NT - 1):
                expert_in(B - 1, t, (x3T_lo_ready, B), last_banks[t])
                if t == 0:
                    turn_logits(B - 1)
            expert_in(B - 1, NT - 1, (rel_ready, B), last_banks[NT - 1])
            turn_hidden(B - 1, (0, 1))
            turn_hidden(B - 1, (2,))
            expert_out(B - 1, range(NT), tile_banks)

        @block.scalar
        def _(act):
            def normalize(i, b, x):
                act.wait_ge(shift_ready[i], b + 1)
                for t in range(NT):
                    act.activation(x[:, t, :], x[:, t, :], ACT.Identity, bias=ln[i]["shift"][:, t:t + 1],
                                   scale=ln[i]["rstd"][:, t:t + 1]).then_inc(x_ready[i], 1)

            def x1T_out(b):
                act.wait_ge(x1T_done, b + 1)
                act.activation(x1T, side[:, :, :], ACT.Copy).then_inc(x1T_ready, 1)

            def squares(b):
                act.wait_ge(x1_ready, NT * (b + 1))
                at_least(act, hm_ready, NT * b)
                for t in range(NT):
                    act.activation(squared[:, t, :], xf[:, t, :], ACT.Square, accum_out=ssq[:, t:t + 1]).then_inc(ssq_ready, 1)

            def gate_exp(b):
                act.wait_ge(zc_ready, b + 1)
                act.activation(gt["e"][:, :, :], gt["zc"][:, :, :], ACT.Exp, scale=-1.0).then_inc(ge_ready, 1)

            def hmT_out(b):
                act.wait_ge(hmT_done, b + 1)
                act.activation(hmT[:, :], side[0:U0, 0, :], ACT.Copy).then_inc(hmT_ready, 1)

            def x2T_out(b):
                act.wait_ge(x2T_done, b + 1)
                act.activation(x2T_hi[:, :, :], side[:, :, :], ACT.Copy).then_inc(x2T_hi_ready, 1)

            def qk_out(b, parts):
                for i in parts:
                    act.wait_ge(qk_done, 4 * b + i + 1)
                    at_least(act, scratch_out[i % 2], 64 * b + 32 * (i // 2))
                    act.activation(qk_hi[:, i % 2, :], side[:, i % 2, :], ACT.Copy).then_inc(qk_hi_ready, 1)

            def value_out(b):
                if isinstance(b, int) and b == 0:
                    act.wait_ge(v_ones_ready, 1)
                for i in range(2):
                    act.wait_ge(vp_done, 2 * b + i + 1)
                    act.activation(v[:, 2 * i:2 * i + 2, :, 0:DH1], side[:, i, :].rearrange("p (t h d) -> p t h d", t=2, d=DH1),
                                   ACT.Copy).then_inc(v_ready, 1)

            def exponentials(b, s, js):
                if 0 in js:
                    at_least(act, pv_done, SUBS * b + s - 1)
                for j in js:
                    u = 4 * s + j
                    act.wait_ge(st_done, 64 * b + u + 1)
                    act.activation(probs[:, u % SLOTS, :], bank_st[u % 2][:, :], ACT.Exp, scale=SCALE1).then_inc(p_ready, 1)

            def shift_out(b, g):
                act.wait_ge(maxT_done, 4 * b + g + 1)
                at_least(act, shift_in, 32 * (4 * b + g))
                act.activation(sh[:, :], bank_t[0:8, :], ACT.Copy).then_inc(sh_ready, 1)

            def context_out(b, g):
                act.wait_ge(pv_done, SUBS * b + 4 * g + 4)
                at_least(act, ctT_done, 4 * b + g)
                act.activation(ctT[:, :], bank_c[:, :], ACT.Copy).then_inc(ct_ready, 1)

            def x3T_out(b):
                act.wait_ge(x3T_done, b + 1)
                act.activation(x3T_hi[:, :, :], side[:, :, :], ACT.Copy).then_inc(x3T_hi_ready, 1)

            def expert_in(b, t, banks=side_banks):
                act.wait_ge(in_done, NT * b + t + 1)
                if t >= 2:
                    act.wait_ge(sg_ready, NT * b + t - 1)
                act.activation(th[:, t % 2, :], banks[0][:, 0:E1 * F1], ACT.Tanh, scale=0.5).then_inc(th_ready, 1)

            def lgT_out(b):
                act.wait_ge(lgT_done, b + 1)
                act.activation(lgT, bank_t[0:E1, :], ACT.Copy).then_inc(lgT_ready, 1)

            def route_exp(b):
                act.wait_ge(rel_ready, b + 1)
                act.activation(rt["e"][:, :, :], rt["rel"][:, :, :], ACT.Exp).then_inc(re_ready, 1)

            def hidden_out(b, thirds):
                if 0 in thirds:
                    act.wait_ge(hidT_done, 2 * b + 1)
                    act.activation(hidT[:, 0:2, :], side[:, :, :], ACT.Copy).then_inc(hidT_ready, 1)
                else:
                    act.wait_ge(hidT_done, 2 * b + 2)
                    act.activation(hidT[:, 2, :], side[:, 0, :], ACT.Copy).then_inc(hidT_ready, 1)

            def body(b, front, back):
                for s in range(SUBS):
                    exponentials(b, s, (0, 1))
                    if s == 3 and front:
                        gate_exp(b + 1)
                    if s == 8 and front:
                        qk_out(b + 1, (0, 1))
                    if s == 5 and back:
                        x3T_out(b - 1)
                    if s == 7 and back:
                        lgT_out(b - 1)
                    if s == 13 and back:
                        hidden_out(b - 1, (0, 1))
                    exponentials(b, s, (2, 3))
                    if s == 0 and back:
                        context_out(b - 1, 3)
                        value_out(b)
                    if s in (4, 8, 12):
                        context_out(b, s // 4 - 1)
                    if s in (2, 6, 10):
                        shift_out(b, s // 4 + 1)
                    if s == 14 and front:
                        shift_out(b + 1, 0)
                    if s == 4 and back:
                        normalize(3, b - 1, xk)
                    if s == 15 and back:
                        normalize(4, b - 1, xk)
                    if s == 1 and front:
                        x1T_out(b + 1)
                        squares(b + 1)
                    if s == 4 and front:
                        hmT_out(b + 1)
                    if s == 6 and front:
                        normalize(2, b + 1, xf)
                    if s == 7 and front:
                        x2T_out(b + 1)
                    if s == 8 and back:
                        route_exp(b - 1)
                    if s == 8 and front:
                        qk_out(b + 1, (2, 3))
                    if 9 <= s < 13 and back:
                        expert_in(b - 1, s - 9)
                    if s == 13 and back:
                        hidden_out(b - 1, (2,))

            act.wait_ge(kept.consts_in, 16 * len(kept.consts))
            act.activation(ones_row[:, :], ones[0:2, :], ACT.Copy).then_inc(ones_row_ready, 1)
            x1T_out(0)
            squares(0)
            for i, n0, n1, hi in ((0, 0, KD * 3 * D, wqkv_hi), (1, KD * 3 * D, KD * (3 * D + W1), win_hi)):
                act.wait_ge(raw_in[i], 16)
                act.activation(hi[:, :, :].rearrange("p k n -> p (k n)"), raw[:, n0:n1], ACT.Copy).then_inc(w_hi_ready, 1)
            gate_exp(0)
            hmT_out(0)
            normalize(2, 0, xf)
            x2T_out(0)
            qk_out(0, range(4))
            value_out(0)
            shift_out(0, 0)
            act.wait_ge(w_lo_ready, 2)
            body(0, True, False)
            with act.Fori(1, B - 1) as b:
                body(b, True, True)
            body(B - 1, False, True)
            context_out(B - 1, 3)
            normalize(3, B - 1, xk)
            x3T_out(B - 1)
            lgT_out(B - 1)
            route_exp(B - 1)
            for t in range(NT):
                expert_in(B - 1, t, last_banks[t])
            hidden_out(B - 1, (0, 1))
            hidden_out(B - 1, (2,))
            normalize(4, B - 1, xk)

        @block.vector
        def _(dve):
            def normalize_x1(b):
                if not isinstance(b, int) or b > 0:
                    dve.wait_ge(x2_kept, b)
                for t in range(NT):
                    dve.tensor_scalar(xf[:, t, :], tile(xs, b, t), tile(stats, b, t)[:, 0:1],
                                      rstd1[:, NT * b + t:NT * b + t + 1] if isinstance(b, int) else rstd1[:, bass.ds(NT * b + t, 1)],
                                      ALU.add, ALU.mult).then_inc(x1_ready, 1)

            def first_max(step, values, key, eq, mask, top, ktop):
                step(dve.tensor_reduce(top[:, :], values, AX.X, ALU.max))
                step(dve.tensor_tensor(eq[:, :, :], values, over_last(top[:, :], E0), ALU.is_equal))
                step(dve.tensor_tensor(key[:, :, :], eq[:, :, :], over_tiles(rank[:, :]), ALU.mult))
                step(dve.tensor_reduce(ktop[:, :], key[:, :, :], AX.X, ALU.max))
                step(dve.tensor_tensor(mask[:, :, :], key[:, :, :], over_last(ktop[:, :], E0), ALU.is_equal))

            GATE_STEPS = (6, 8)

            def gate_scores(b):
                step = Steps(dve, gate_step, sum(GATE_STEPS), b)
                dve.wait_ge(pr_done, b + 1)
                dve.tensor_tensor(pr[:, :, :], side4[:, :, 0:W0], over_tiles(fconst[:, :]), ALU.subtract).then_inc(pr_ready, 1)
                dve.wait_ge(pr_ready, b + 1)
                step(dve.tensor_tensor(pr2[:, :, :], pr[:, :, 0:E0 * S0], pr[:, :, 0:E0 * S0], ALU.mult))
                dve.tensor_reduce(gt["score"][:, :, :], pr2[:, :, :].rearrange("p t (n s) -> p t n s", s=S0), AX.X, ALU.add)
                dve.wait_ge(ssq_ready, NT * (b + 1))
                step(dve.scalar_tensor_tensor(out=gt["dist"][:, :, :], in0=pr[:, :, W0 - E0:W0], scalar=-2.0,
                                              in1=over_last(ssq[:, :], E0), op0=ALU.mult, op1=ALU.add))
                step(dve.reciprocal(gt["rdist"][:, :, :], gt["dist"][:, :, :]))
                step(dve.tensor_tensor(gt["rel"][:, :, :], gt["score"][:, :, :], gt["rdist"][:, :, :], ALU.mult))
                step(dve.tensor_tensor(gt["cent"][:, :, :], gt["rel"][:, :, :], over_tiles(center[:, :]), ALU.subtract))
                step(dve.tensor_tensor(gt["z"][:, :, :], gt["cent"][:, :, :], over_tiles(slope[:, :]), ALU.mult))
                dve.tensor_scalar(gt["zc"][:, :, :], gt["z"][:, :, :], Z_MIN, None, ALU.max).then_inc(zc_ready, 1)

            def gate_pick(b):
                step = Steps(dve, gate_step, sum(GATE_STEPS), b)
                step.n = GATE_STEPS[0]
                dve.wait_ge(ge_ready, b + 1)
                step(dve.tensor_scalar(gt["e1"][:, :, :], gt["e"][:, :, :], 1.0, None, ALU.add))
                step(dve.reciprocal(gt["gate"][:, :, :], gt["e1"][:, :, :]))
                first_max(step, gt["gate"][:, :, :], gt["key"], gt["eq"], gt["pick"], gmax, kmax)
                step(dve.tensor_scalar(keep[:, :], gmax[:, :], -1.0, 2.0, ALU.mult, ALU.add))
                dve.tensor_tensor(hm[:, :, E0 * R0:U0], gt["pick"][:, :, :], over_last(gmax[:, :], E0), ALU.mult).then_inc(gate_ready, 1)

            def stats_of(i, b, x, by_tile_=False):
                ready = {2: r2_ready, 3: r3_ready, 4: r4_ready}[i]
                for t in range(NT):
                    if i == 2:
                        dve.wait_ge(ready, NT * b + t + 1)
                    elif by_tile_:
                        dve.wait_ge(ready, (1 if i == 3 else 2) * b + t + 1)
                    elif t == 0:
                        dve.wait_ge(ready, (1 if i == 3 else 2) * (b + 1))
                    dve.bn_stats(ln[i]["bn"][:, t, :], x[:, t, :]).then_inc(bn_ready[i], 1)
                dve.wait_ge(bn_ready[i], NT * (b + 1))
                merge_stats(dve, Steps(dve, merge_step[i], MERGE_STEPS, b), ln[i]["bn"], ln[i]["tmp"],
                            by_tile(ln[i]["mean_neg"]), by_tile(ln[i]["var"])).then_inc(var_ready[i], 1)

            def add_update(b, tiles_=side_tiles):
                whole_ = tiles_ is side_tiles
                for t in range(NT):
                    if whole_ and t == 0:
                        dve.wait_ge(up_done, NT * (b + 1))
                    elif not whole_:
                        dve.wait_ge(up_done, NT * b + t + 1)
                    dve.scalar_tensor_tensor(out=xf[:, t, :], in0=xf[:, t, :], scalar=keep[:, t:t + 1], in1=tiles_[t],
                                             op0=ALU.mult, op1=ALU.add).then_inc(r2_ready, 1)

            def x2T_rest(b):
                dve.wait_ge(x2T_hi_ready, b + 1)
                dve.tensor_tensor(x2T_lo[:, :, :], side[:, :, :], x2T_hi[:, :, :].bitcast(F32), ALU.subtract).then_inc(x2T_lo_ready, 1)

            def qk_rest(b, parts):
                for i in parts:
                    dve.wait_ge(qk_hi_ready, 4 * b + i + 1)
                    dve.tensor_tensor(qk_lo[:, i % 2, :], side[:, i % 2, :], qk_hi[:, i % 2, :].bitcast(F32), ALU.subtract).then_inc(qk_lo_ready, 1)

            def maxima(b, h, ts):
                g, j = divmod(h, 4)
                for t in ts:
                    u = 4 * h + t
                    dve.wait_ge(s_done, 64 * b + u + 1)
                    dve.tensor_reduce(nmax[:, g, t, j:j + 1], bank_s[u % 2][:, :], AX.X, ALU.max, negate=True).then_inc(max_ready, 1)

            def split_maxima(b, g):
                dve.wait_ge(max_ready, 64 * b + 16 * (g + 1))
                at_least(dve, maxT_done, 4 * b + g)
                dve.tensor_copy(nmax_parts[:, :, 0:4], nmax[:, g, :, :]).then_inc(nmax_hi_ready, 1)
                dve.wait_ge(nmax_hi_ready, 4 * b + g + 1)
                dve.tensor_tensor(nmax_parts[:, :, 4:8], nmax[:, g, :, :], nmax_parts[:, :, 0:4].bitcast(F32), ALU.subtract).then_inc(nmax_lo_ready, 1)

            def context_out(b, g):
                dve.wait_ge(ctT_done, 4 * b + g + 1)
                if g == 0:
                    at_least(dve, wo_done, NT * b)
                tj = bank_t[:, :].rearrange("p (t j c) -> p t j c", t=NT, j=4)
                dve.reciprocal(rsum[:, :, :].rearrange("p t (j o) -> p t j o", o=1), tj[:, :, :, DH1:DH1 + 1]).then_inc(rsum_ready, 1)
                dve.wait_ge(rsum_ready, 4 * b + g + 1)
                for t in range(NT):
                    cp = dve.tensor_tensor(cx[:, t, 4 * g * DH1:4 * (g + 1) * DH1].rearrange("p (j d) -> p j d", d=DH1),
                                           tj[:, t, :, 0:DH1], over_last(rsum[:, t, :], DH1), ALU.mult)
                cp.then_inc(cx_ready, 1)

            def add_attention(b):
                dve.wait_ge(wo_done, NT * (b + 1))
                dve.wait_ge(x2_kept, b + 1)
                dve.wait_ge(stored, 16 * b + 16)
                dve.tensor_tensor(xk[:, :, :], side4, tiles(xs, b), ALU.add).then_inc(r3_ready, 1)

            def x3T_rest(b):
                dve.wait_ge(x3T_hi_ready, b + 1)
                dve.tensor_tensor(x3T_lo[:, :, :], side[:, :, :], x3T_hi[:, :, :].bitcast(F32), ALU.subtract).then_inc(x3T_lo_ready, 1)

            def hidden(b, t, banks=side_banks):
                def by_expert(x):
                    return x.rearrange("p (e f) -> p e f", e=E1)

                if t == 0:
                    dve.wait_ge(w_ready, 2 * (b + 1))
                else:
                    dve.wait_ge(hid_ready, NT * b + t)
                dve.wait_ge(in_done, NT * b + t + 1)
                dve.tensor_tensor(by_expert(uw[:, :]), by_expert(banks[1][:, 0:WB]), over_last(rt["wh"][:, t, :], F1), ALU.mult).then_inc(uw_ready, 1)
                dve.wait_ge(th_ready, NT * b + t + 1)
                dve.tensor_tensor(by_expert(hid[:, t, E1 * F1:3 * P]), by_expert(banks[0][:, E1 * F1:WA]), over_last(rt["w"][:, t, :], R1), ALU.mult)
                dve.scalar_tensor_tensor(out=sg[:, :], in0=th[:, t % 2, :], scalar=1.0, in1=banks[0][:, 0:E1 * F1],
                                         op0=ALU.add, op1=ALU.mult).then_inc(sg_ready, 1)
                dve.wait_ge(uw_ready, NT * b + t + 1)
                dve.wait_ge(sg_ready, NT * b + t + 1)
                dve.tensor_tensor(hid[:, t, 0:E1 * F1], uw[:, :], sg[:, :], ALU.mult).then_inc(hid_ready, 1)

            ROUTE_STEPS = (1, 8, 7)

            def route_rel(b):
                step = Steps(dve, route_step, sum(ROUTE_STEPS), b)
                dve.wait_ge(lg_done, b + 1)
                lg = bank_t[:, 0:NT * E1].rearrange("p (t e) -> p t e", e=E1)
                step(dve.tensor_reduce(rm["max"][:, :], lg, AX.X, ALU.max))
                dve.tensor_tensor(rt["rel"][:, :, :], lg, over_last(rm["max"][:, :], E1), ALU.subtract).then_inc(rel_ready, 1)

            def route_first(b):
                step = Steps(dve, route_step, sum(ROUTE_STEPS), b)
                step.n = ROUTE_STEPS[0]
                dve.wait_ge(re_ready, b + 1)
                step(dve.tensor_reduce(rm["sum"][:, :], rt["e"][:, :, :], AX.X, ALU.add))
                step(dve.reciprocal(rm["rsum"][:, :], rm["sum"][:, :]))
                step(dve.tensor_tensor(rt["sc"][:, :, :], rt["e"][:, :, :], over_last(rm["rsum"][:, :], E1), ALU.mult))
                first_max(step, rt["sc"][:, :, :], rt["key1"], rt["eq1"], rt["pick1"], rm["max1"], rm["kmax1"])

            def route_second(b):
                step = Steps(dve, route_step, sum(ROUTE_STEPS), b)
                step.n = ROUTE_STEPS[0] + ROUTE_STEPS[1]
                step(dve.scalar_tensor_tensor(out=rt["less"][:, :, :], in0=rt["pick1"][:, :, :], scalar=-2.0, in1=rt["sc"][:, :, :],
                                              op0=ALU.mult, op1=ALU.add))
                first_max(step, rt["less"][:, :, :], rt["key2"], rt["eq2"], rt["pick2"], rm["max2"], rm["kmax2"])
                step(dve.tensor_tensor(rt["both"][:, :, :], rt["pick1"][:, :, :], rt["pick2"][:, :, :], ALU.add))
                dve.tensor_tensor(rt["w"][:, :, :], rt["both"][:, :, :], rt["sc"][:, :, :], ALU.mult).then_inc(w_ready, 1)
                dve.scalar_tensor_tensor(out=rt["wh"][:, :, :], in0=rt["both"][:, :, :], scalar=0.5, in1=rt["sc"][:, :, :],
                                         op0=ALU.mult, op1=ALU.mult).then_inc(w_ready, 1)

            def add_experts(b, i):
                dve.wait_ge(down_done, NT * b + 2 * (i + 1))
                ts = slice(2 * i, 2 * i + 2)
                dve.tensor_tensor(xk[:, ts, :], side4[:, ts, :], xk[:, ts, :], ALU.add).then_inc(r4_ready, 1)

            def add_tiles(done, other, ready):
                for t in range(NT):
                    dve.wait_ge(done, NT * (B - 1) + t + 1)
                    dve.tensor_tensor(xk[:, t, :], tile_banks[t], other[:, t, :], ALU.add).then_inc(ready, 1)

            def pair(b, s, ts, front):
                if s + LEAD < H1:
                    maxima(b, s + LEAD, ts)
                elif front:
                    maxima(b + 1, s + LEAD - H1, ts)

            def body(b, front, back):
                for s in range(SUBS):
                    pair(b, s, (0, 1), front)
                    if s == 0 and front:
                        normalize_x1(b + 1)
                    if s == 5 and back:
                        x3T_rest(b - 1)
                    if s == 9 and back:
                        route_second(b - 1)
                    if s == 3 and front:
                        gate_pick(b + 1)
                    if s == 4 and back:
                        stats_of(3, b - 1, xk)
                    if s == 6 and front:
                        stats_of(2, b + 1, xf)
                    if s == 8 and front:
                        qk_rest(b + 1, (0, 1))
                    if s == 8 and back:
                        route_rel(b - 1)
                    if s == 15 and back:
                        add_experts(b - 1, 1)
                        stats_of(4, b - 1, xk)
                    pair(b, s, (2, 3), front)
                    if s == 1 and back:
                        context_out(b - 1, 3)
                    if s in (1, 5, 9):
                        split_maxima(b, s // 4 + 1)
                    if s == 13 and front:
                        split_maxima(b + 1, 0)
                    if s == 2 and front:
                        gate_scores(b + 1)
                    if s == 3 and back:
                        add_attention(b - 1)
                    if s in (5, 9, 13):
                        context_out(b, s // 4 - 1)
                    if s == 5 and front:
                        add_update(b + 1)
                    if s == 7 and front:
                        x2T_rest(b + 1)
                    if s == 8 and front:
                        qk_rest(b + 1, (2, 3))
                    if s == 8 and back:
                        route_first(b - 1)
                    if 9 <= s < 13 and back:
                        hidden(b - 1, s - 9)
                    if s == 14 and back:
                        add_experts(b - 1, 0)

            dve.wait_ge(kept.consts_in, 16 * len(kept.consts))
            dve.wait_ge(rstd1_ready, 1)
            normalize_x1(0)
            for k in range(KD):
                sel = fw[:, k, 0:E0 * (S0 + R0)].rearrange("p (m n s) -> p m n s", m=2, s=S0)
                dst = fprod[:, k, 0:E0 * (S0 + R0)].rearrange("p (m n s) -> p m n s", m=2, s=S0)
                for m in range(2):
                    pd = dve.tensor_tensor(dst[:, m], sel[:, m], over_last(md[:, k, m * E0:(m + 1) * E0], S0), ALU.mult)
                pd.then_inc(fprod_ready, 1)
            dve.scalar_tensor_tensor(out=fprod[:, :, W0 - E0:W0], in0=md[:, :, 0:E0], scalar=0.5, in1=md[:, :, 0:E0],
                                     op0=ALU.mult, op1=ALU.mult).then_inc(fprod_ready, 1)
            dve.wait_ge(fsum_done, 1)
            dve.tensor_copy(fconst[:, :], bank_t[:, 0:W0]).then_inc(fconst_ready, 1)
            dve.wait_ge(fconst_ready, 1)
            dve.wait_ge(rstd1_ready, 2)
            gate_scores(0)
            gate_pick(0)
            for i, n0, n1, hi, lo in ((0, 0, KD * 3 * D, wqkv_hi, wqkv_lo), (1, KD * 3 * D, KD * (3 * D + W1), win_hi, win_lo)):
                dve.wait_ge(w_hi_ready, i + 1)
                dve.tensor_tensor(lo[:, :, :].rearrange("p k n -> p (k n)"), raw[:, n0:n1],
                                  hi[:, :, :].rearrange("p k n -> p (k n)").bitcast(F32), ALU.subtract).then_inc(w_lo_ready, 1)
            add_update(0, tile_banks)
            stats_of(2, 0, xf)
            x2T_rest(0)
            qk_rest(0, range(4))
            for h in range(LEAD):
                maxima(0, h, range(NT))
                if h == 3:
                    split_maxima(0, 0)
            body(0, True, False)
            with dve.Fori(1, B - 1) as b:
                body(b, True, True)
            body(B - 1, False, True)
            context_out(B - 1, 3)
            dve.wait_ge(stored, 16 * B)
            add_tiles(wo_done, tiles(xs, B - 1), r3_ready)
            stats_of(3, B - 1, xk, True)
            x3T_rest(B - 1)
            route_rel(B - 1)
            route_first(B - 1)
            route_second(B - 1)
            for t in range(NT):
                hidden(B - 1, t, last_banks[t])
            add_tiles(down_done, xk, r4_ready)
            stats_of(4, B - 1, xk, True)


class Kept:

    CONSTS = (("ident", [P]), ("ones_pp", [P]), ("fw", [KD, W0]), ("md", [KD, 2 * E0]), ("slope", [E0]), ("center", [E0]), ("rank", [E0]))

    def __init__(self, nc, ctx):
        def sb(name, shape):
            return ctx.enter_context(nc.sbuf_tensor(name, [P] + shape, F32))

        self.xs, self.stats = sb("xs", [B * NT, D]), sb("stats", [B * NT, 2])
        with nc.sbuf_tensor("wkv", [P, 2, KD, 1024], F32R) as self.wkv:
            pass
        self.shared = sb("shared", [8, T])
        self.consts = {name: sb(name, shape) for name, shape in self.CONSTS}
        self.consts_in = ctx.enter_context(nc.semaphore("kept_consts_in"))
        self.raw_in = [ctx.enter_context(nc.semaphore(f"raw_in{i}")) for i in range(2)]


def program(nc, a, out):
    with ExitStack() as ctx:
        kept = Kept(nc, ctx)
        layer0_attention(nc, a, kept)
        update_attention_experts(nc, a, kept, out)


def constants():
    import numpy as np

    pick = np.zeros((P, H0), np.float32)
    part_c, part_m = np.zeros((P, 1), np.float32), np.zeros((P, 1), np.float32)
    for g in range(G0):
        for j in range(J0):
            pick[32 * g + j, J0 * g + j] = pick[32 * g + 4 + j, J0 * g + j] = 1.0
            part_c[32 * g + j], part_c[32 * g + 4 + j], part_m[32 * g + 4 + j] = 1.0, -1.0, 1.0
    return {"pick": pick, "part_c": part_c, "part_m": part_m, "ones": np.ones((P, 1), np.float32),
            "ident": np.eye(P, dtype=np.float32), "ones_pp": np.ones((P, P), np.float32),
            "rank": np.broadcast_to(np.arange(E0, 0, -1).astype(np.float32), (P, E0))}


def laid_out(i):
    import numpy as np

    def cut(w):
        return w.reshape(KD, P, -1).transpose(1, 0, 2)

    i = {k: np.asarray(v) for k, v in i.items()}
    x = i["L0_attn_hidden_states"]
    arrays = {
        "x": x,
        "xT": x.reshape(B, 2, P, 2, KD, P).transpose(5, 0, 4, 1, 3, 2).reshape(P, B, KD, T),
        "wqT0": cut(i["L0_attn_Wq"].T),
        "wkvT0": cut(np.concatenate([i["L0_attn_Wk"], i["L0_attn_Wv"]]).T).reshape(P, -1),
        "woT0": i["L0_attn_Wo"].reshape(D, H0, DH0).transpose(2, 1, 0),
        "bq": i["L0_attn_bq"].reshape(H0, DH0).T,
        "bk": np.broadcast_to(i["L0_attn_bk"], (P, 512)),
        "bv": np.broadcast_to(i["L0_attn_bv"], (P, 512)),
        "fw": cut(np.concatenate([i["L0_ffn_select_weight"].transpose(1, 0, 2).reshape(D, -1),
                                  i["L0_ffn_lora_update"].transpose(1, 0, 2).reshape(D, -1),
                                  i["L0_ffn_select_mean_diff"].T], axis=1)),
        "md": cut(np.concatenate([i["L0_ffn_select_mean_diff"].T, i["L0_ffn_debias_w"].T], axis=1)),
        "slope": np.broadcast_to(i["L0_ffn_imp_slope"], (P, E0)),
        "center": np.broadcast_to(i["L0_ffn_imp_center"], (P, E0)),
        "down0": np.concatenate([i["L0_ffn_lora_degen"].transpose(0, 2, 1).reshape(E0 * R0, D), i["L0_ffn_bias_w"]]),
        "wqkv1": cut(np.concatenate([i["L1_attn_Wq"], i["L1_attn_Wk"], i["L1_attn_Wv"]], axis=1)).reshape(P, -1),
        "wo1": i["L1_attn_Wo"].reshape(P, 2, D),
        "bo": np.broadcast_to(i["L1_attn_bo"], (P, D)),
        "win1": cut(np.concatenate([i["L1_ffn_gate_w"].reshape(-1, D), i["L1_ffn_lora_A"].reshape(-1, D),
                                    i["L1_ffn_up_w"].reshape(-1, D), i["L1_ffn_G"].T]).T).reshape(P, -1),
        "down1": np.concatenate([i["L1_ffn_down_w"].transpose(0, 2, 1).reshape(E1 * F1, D),
                                 i["L1_ffn_lora_B"].transpose(0, 2, 1).reshape(E1 * R1, D)]).reshape(3, P, D).transpose(1, 0, 2),
    }
    arrays.update(constants())
    return {k: np.ascontiguousarray(v) for k, v in arrays.items()}


def kernel(**inputs):
    import numpy as np
    import concourse.bacc as bacc
    from concourse.bass_utils import run_bass_kernel_spmd

    nc = bacc.Bacc("TRN2", target_bir_lowering=False, num_devices=1)
    arrays = laid_out(inputs)
    aps = {k: nc.dram_tensor(f"in_{k}", v.shape, F32, kind="ExternalInput").ap() for k, v in arrays.items()}
    out = nc.dram_tensor("out", (B, T, D), F32, kind="ExternalOutput").ap()
    program(nc, aps, out)
    r = run_bass_kernel_spmd(nc, [{f"in_{k}": v for k, v in arrays.items()}], core_ids=[0])
    return r.results[0]["out"]
```
